# Optimizing a Trainium2 kernel written in Bass

```python
import numpy as np
import jax
import jax.numpy as jnp

def _softmax(x, axis=-1):
    return jax.nn.softmax(x, axis=axis)

def _gelu(x):
    return jax.nn.gelu(x, approximate=True)

def _silu(x):
    return jax.nn.silu(x)

def _sigmoid(x):
    return jax.nn.sigmoid(x)

def _layernorm(x, axis=-1, eps=1e-05):
    m = jnp.mean(x, axis=axis, keepdims=True)
    v = jnp.var(x, axis=axis, keepdims=True)
    return (x - m) / jnp.sqrt(v + eps)

def _scatter_add(tgt, idx, src, axis=0):
    return tgt.at[idx].add(src)

def _segment_sum(src, seg, n):
    return jax.ops.segment_sum(src, seg, n)
kernel_name = 'mk_adaln_d1_jaxref_r4_4acef3'

def setup_inputs(seed: int=0):
    np.random.seed(seed)
    _w = jnp.asarray

    def _L0_attn_setup():
        import jax, jax.numpy as jnp
        import numpy as np
        import math
        D_MODEL = 512
        NUM_HEADS = 16
        HEAD_DIM = D_MODEL // NUM_HEADS
        key = jax.random.key(seed)
        k_x, k_wqkv, k_bqkv, k_wo, k_bo = jax.random.split(key, 5)
        B, S = (2, 512)
        scale = 1.0 / math.sqrt(D_MODEL)
        return {'x': jax.random.normal(k_x, (B, S, D_MODEL), dtype=jnp.float32), 'w_qkv': jax.random.normal(k_wqkv, (3 * D_MODEL, D_MODEL), dtype=jnp.float32) * scale, 'b_qkv': jax.random.normal(k_bqkv, (3 * D_MODEL,), dtype=jnp.float32) * 0.01, 'w_out': jax.random.normal(k_wo, (D_MODEL, D_MODEL), dtype=jnp.float32) * scale, 'b_out': jax.random.normal(k_bo, (D_MODEL,), dtype=jnp.float32) * 0.01}
    _L0_attn_in = _L0_attn_setup()

    def _L0_ffn_setup():
        import jax, jax.numpy as jnp
        import numpy as np
        H = 512
        F = 352
        E = 64
        TOP_K = 6
        CAP = 128
        SCALE = 1.0
        F_SH = 2 * F
        B, S = (1, 512)
        key = jax.random.key(seed)
        ks = jax.random.split(key, 8)
        s = 0.02
        return {'hidden_states': jax.random.normal(ks[0], (B, S, H), jnp.float32), 'gate_w': jax.random.normal(ks[1], (E, H), jnp.float32) * s, 'w_gate': jax.random.normal(ks[2], (E, H, F), jnp.float32) * s, 'w_up': jax.random.normal(ks[3], (E, H, F), jnp.float32) * s, 'w_down': jax.random.normal(ks[4], (E, F, H), jnp.float32) * s, 'sh_gate': jax.random.normal(ks[5], (F_SH, H), jnp.float32) * s, 'sh_up': jax.random.normal(ks[6], (F_SH, H), jnp.float32) * s, 'sh_down': jax.random.normal(ks[7], (H, F_SH), jnp.float32) * s}
    _L0_ffn_in = _L0_ffn_setup()
    _L0_c = _w((lambda *s: np.random.randn(*s).astype(np.float32) * 0.05)(2, 512))
    _L0_wmod = _w((lambda *s: np.random.randn(*s).astype(np.float32) * 0.05)(512, 6 * 512) * 512 ** (-0.5))
    _d = {'L0_attn_x': _L0_attn_in['x'], 'L0_attn_w_qkv': _L0_attn_in['w_qkv'], 'L0_attn_b_qkv': _L0_attn_in['b_qkv'], 'L0_attn_w_out': _L0_attn_in['w_out'], 'L0_attn_b_out': _L0_attn_in['b_out'], 'L0_ffn_gate_w': _L0_ffn_in['gate_w'], 'L0_ffn_w_gate': _L0_ffn_in['w_gate'], 'L0_ffn_w_up': _L0_ffn_in['w_up'], 'L0_ffn_w_down': _L0_ffn_in['w_down'], 'L0_ffn_sh_gate': _L0_ffn_in['sh_gate'], 'L0_ffn_sh_up': _L0_ffn_in['sh_up'], 'L0_ffn_sh_down': _L0_ffn_in['sh_down'], 'L0_c': _L0_c, 'L0_wmod': _L0_wmod}
    _x0 = _d['L0_attn_x']
    _d['L0_attn_x'] = jax.random.normal(jax.random.fold_in(jax.random.key(seed), 1), (2, 1024, 512), dtype=_x0.dtype)
    del _x0
    return _d

def reference(L0_attn_x, L0_attn_w_qkv, L0_attn_b_qkv, L0_attn_w_out, L0_attn_b_out, L0_ffn_gate_w, L0_ffn_w_gate, L0_ffn_w_up, L0_ffn_w_down, L0_ffn_sh_gate, L0_ffn_sh_up, L0_ffn_sh_down, L0_c, L0_wmod):

    def _L0_attn_ref(x, w_qkv, b_qkv, w_out, b_out):
        import jax, jax.numpy as jnp
        import numpy as np
        import math
        D_MODEL = 512
        NUM_HEADS = 16
        HEAD_DIM = D_MODEL // NUM_HEADS
        B, S, D = x.shape
        H, Hd = (NUM_HEADS, HEAD_DIM)
        qkv = jnp.einsum('bsd,ed->bse', x, w_qkv) + b_qkv
        qkv = qkv.reshape(B, S, 3, H, Hd)
        q = jnp.transpose(qkv[:, :, 0], (0, 2, 1, 3))
        k = jnp.transpose(qkv[:, :, 1], (0, 2, 1, 3))
        v = jnp.transpose(qkv[:, :, 2], (0, 2, 1, 3))
        scores = jnp.einsum('bhqd,bhkd->bhqk', q, k) / math.sqrt(Hd)
        causal = jnp.triu(jnp.full((S, S), -jnp.inf, dtype=scores.dtype), k=1)
        scores = scores + causal[None, None]
        attn = jax.nn.softmax(scores, axis=-1)
        out = jnp.einsum('bhqk,bhkd->bhqd', attn, v)
        out = jnp.transpose(out, (0, 2, 1, 3)).reshape(B, S, D)
        return jnp.einsum('bsd,ed->bse', out, w_out) + b_out

    def _L0_ffn_ref(hidden_states, gate_w, w_gate, w_up, w_down, sh_gate, sh_up, sh_down):
        import jax, jax.numpy as jnp
        import numpy as np
        H = 512
        F = 352
        E = 64
        TOP_K = 6
        CAP = 128
        SCALE = 1.0
        F_SH = 2 * F
        B, S = (1, 512)
        b, s, _ = hidden_states.shape
        x = hidden_states.reshape(-1, H)
        T = x.shape[0]
        logits = x.astype(jnp.float32) @ gate_w.astype(jnp.float32).T
        scores = jax.nn.softmax(logits, axis=-1)
        topk_w, topk_idx = jax.lax.top_k(scores, TOP_K)
        topk_w = topk_w * SCALE
        eid = topk_idx.reshape(-1)
        x_exp = jnp.repeat(x, TOP_K, axis=0)
        order = jnp.argsort(eid)
        eid_s = eid[order]
        counts = jnp.bincount(eid, length=E)
        starts = jnp.cumsum(counts) - counts
        pos = jnp.arange(T * TOP_K) - starts[eid_s]
        valid = pos < CAP
        pos_c = jnp.where(valid, pos, CAP)
        buf = jnp.zeros((E, CAP + 1, H), x.dtype).at[eid_s, pos_c].set(x_exp[order])
        g = jax.nn.silu(jnp.einsum('ech,ehf->ecf', buf, w_gate))
        u = jnp.einsum('ech,ehf->ecf', buf, w_up)
        d = jnp.einsum('ecf,efh->ech', g * u, w_down)
        out_s = jnp.where(valid[:, None], d[eid_s, pos_c], 0.0)
        out_exp = jnp.zeros_like(out_s).at[order].set(out_s)
        y = jnp.einsum('tkh,tk->th', out_exp.reshape(T, TOP_K, H), topk_w)
        y = y.astype(x.dtype).reshape(b, s, H)
        gs = jax.nn.silu(hidden_states @ sh_gate.T)
        us = hidden_states @ sh_up.T
        y = y + gs * us @ sh_down.T
        return y
    x = L0_attn_x
    mod = (_silu(L0_c) @ L0_wmod).reshape(L0_c.shape[0], 6, 1, -1)
    sa, ca, ga, sb, cb, gb = (mod[:, 0], mod[:, 1], mod[:, 2], mod[:, 3], mod[:, 4], mod[:, 5])
    ga = (2 * (ga >= 0) - 1) * jnp.maximum(jnp.abs(ga), 0.25)
    gb = (2 * (gb >= 0) - 1) * jnp.maximum(jnp.abs(gb), 0.25)
    h = _layernorm(x, axis=-1) * (1 + ca) + sa
    x = x + ga * _L0_attn_ref(h, L0_attn_w_qkv, L0_attn_b_qkv, L0_attn_w_out, L0_attn_b_out)
    h = _layernorm(x, axis=-1) * (1 + cb) + sb
    x = x + gb * _L0_ffn_ref(h, L0_ffn_gate_w, L0_ffn_w_gate, L0_ffn_w_up, L0_ffn_w_down, L0_ffn_sh_gate, L0_ffn_sh_up, L0_ffn_sh_down)
    return x

_drawn_inputs = setup_inputs


def setup_inputs(seed=0):
    import zlib

    import numpy as np

    out = dict(_drawn_inputs(seed))
    spreads = {}
    factors = {'L0_attn_b_qkv': 8.0,
     'L0_attn_b_out': 8.0,
     'L0_ffn_gate_w': 8.0,
     'L0_ffn_w_gate': 8.0,
     'L0_ffn_w_up': 8.0,
     'L0_ffn_w_down': 8.0,
     'L0_ffn_sh_gate': 4.014,
     'L0_ffn_sh_up': 3.924,
     'L0_ffn_sh_down': 3.919}
    for name, (base, spread) in spreads.items():
        noise = np.random.default_rng([zlib.crc32(name.encode()), seed]).standard_normal(out[name].shape)
        drawn = base * np.exp(spread * noise) if base else spread * noise
        out[name] = jnp.asarray(drawn.astype(out[name].dtype))
    for name, factor in factors.items():
        out[name] = (out[name] * factor).astype(out[name].dtype)
    return out
```

```python
from contextlib import ExitStack

import concourse.bass as bass
from concourse import mybir

P = 128
F32 = mybir.dt.float32
BF16 = mybir.dt.bfloat16
U32 = mybir.dt.uint32
ACT = mybir.ActivationFunctionType
ALU = mybir.AluOpType
AX_X = mybir.AxisListType.X

B, S, D = 2, 1024, 512
T = B * S
KD = D // P
NT = T // P
TB = S // P
H, HD = 16, 32
HG = P // HD
NG = H // HG
GT = 4
GN = GT * P
E, F, TOPK, CAP = 64, 352, 6, 128
FC = -(-F // P)
FR = F - (FC - 1) * P
FS = 2 * F
SC = -(-FS // P)
SR = FS - (SC - 1) * P
TD = T + P
EPS = 1e-5
SCALE = float(HD) ** -0.5
MASKED = 1e30
DROPPED = float(1 << 20)
SA, CA, GA, SB, CB, GB = range(6)
START, DSTART = 1, 16
UNROLL = 4


def build(nc, x, wqkv, bqkv, wo, bo, gatew, wgu, wd, shgu, shd, c, wmod, out):
    x_rows = x.rearrange("(t p) d -> p t d", p=P)
    out_rows = out.rearrange("(t p) d -> p t d", p=P)
    h2_dram = nc.dram_tensor("h2_dram", [TD, D], F32, kind="Internal").ap()
    y_dram = nc.dram_tensor("y_dram", [TD, D], F32, kind="Internal").ap()
    slot_dram = nc.dram_tensor("slot_dram", [CAP * E, 2], F32, kind="Internal").ap()
    h2_rows = h2_dram.rearrange("(t p) d -> p t d", p=P)
    y_rows = y_dram.rearrange("(t p) d -> p t d", p=P)

    ctx = ExitStack()
    with ctx:
        def sb(name, shape, dt=F32):
            return ctx.enter_context(nc.sbuf_tensor(name, shape, dt))

        def sem(name):
            return ctx.enter_context(nc.semaphore(name))

        def wait_alone(eng, what, value):
            eng.wait_ge(what, value)
            eng.nop(nofuse=True)

        psum = ctx.enter_context(nc.psum_tensor("psum", [P, 8, 512], F32))

        xs = sb("xs", [P, NT, D])
        hT = sb("hT", [P, KD, T])
        oT = sb("oT", [P, KD, T])
        arena = sb("arena", [P, 20 * 1024])
        ident = sb("ident", [P, P])
        ident_bf = sb("ident_bf", [P, P], BF16)
        mask_bf = sb("mask_bf", [P, P], BF16)
        before_bf = sb("before_bf", [P, P], BF16)
        ones_bf = sb("ones_bf", [P, P], BF16)
        ones = sb("ones", [P, P])
        modT = sb("modT", [P, 6, KD, B])
        rowsB = sb("rowsB", [P, 3, B, D])
        bq = sb("bq", [P, 3, NG])
        boT = sb("boT", [P, KD])
        iota_e = sb("iota_e", [P, E])
        tok_id = sb("tok_id", [P, GT])

        used = [0]

        def carve(shape, dt=F32, at=None):
            n = 1
            for s in shape[1:]:
                n *= s
            words = n if dt is not BF16 else (n + 1) // 2
            start = used[0] if at is None else at
            if at is None:
                used[0] += words
                assert used[0] <= 20 * 1024, used[0]
            v = arena[0:shape[0], start:start + words]
            if dt is not F32:
                v = v.bitcast(dt)
            if len(shape) == 3:
                v = v.rearrange("p (a b) -> p a b", b=shape[2])
            elif len(shape) == 4:
                v = v.rearrange("p (a b c) -> p a b c", b=shape[2], c=shape[3])
            return v

        cT = carve([P, KD, B])
        cs = carve([P, KD, B])
        wm = [carve([P, KD, D]) for _ in range(2)]
        xn = carve([P, 2, GT * D]).rearrange("p n (t d) -> p n t d", d=D)
        stats = carve([P, TB, 6])
        mv = carve([P, TB, 2])
        var = carve([P, TB])
        std = carve([P, TB])
        rstd = carve([P, TB])
        clamp = carve([P, KD, B])
        diag = [carve([P, P]) for _ in range(2)]
        zeros = carve([P, D])
        empty = carve([P, E, 2])

        small_in = sem("small_in")
        x_in = sem("x_in")
        wm_in = [sem(f"wm_in{i}") for i in range(2)]
        const_v = sem("const_v")
        const_g = sem("const_g")
        c_silu = sem("c_silu")
        mod_mm = sem("mod_mm")
        mod_out = sem("mod_out")
        mod_fix = sem("mod_fix")
        diag_ready = sem("diag_ready")
        row_mm = sem("row_mm")
        row_out = sem("row_out")
        ln_v = sem("ln_v")
        ln_var = sem("ln_var")
        ln_std = sem("ln_std")
        xn_ready = sem("xn_ready")
        h_mm = sem("h_mm")
        h_out = sem("h_out")
        init_out = sem("init_out")
        scattered = sem("scattered")
        added = sem("added")
        ROW_SRC = (CB, SB, GB)

        with nc.Block() as block:
            @block.sync
            def _(sp):
                sp.dma_start(cT, c).then_inc(small_in, 16)
                sp.dma_start(bq[:, :, :], bqkv).then_inc(small_in, 16)
                sp.dma_start(boT[:, :], bo).then_inc(small_in, 16)
                for w in range(6):
                    if w >= 2:
                        sp.wait_ge(mod_mm, w - 1)
                    sp.dma_start(wm[w % 2], wmod[w]).then_inc(wm_in[w % 2], 16)
                    if w < NT // GT:
                        if w:
                            sp.wait_ge(x_in, 16 * w)
                        sp.dma_start(xs[:, w * GT:(w + 1) * GT, :], x_rows[:, w * GT:(w + 1) * GT, :])\
                            .then_inc(x_in, 16)
                sp.wait_ge(const_v, 5)
                sp.wait_ge(const_g, 7)
                n_init = 0
                for t in range(NT):
                    sp.dma_start(y_rows[:, t, :], zeros).then_inc(init_out, 16)
                    n_init += 1
                sp.dma_start(slot_dram.rearrange("(p e) w -> p e w", e=E), empty).then_inc(init_out, 16)
                sp.wait_ge(init_out, 16 * (n_init + 1))

            @block.gpsimd
            def _(pool):
                nc.gpsimd.iota(iota_e[:, :], [[1, E]], base=0, channel_multiplier=0,
                               allow_small_or_imprecise_dtypes=True).then_inc(const_g, 1)
                nc.gpsimd.iota(tok_id[:, :], [[P, GT]], base=0, channel_multiplier=1,
                               allow_small_or_imprecise_dtypes=True).then_inc(const_g, 1)
                nc.gpsimd.iota(empty[:, :, 0], [[0, E]], base=T, channel_multiplier=1,
                               allow_small_or_imprecise_dtypes=True).then_inc(const_g, 1)
                pool.wait_ge(const_v, 5)
                nc.gpsimd.affine_select(out=ident[:, :], in_=ident[:, :], compare_op=ALU.not_equal, fill=1.0,
                                        base=0, pattern=[[-1, P]], channel_multiplier=1).then_inc(const_g, 1)
                nc.gpsimd.affine_select(out=ident_bf[:, :], in_=ident_bf[:, :], compare_op=ALU.not_equal,
                                        fill=1.0, base=0, pattern=[[-1, P]], channel_multiplier=1)\
                    .then_inc(const_g, 1)
                nc.gpsimd.affine_select(out=mask_bf[:, :], in_=mask_bf[:, :], compare_op=ALU.is_ge, fill=MASKED,
                                        base=0, pattern=[[-1, P]], channel_multiplier=1).then_inc(const_g, 1)
                nc.gpsimd.affine_select(out=before_bf[:, :], in_=ones_bf[:, :], compare_op=ALU.is_gt, fill=0.0,
                                        base=0, pattern=[[1, P]], channel_multiplier=-1).then_inc(const_g, 1)
                pool.dma_start(h2_rows[:, NT, :], zeros).then_inc(scattered, 16)
                pool.dma_start(y_rows[:, NT, :], zeros).then_inc(added, 16)
                pool.wait_ge(scattered, 16)
                pool.wait_ge(added, 16)

            @block.tensor
            def _(pe):
                pe.sem_inc(h_mm, START)
                pe.wait_ge(c_silu, 1)
                for w in range(6):
                    pe.wait_ge(wm_in[w % 2], 16 * (w // 2 + 1))
                    if w >= 2:
                        pe.wait_ge(mod_out, w - 1)
                    for j in range(KD):
                        for k in range(KD):
                            last = nc.tensor.matmul(psum[:, 7 * (w % 2), j * B:(j + 1) * B],
                                                    wm[w % 2][:, k, j * P:(j + 1) * P], cs[:, k, :],
                                                    start=(k == 0), stop=(k == KD - 1))
                    last.then_inc(mod_mm, 1)
                pe.wait_ge(const_v, 5)
                for n in range(3 * B):
                    for k in range(KD):
                        pe.wait_ge(diag_ready, n * KD + k + 1)
                        last = nc.tensor.matmul(psum[:, 1 + n, k * P:(k + 1) * P], ones[:, :],
                                                diag[(n * KD + k) % 2], start=True, stop=True)
                        last.then_inc(row_mm, 1)
                pe.wait_ge(const_g, 7)
                pe.wait_ge(row_out, 3 * B)
                with pe.Fori(0, B) as b:
                    for n in range(2):
                        pe.wait_ge(h_out, START + b * 2 * KD)
                        for t in range(GT):
                            pe.wait_ge(xn_ready, b * TB + n * GT + t + 1)
                            for k in range(KD):
                                last = nc.tensor.transpose(psum[:, n * KD + k, t * P:(t + 1) * P],
                                                           xn[:, n, t, k * P:(k + 1) * P], ident[:, :])
                        last.then_inc(h_mm, 1)

            @block.scalar
            def _(act):
                act.sem_inc(h_out, START)
                act.wait_ge(small_in, 48)
                nc.scalar.activation(cs, cT, ACT.Silu).then_inc(c_silu, 1)
                with act.Fori(0, B) as b:
                    act.wait_ge(ln_var, b + 1)
                    nc.scalar.activation(std, var, ACT.Sqrt).then_inc(ln_std, 1)
                    act.wait_ge(mod_fix, 5)
                    for n in range(2):
                        act.wait_ge(h_mm, START + b * 2 + n + 1)
                        for k in range(KD):
                            nc.scalar.activation(hT[:, k, bass.ds(b * S + n * GN, GN)], psum[:, n * KD + k, :],
                                                 ACT.Identity, bias=modT[:, SA, k, bass.ds(b, 1)],
                                                 scale=modT[:, CA, k, bass.ds(b, 1)]).then_inc(h_out, 1)

            @block.vector
            def _(dve):
                nc.vector.memset(ident[:, :], 0.0).then_inc(const_v, 1)
                nc.vector.memset(ident_bf[:, :], 0.0).then_inc(const_v, 1)
                nc.vector.memset(mask_bf[:, :], 0.0).then_inc(const_v, 1)
                nc.vector.memset(ones_bf[:, :], 1.0).then_inc(const_v, 1)
                nc.vector.memset(zeros, 0.0)
                nc.vector.memset(empty[:, :, 1], 0.0)
                nc.vector.memset(ones[:, :], 1.0).then_inc(const_v, 1)
                for w in range(6):
                    dve.wait_ge(mod_mm, w + 1)
                    nc.vector.tensor_copy(modT[:, w, :, :].rearrange("p k b -> p (k b)"),
                                          psum[:, 7 * (w % 2), 0:KD * B]).then_inc(mod_out, 1)
                dve.wait_ge(mod_out, 6)
                fixed = 0
                for w in (CA, CB):
                    nc.vector.tensor_scalar(modT[:, w, :, :], modT[:, w, :, :], 1.0, None, ALU.add)\
                        .then_inc(mod_fix, 1)
                    fixed += 1
                for w in (GA, GB):
                    nc.vector.tensor_scalar(clamp, modT[:, w, :, :], -0.25, None, ALU.min).then_inc(mod_fix, 1)
                    nc.vector.tensor_scalar(cT, modT[:, w, :, :], 0.0, None, ALU.is_ge).then_inc(mod_fix, 1)
                    nc.vector.tensor_scalar(modT[:, w, :, :], modT[:, w, :, :], 0.25, None, ALU.max)\
                        .then_inc(mod_fix, 1)
                    fixed += 3
                    dve.wait_ge(mod_fix, fixed)
                    nc.vector.tensor_tensor(modT[:, w, :, :], modT[:, w, :, :], clamp, ALU.subtract)\
                        .then_inc(mod_fix, 1)
                    fixed += 1
                    dve.wait_ge(mod_fix, fixed)
                    nc.vector.tensor_tensor(modT[:, w, :, :], modT[:, w, :, :], cT, ALU.mult).then_inc(mod_fix, 1)
                    fixed += 1
                    dve.wait_ge(mod_fix, fixed)
                    nc.vector.tensor_tensor(modT[:, w, :, :], modT[:, w, :, :], clamp, ALU.add)\
                        .then_inc(mod_fix, 1)
                    fixed += 1
                    dve.wait_ge(mod_fix, fixed)
                dve.wait_ge(const_g, 4)
                for n in range(3 * B):
                    r, b = divmod(n, B)
                    for k in range(KD):
                        m = n * KD + k
                        if m >= 2:
                            dve.wait_ge(row_mm, m - 1)
                        nc.vector.tensor_scalar(diag[m % 2], ident[:, :], modT[:, ROW_SRC[r], k, b:b + 1], None,
                                                ALU.mult).then_inc(diag_ready, 1)
                for n in range(3 * B):
                    dve.wait_ge(row_mm, (n + 1) * KD)
                    nc.vector.tensor_copy(rowsB[:, n // B, n % B, :], psum[:, 1 + n, :]).then_inc(row_out, 1)
                with dve.Fori(0, B) as b:
                    dve.wait_ge(x_in, b * 32 + 32)
                    for t in range(TB):
                        nc.vector.bn_stats(stats[:, t, :], xs[:, b * TB + t, :]).then_inc(ln_v, 1)
                    wait_alone(dve, ln_v, b * 17 + 8)
                    for t in range(TB):
                        nc.vector.bn_aggr(mv[:, t, :], stats[:, t, :]).then_inc(ln_v, 1)
                    dve.wait_ge(ln_v, b * 17 + 16)
                    nc.vector.tensor_scalar(var, mv[:, :, 1], EPS, None, ALU.add).then_inc(ln_var, 1)
                    dve.wait_ge(ln_std, b + 1)
                    nc.vector.reciprocal(rstd, std).then_inc(ln_v, 1)
                    dve.wait_ge(ln_v, b * 17 + 17)
                    for t in range(TB):
                        n = t // GT
                        if t % GT == 0:
                            dve.wait_ge(h_mm, START + b * 2)
                        nc.vector.tensor_scalar(xn[:, n, t % GT, :], xs[:, b * TB + t, :], mv[:, t, 0:1],
                                                rstd[:, t:t + 1], ALU.subtract, ALU.mult).then_inc(xn_ready, 1)

        used[0] = 0
        wg = carve([P, KD * 3, P])
        qT = carve([P, S])
        kT = carve([P, S])
        vT = carve([P, S])
        v = carve([P, TB, P])
        prob = carve([P, 4, S])
        pT = carve([P, 2, HG, TB * P])
        low = carve([P, 2, HG])
        den = carve([P, 2, HG])
        rden = carve([P, 2, HG])
        rden_T = carve([P, 2, P])
        bqs = carve([P, NG])

        wg_in = sem("wg_in")
        bqs_ready = sem("bqs_ready")
        t_ready = [sem("t_ready_act"), sem("t_ready_dve")]
        t_free = [sem("t_free_act"), sem("t_free_dve")]
        s_ready = sem("s_ready")
        low_ready = sem("low_ready")
        probs = sem("probs")
        pv_done = sem("pv_done")
        rden_ready = sem("rden_ready")
        rb_done = sem("rb_done")
        rb_copied = sem("rb_copied")
        o_done = sem("o_done")

        BANKS = (4, 5)
        O_BANKS = (6, 7)
        units = [(i, h) for i in range(TB) for h in range(HG)]
        NU = len(units)
        uses = [("q", 0), ("q", 1), ("k", 0), ("k", 1), ("v", 0), ("v", 1), ("vt", 0), ("vt", 1)]
        QKV_USES = len(uses)
        of_unit = []
        for i, h in units:
            of_unit.append([])
            for j0 in range(0, i + 1, 4):
                of_unit[-1].append(len(uses))
                uses.append(("p", i, h, j0))
        PER = len(uses) // 2
        assert len(uses) % 2 == 0

        def s_bank(n):
            return psum[:, 2 * (n % 2):2 * (n % 2) + 2, :].rearrange("p a b -> p (a b)")

        def empty_bank(eng, mine, it, m):
            if m % 2 != mine:
                return
            what = uses[m]
            eng.wait_ge(t_ready[mine], it * PER + m // 2 + 1)
            src = psum[:, BANKS[mine], :]
            if what[0] in "qkv" and len(what[0]) == 1:
                part = "qkv".index(what[0])
                dst = (qT, kT, vT)[part][:, what[1] * GN:(what[1] + 1) * GN]
                scale = -SCALE if part == 0 else 1.0
                bias = (bqs[:, bass.ds(it_g[mine], 1)] if part == 0 else bq[:, part, bass.ds(it_g[mine], 1)])
                if mine == 0:
                    ins = nc.scalar.activation(dst, src, ACT.Identity, bias=bias, scale=scale)
                else:
                    ins = nc.vector.tensor_scalar(dst, src, scale, bias, ALU.mult, ALU.add)
            else:
                if what[0] == "vt":
                    dst = v[:, what[1] * 4:what[1] * 4 + 4, :].rearrange("p a b -> p (a b)")
                else:
                    _, i, h, j0 = what
                    w = (min(i + 1, j0 + 4) - j0) * P
                    if h == 0 and j0 == 0 and i >= 2 or (i >= 2 and m % 2 == mine):
                        eng.wait_ge(pv_done, it * TB + i - 1)
                    dst = pT[:, i % 2, h, j0 * P:j0 * P + w]
                    src = psum[:, BANKS[mine], 0:w]
                ins = nc.scalar.copy(dst, src) if mine == 0 else nc.vector.tensor_copy(dst, src)
            ins.then_inc(t_free[mine], 1)

        it_g = [None, None]

        with nc.Block() as block:
            @block.sync
            def _(sp):
                with sp.Fori(0, B) as b:
                    with sp.Fori(0, NG) as g:
                        sp.wait_ge(s_ready, START + (b * NG + g) * NU)
                        sp.dma_start(wg, wqkv[g].rearrange("p (a c) -> p a c", c=P)).then_inc(wg_in, 16)

            @block.tensor
            def _(pe):
                pe.sem_inc(s_ready, START)
                def qkv(it, b, m):
                    kind, n = uses[m]
                    pe.wait_ge(t_free[m % 2], START + it * PER + m // 2)
                    bank = psum[:, BANKS[m % 2], :]
                    part = "qkv".index(kind)
                    for k in range(KD):
                        last = nc.tensor.matmul(bank, wg[:, k * 3 + part, :],
                                                hT[:, k, bass.ds(b * S + n * GN, GN)],
                                                start=(k == 0), stop=(k == KD - 1))
                    last.then_inc(t_ready[m % 2], 1)

                def scores(it, n):
                    i, h = units[n]
                    if n >= 2:
                        pe.wait_ge(probs, it * NU + n - 1)
                    s = s_bank(n)
                    w = (i + 1) * P
                    for a in range(0, w, 512):
                        e = min(w, a + 512)
                        last = nc.tensor.matmul(s[:, a:e], qT[h * HD:(h + 1) * HD, i * P:(i + 1) * P],
                                                kT[h * HD:(h + 1) * HD, a:e], start=True, stop=(e < w))
                    last = nc.tensor.matmul(s[:, i * P:w], ident_bf[:, :], mask_bf[:, :], start=False, stop=True)
                    last.then_inc(s_ready, 1)

                def turn(it, n):
                    i, h = units[n]
                    pe.wait_ge(probs, it * NU + n + 1)
                    for m in of_unit[n]:
                        j0 = uses[m][3]
                        pe.wait_ge(t_free[m % 2], START + it * PER + m // 2)
                        for j in range(j0, min(i + 1, j0 + 4)):
                            last = nc.tensor.transpose(psum[:, BANKS[m % 2], (j - j0) * P:(j - j0 + 1) * P],
                                                       prob[:, n % 4, j * P:(j + 1) * P], ident[:, :])
                        last.then_inc(t_ready[m % 2], 1)

                def values(it, i):
                    for x in range(2):
                        done = sum(1 for m in range(of_unit[4 * i + 3][-1] + 1) if m % 2 == x)
                        pe.wait_ge(t_free[x], START + it * PER + done)
                    if i >= 2:
                        pe.wait_ge(o_done, START + it * TB + i - 1)
                    bank = O_BANKS[i % 2]
                    for j in range(i + 1):
                        for h in range(HG):
                            last = nc.tensor.matmul(psum[h * HD:(h + 1) * HD, bank, 0:P],
                                                    v[:, j, h * HD:(h + 1) * HD], pT[:, i % 2, h, j * P:(j + 1) * P],
                                                    start=(j == 0), stop=(j == i))
                    last.then_inc(pv_done, 1)
                    pe.wait_ge(rden_ready, it * TB + i + 1)
                    for h in range(HG):
                        last = nc.tensor.matmul(psum[h * HD:(h + 1) * HD, bank, P:2 * P],
                                                rden[:, i % 2, h:h + 1].broadcast_to([P, HD]), ident[:, :],
                                                start=True, stop=True)
                    last.then_inc(rb_done, 1)

                with pe.Fori(0, B) as b:
                    with pe.Fori(0, NG) as g:
                        it = b * NG + g
                        pe.wait_ge(wg_in, it * 16 + 16)
                        pe.wait_ge(o_done, START + it * TB)
                        for m in range(6):
                            qkv(it, b, m)
                        for x in range(2):
                            pe.wait_ge(t_free[x], START + it * PER + 3)
                        for m in (6, 7):
                            for j in range(4):
                                last = nc.tensor.transpose(psum[:, BANKS[m % 2], j * P:(j + 1) * P],
                                                           vT[:, ((m - 6) * 4 + j) * P:((m - 6) * 4 + j + 1) * P],
                                                           ident[:, :])
                            last.then_inc(t_ready[m % 2], 1)
                        scores(it, 0)
                        scores(it, 1)
                        for n in range(NU):
                            turn(it, n)
                            if n + 2 < NU:
                                scores(it, n + 2)
                            if n % HG == 0 and n:
                                values(it, n // HG - 1)
                        values(it, TB - 1)

            @block.scalar
            def _(act):
                act.sem_inc(t_free[0], START)
                act.wait_ge(bqs_ready, 1)

                def exps(it, n):
                    i, h = units[n]
                    w = (i + 1) * P
                    act.wait_ge(low_ready, it * NU + n + 1)
                    if n >= 4:
                        m = of_unit[n - 4][-1]
                        act.wait_ge(t_ready[m % 2], it * PER + m // 2 + 1)
                    if h == 0 and i >= 2:
                        act.wait_ge(rden_ready, it * TB + i - 1)
                    nc.scalar.activation(prob[:, n % 4, 0:w], s_bank(n)[:, 0:w], ACT.Exp,
                                         bias=low[:, i % 2, h:h + 1], scale=-1.0,
                                         accum_out=den[:, i % 2, h:h + 1]).then_inc(probs, 1)

                with act.Fori(0, B) as b:
                    with act.Fori(0, NG) as g:
                        it = b * NG + g
                        it_g[0] = g
                        for m in range(QKV_USES):
                            empty_bank(act, 0, it, m)
                        exps(it, 0)
                        exps(it, 1)
                        for n in range(NU):
                            for m in of_unit[n]:
                                empty_bank(act, 0, it, m)
                            if n + 2 < NU:
                                exps(it, n + 2)

            @block.vector
            def _(dve):
                dve.sem_inc(t_free[1], START)
                dve.sem_inc(o_done, START)
                nc.vector.tensor_scalar(bqs, bq[:, 0, :], -SCALE, None, ALU.mult).then_inc(bqs_ready, 1)
                dve.wait_ge(bqs_ready, 1)

                def lows(it, n):
                    i, h = units[n]
                    dve.wait_ge(s_ready, START + it * NU + n + 1)
                    if h == 0 and i >= 2:
                        dve.wait_ge(probs, it * NU + 4 * (i - 1))
                    nc.vector.tensor_reduce(low[:, i % 2, h:h + 1], s_bank(n)[:, 0:(i + 1) * P], AX_X, ALU.min)\
                        .then_inc(low_ready, 1)

                def combine(it, i, b, g):
                    bank = O_BANKS[i % 2]
                    dve.wait_ge(rb_done, it * TB + i + 1)
                    nc.vector.tensor_copy(rden_T[:, i % 2, :], psum[:, bank, P:2 * P])\
                        .then_inc(rb_copied, 1)
                    dve.wait_ge(rb_copied, it * TB + i + 1)
                    nc.vector.tensor_tensor(oT[:, g, bass.ds(b * S + i * P, P)], psum[:, bank, 0:P],
                                            rden_T[:, i % 2, :], ALU.mult).then_inc(o_done, 1)

                with dve.Fori(0, B) as b:
                    with dve.Fori(0, NG) as g:
                        it = b * NG + g
                        it_g[1] = g
                        for m in range(QKV_USES):
                            empty_bank(dve, 1, it, m)
                        lows(it, 0)
                        lows(it, 1)
                        for n in range(NU):
                            for m in of_unit[n]:
                                empty_bank(dve, 1, it, m)
                            if n + 2 < NU:
                                lows(it, n + 2)
                            if n % HG == HG - 1:
                                i = n // HG
                                dve.wait_ge(probs, it * NU + n + 1)
                                nc.vector.reciprocal(rden[:, i % 2, :], den[:, i % 2, :]).then_inc(rden_ready, 1)
                            if n % HG == 0 and n:
                                combine(it, n // HG - 1, b, g)
                        combine(it, TB - 1, b, g)

        used[0] = 0
        woT = carve([P, KD, D])
        gw = carve([P, KD, E])
        sgu = carve([P, KD * (2 * SC - 1), P])
        sd = carve([P, SC, D])
        yT = carve([P, KD, GN])
        h2 = yT.rearrange("p k (t x) -> p (k t x)", x=P).rearrange("p (t d) -> p t d", d=D)
        h2T = carve([P, KD, GN])
        guS = carve([P, SC, GN])
        silu = hT[:, 0, 0:2 * GN].rearrange("p (a b) -> p a b", b=GN)
        x_mod = hT[:, 1, 0:2 * D].rearrange("p (a b) -> p a b", b=D)
        scr = hT[:, 2, :]
        hot = scr[:, 0:GT * TOPK * E].rearrange("p (t k e) -> p t k e", k=TOPK, e=E)
        scr2 = hT[:, 3, :]
        hot_pos = scr2[:, 0:GT * TOPK * E].rearrange("p (t k e) -> p t k e", k=TOPK, e=E)
        c3 = [0]
        base3 = hT[:, 1, 2 * D:T]

        def c3arve(shape, dt=F32):
            n = 1
            for q in shape[1:]:
                n *= q
            words = n if dt is not BF16 else (n + 1) // 2
            vv = base3[:, c3[0]:c3[0] + words]
            c3[0] += words
            assert c3[0] <= T - 2 * D
            if dt is not F32:
                vv = vv.bitcast(dt)
            if len(shape) == 3:
                vv = vv.rearrange("p (a b) -> p a b", b=shape[2])
            if len(shape) == 4:
                vv = vv.rearrange("p (a b c) -> p a b c", b=shape[2], c=shape[3])
            return vv

        stats3 = c3arve([P, GT, 6])
        mv3 = c3arve([P, GT, 2])
        var3 = c3arve([P, GT])
        std3 = c3arve([P, GT])
        rstd3 = c3arve([P, GT])
        boga = c3arve([P, KD, B])
        lmax = c3arve([P, GT])
        lsub = c3arve([P, GT, E])
        lexp = c3arve([P, GT, E])
        lsum = c3arve([P, GT])
        lrec = c3arve([P, GT])
        top = sb("top", [P, GT, 8])
        top_i = sb("top_i", [P, GT, 8], U32)
        top_f = c3arve([P, GT, 8])
        picked = sb("picked", [P, GT, E], BF16)
        carry = sb("carry", [P, E])
        carry_bf = sb("carry_bf", [P, E], BF16)
        gsum = sb("gsum", [P, E])
        pos_k = sb("pos_k", [P, GT, TOPK])
        over = sb("over", [P, GT, TOPK])
        dest = sb("dest", [P, GT, TOPK])
        dest_u = sb("dest_u", [P, GT, TOPK], U32)
        entry = sb("entry", [P, GT, TOPK, 2])

        w3_in = sem("w3_in")
        bg_ready = sem("bg_ready")
        y_mm = sem("y_mm")
        y_act = sem("y_act")
        y_dve = sem("y_dve")
        yt_mm = sem("yt_mm")
        x1_done = sem("x1_done")
        l2_v = sem("l2_v")
        l2_var = sem("l2_var")
        l2_std = sem("l2_std")
        h2_ready = sem("h2_ready")
        h2_out = sem("h2_out")
        h2t_mm = sem("h2t_mm")
        h2t_act = sem("h2t_act")
        h2t_dve = sem("h2t_dve")
        lg_mm = sem("lg_mm")
        r_v = sem("r_v")
        r_sub = sem("r_sub")
        r_exp = sem("r_exp")
        pick_ready = sem("pick_ready")
        pos_mm = sem("pos_mm")
        dest_ready = sem("dest_ready")
        gu_mm = sem("gu_mm")
        gu_silu = sem("gu_silu")
        gu_done = sem("gu_done")
        sd_mm = sem("sd_mm")
        sd_tmp = sem("sd_tmp")
        sd_done = sem("sd_done")
        NGRP = T // GN
        HB = S // GN

        with nc.Block() as block:
            @block.sync
            def _(sp):
                sp.sem_inc(h2_out, DSTART)
                sp.dma_start(woT, wo).then_inc(w3_in, 16)
                sp.dma_start(gw, gatew).then_inc(w3_in, 16)
                sp.dma_start(sgu, shgu.rearrange("p (a c) -> p a c", c=P)).then_inc(w3_in, 16)
                sp.dma_start(sd[:, 0:SC - 1, :], shd[0:(SC - 1) * P, :].rearrange("(a p) d -> p a d", p=P))\
                    .then_inc(w3_in, 16)
                sp.dma_start(sd[0:SR, SC - 1, :], shd[(SC - 1) * P:FS, :]).then_inc(w3_in, 16)
                with sp.Fori(0, NGRP) as it:
                    sp.wait_ge(h2_ready, it * GT + GT)
                    sp.dma_start(h2_rows[:, bass.ds(it * GT, GT), :], h2).then_inc(h2_out, 16)
                sp.wait_ge(h2_out, DSTART + 16 * NGRP)

            @block.gpsimd
            def _(pool):
                with pool.Fori(0, NGRP) as it:
                    wait_alone(pool, dest_ready, it + 1)
                    for t in range(GT):
                        for k in range(TOPK):
                            pool.indirect_dma_start(
                                out=slot_dram, out_offset=bass.IndirectOffsetOnAxis(ap=dest_u[:, t, k:k + 1], axis=0),
                                in_=entry[:, t, k, :], in_offset=None, bounds_check=CAP * E - 1,
                                oob_is_err=False).then_inc(scattered, 16)
                pool.wait_ge(scattered, DSTART + NGRP * GT * TOPK * 16)

            @block.tensor
            def _(pe):
                pe.wait_ge(w3_in, 80)
                with pe.Fori(0, NGRP) as it:
                    pe.wait_ge(sd_done, START + it * GT)
                    for j in range(KD):
                        for k in range(KD):
                            last = nc.tensor.matmul(psum[:, j, :], woT[:, k, j * P:(j + 1) * P],
                                                    oT[:, k, bass.ds(it * GN, GN)], start=(k == 0), stop=(k == KD - 1))
                        last.then_inc(y_mm, 1)
                    pe.wait_ge(y_act, it * 2 + 2)
                    pe.wait_ge(y_dve, it * 2 + 2)
                    for t in range(GT):
                        for j in range(KD):
                            last = nc.tensor.transpose(psum[:, 4 + t, j * P:(j + 1) * P],
                                                       yT[:, j, t * P:(t + 1) * P], ident[:, :])
                        last.then_inc(yt_mm, 1)
                    for t in range(GT):
                        pe.wait_ge(h2_ready, it * GT + t + 1)
                        for k in range(KD):
                            last = nc.tensor.transpose(psum[:, k, t * P:(t + 1) * P],
                                                       h2[:, t, k * P:(k + 1) * P], ident[:, :])
                    last.then_inc(h2t_mm, 1)
                    pe.wait_ge(h2t_act, it * 2 + 2)
                    pe.wait_ge(h2t_dve, it * 2 + 2)
                    pe.wait_ge(x1_done, it * GT + GT)
                    for t in range(GT):
                        for k in range(KD):
                            last = nc.tensor.matmul(psum[:, 4, t * E:(t + 1) * E], h2T[:, k, t * P:(t + 1) * P],
                                                    gw[:, k, :], start=(k == 0), stop=(k == KD - 1))
                    last.then_inc(lg_mm, 1)

                    def gate_up(f):
                        if f >= 2:
                            pe.wait_ge(gu_done, it * SC + f - 1)
                        for half in range(2 if f < SC - 1 else 1):
                            for k in range(KD):
                                last = nc.tensor.matmul(psum[:, (f % 2) * 2 + half, :],
                                                        sgu[:, k * (2 * SC - 1) + 2 * f + half, :], h2T[:, k, :],
                                                        start=(k == 0), stop=(k == KD - 1))
                        last.then_inc(gu_mm, 1)

                    for f in range(2):
                        gate_up(f)
                    pe.wait_ge(pick_ready, it + 1)
                    for t in range(GT):
                        nc.tensor.matmul(psum[:, 5, t * E:(t + 1) * E], before_bf[:, :], picked[:, t, :],
                                         start=True, stop=False)
                        for u in range(t):
                            nc.tensor.matmul(psum[:, 5, t * E:(t + 1) * E], ones_bf[:, :], picked[:, u, :],
                                             start=False, stop=False)
                        last = nc.tensor.matmul(psum[:, 5, t * E:(t + 1) * E], ones_bf[:, :], carry_bf[:, :],
                                                start=False, stop=True)
                    last.then_inc(pos_mm, 1)
                    for f in range(2, SC):
                        gate_up(f)
                    pe.wait_ge(gu_done, it * SC + SC)
                    for t in range(GT):
                        if t >= 2:
                            pe.wait_ge(sd_done, START + it * GT + t - 1)
                        for f in range(SC):
                            rows = P if f < SC - 1 else SR
                            last = nc.tensor.matmul(psum[:, 6 + t % 2, :], guS[0:rows, f, t * P:(t + 1) * P],
                                                    sd[0:rows, f, :], start=(f == 0), stop=(f == SC - 1))
                        last.then_inc(sd_mm, 1)

            @block.scalar
            def _(act):
                act.wait_ge(bg_ready, 1)
                with act.Fori(0, B) as b:
                    with act.Fori(0, HB) as m:
                        it = b * HB + m
                        act.wait_ge(h2_out, DSTART + it * 16)
                        for j in (0, 2):
                            act.wait_ge(y_mm, it * KD + j + 1)
                            nc.scalar.activation(yT[:, j, :], psum[:, j, :], ACT.Identity,
                                                 bias=boga[:, j, bass.ds(b, 1)],
                                                 scale=modT[:, GA, j, bass.ds(b, 1)]).then_inc(y_act, 1)
                        act.wait_ge(l2_var, it + 1)
                        nc.scalar.activation(std3, var3, ACT.Sqrt).then_inc(l2_std, 1)
                        act.wait_ge(h2t_mm, it + 1)
                        for k in (0, 2):
                            nc.scalar.copy(h2T[:, k, :], psum[:, k, :]).then_inc(h2t_act, 1)
                        act.wait_ge(r_sub, it + 1)
                        nc.scalar.activation(lexp, lsub, ACT.Exp).then_inc(r_exp, 1)
                        for f in range(SC):
                            act.wait_ge(gu_mm, it * SC + f + 1)
                            if f >= 2:
                                act.wait_ge(gu_done, it * SC + f - 1)
                            rows = P if f < SC - 1 else SR
                            nc.scalar.activation(silu[0:rows, f % 2, :], psum[0:rows, (f % 2) * 2, :], ACT.Silu)\
                                .then_inc(gu_silu, 1)

            @block.vector
            def _(dve):
                dve.sem_inc(sd_done, START)
                for b in range(B):
                    i_ = nc.vector.tensor_tensor(boga[:, :, b], boT[:, :], modT[:, GA, :, b], ALU.mult)
                nc.vector.memset(carry[:, :], 0.0)
                nc.vector.memset(carry_bf[:, :], 0.0).then_inc(bg_ready, 1)
                dve.wait_ge(bg_ready, 1)
                with dve.Fori(0, B) as b:
                    with dve.Fori(0, HB) as m:
                        it = b * HB + m
                        dve.wait_ge(h2_out, DSTART + it * 16)
                        for j in (1, 3):
                            dve.wait_ge(y_mm, it * KD + j + 1)
                            nc.vector.tensor_scalar(yT[:, j, :], psum[:, j, :], modT[:, GA, j, bass.ds(b, 1)],
                                                    boga[:, j, bass.ds(b, 1)], ALU.mult, ALU.add).then_inc(y_dve, 1)
                        N2 = 3 * GT + 1
                        for t in range(GT):
                            xt = xs[:, bass.ds(it * GT + t, 1), :].rearrange("p a d -> p (a d)")
                            dve.wait_ge(yt_mm, it * GT + t + 1)
                            nc.vector.tensor_tensor(xt, xt, psum[:, 4 + t, :], ALU.add).then_inc(x1_done, 1)
                            wait_alone(dve, x1_done, it * GT + t + 1)
                            nc.vector.bn_stats(stats3[:, t, :], xt).then_inc(l2_v, 1)
                        wait_alone(dve, l2_v, it * N2 + GT)
                        for t in range(GT):
                            nc.vector.bn_aggr(mv3[:, t, :], stats3[:, t, :]).then_inc(l2_v, 1)
                        dve.wait_ge(l2_v, it * N2 + 2 * GT)
                        nc.vector.tensor_scalar(var3, mv3[:, :, 1], EPS, None, ALU.add).then_inc(l2_var, 1)
                        dve.wait_ge(l2_std, it + 1)
                        nc.vector.reciprocal(rstd3, std3).then_inc(l2_v, 1)
                        dve.wait_ge(l2_v, it * N2 + 2 * GT + 1)
                        for t in range(GT):
                            xt = xs[:, bass.ds(it * GT + t, 1), :].rearrange("p a d -> p (a d)")
                            r1 = rowsB[:, 0, bass.ds(b, 1), :].rearrange("p a d -> p (a d)")
                            r2 = rowsB[:, 1, bass.ds(b, 1), :].rearrange("p a d -> p (a d)")
                            nc.vector.scalar_tensor_tensor(out=x_mod[:, t % 2, :], in0=xt, scalar=mv3[:, t, 0:1], in1=r1,
                                                           op0=ALU.subtract, op1=ALU.mult).then_inc(l2_v, 1)
                            dve.wait_ge(l2_v, it * N2 + 2 * GT + 2 + t)
                            nc.vector.scalar_tensor_tensor(out=h2[:, t, :], in0=x_mod[:, t % 2, :],
                                                           scalar=rstd3[:, t:t + 1], in1=r2,
                                                           op0=ALU.mult, op1=ALU.add).then_inc(h2_ready, 1)
                        dve.wait_ge(h2t_mm, it + 1)
                        for k in (1, 3):
                            nc.vector.tensor_copy(h2T[:, k, :], psum[:, k, :]).then_inc(h2t_dve, 1)
                        NR = 22
                        step = [0]

                        def then(ins):
                            step[0] += 1
                            ins.then_inc(r_v, 1)
                            wait_alone(dve, r_v, it * NR + step[0])

                        lg = psum[:, 4, 0:GT * E].rearrange("p (t e) -> p t e", e=E)
                        dve.wait_ge(lg_mm, it + 1)
                        then(nc.vector.tensor_reduce(lmax, lg, AX_X, ALU.max))
                        nc.vector.tensor_tensor(lsub, lg,
                                                lmax.rearrange("p (t o) -> p t o", o=1).broadcast_to([P, GT, E]),
                                                ALU.subtract).then_inc(r_sub, 1)
                        dve.wait_ge(r_exp, it + 1)
                        then(nc.vector.tensor_reduce(lsum, lexp, AX_X, ALU.add))
                        then(nc.vector.reciprocal(lrec, lsum))
                        then(nc.vector.tensor_tensor(lexp, lexp,
                                                     lrec.rearrange("p (t o) -> p t o", o=1).broadcast_to([P, GT, E]),
                                                     ALU.mult))
                        wait_alone(dve, scattered, DSTART + it * GT * TOPK * 16)
                        for t in range(GT):
                            i_ = nc.vector.max(top[:, t, :], lexp[:, t, :])
                        then(i_)
                        for t in range(GT):
                            i_ = nc.vector.max_index(top_i[:, t, :], top[:, t, :], lexp[:, t, :])
                        then(i_)
                        then(nc.vector.tensor_copy(top_f, top_i[:, :, :]))
                        for t in range(GT):
                            i_ = nc.vector.tensor_tensor(
                                hot[:, t], iota_e[:, :].rearrange("p (o e) -> p o e", o=1).broadcast_to([P, TOPK, E]),
                                top_f[:, t, 0:TOPK].rearrange("p (k o) -> p k o", o=1).broadcast_to([P, TOPK, E]),
                                ALU.is_equal)
                        then(i_)
                        with nc.allow_low_precision(reason="zeros and ones, exact in bfloat16"):
                            for t in range(GT):
                                i_ = nc.vector.tensor_reduce(picked[:, t, :], hot[:, t].rearrange("p k e -> p e k"),
                                                             AX_X, ALU.add)
                        i_.then_inc(pick_ready, 1)
                        dve.wait_ge(pick_ready, it + 1)
                        then(nc.vector.tensor_reduce(gsum[:, :], picked[:, :, :].rearrange("p t e -> p e t"), AX_X,
                                                     ALU.add))
                        then(nc.vector.tensor_tensor(carry[:, :], carry[:, :], gsum[:, :], ALU.add))
                        dve.wait_ge(pos_mm, it + 1)
                        then(nc.vector.tensor_copy(carry_bf[:, :], carry[:, :]))
                        for t in range(GT):
                            i_ = nc.vector.tensor_tensor(
                                hot_pos[:, t], hot[:, t],
                                psum[:, 5, t * E:(t + 1) * E].rearrange("p (o e) -> p o e", o=1)
                                .broadcast_to([P, TOPK, E]), ALU.mult)
                        then(i_)
                        for t in range(GT):
                            i_ = nc.vector.tensor_reduce(pos_k[:, t, :], hot_pos[:, t], AX_X, ALU.add)
                        then(i_)
                        then(nc.vector.tensor_scalar(over[:, :, :], pos_k[:, :, :], float(CAP), DROPPED, ALU.is_ge,
                                                     ALU.mult))
                        then(nc.vector.scalar_tensor_tensor(out=dest[:, :, :], in0=pos_k[:, :, :], scalar=float(E),
                                                            in1=top_f[:, :, 0:TOPK], op0=ALU.mult, op1=ALU.add))
                        then(nc.vector.tensor_tensor(dest[:, :, :], dest[:, :, :], over[:, :, :], ALU.add))
                        then(nc.vector.tensor_copy(dest_u[:, :, :], dest[:, :, :]))
                        then(nc.vector.tensor_copy(entry[:, :, :, 1], top[:, :, 0:TOPK]))
                        then(nc.vector.tensor_copy(
                            entry[:, :, :, 0],
                            tok_id[:, :].rearrange("p (t o) -> p t o", o=1).broadcast_to([P, GT, TOPK])))
                        nc.vector.tensor_scalar(tok_id[:, :], tok_id[:, :], float(GN), None, ALU.add)\
                            .then_inc(dest_ready, 1)
                        assert step[0] <= NR
                        for _ in range(NR - step[0]):
                            dve.sem_inc(r_v, 1)
                        for f in range(SC):
                            dve.wait_ge(gu_silu, it * SC + f + 1)
                            rows = P if f < SC - 1 else SR
                            up = psum[:, (f % 2) * 2 + 1, :] if f < SC - 1 else psum[SR:SR + SR, (f % 2) * 2, :]
                            nc.vector.tensor_tensor(guS[0:rows, f, :], silu[0:rows, f % 2, :], up, ALU.mult)\
                                .then_inc(gu_done, 1)
                        for t in range(GT):
                            xt = xs[:, bass.ds(it * GT + t, 1), :].rearrange("p a d -> p (a d)")
                            r3 = rowsB[:, 2, bass.ds(b, 1), :].rearrange("p a d -> p (a d)")
                            dve.wait_ge(sd_mm, it * GT + t + 1)
                            nc.vector.tensor_tensor(x_mod[:, t % 2, :], psum[:, 6 + t % 2, :], r3, ALU.mult)\
                                .then_inc(sd_tmp, 1)
                            dve.wait_ge(sd_tmp, it * GT + t + 1)
                            nc.vector.tensor_tensor(xt, xt, x_mod[:, t % 2, :], ALU.add).then_inc(sd_done, 1)

        used[0] = 0
        NW = KD * 2 * F
        WORDS = NW + FC * D
        whole = [hT[:, :, :].rearrange("p k t -> p (k t)"), oT[:, :, :].rearrange("p k t -> p (k t)")]
        wbuf = [whole[0][:, 0:WORDS], whole[1][:, 0:WORDS], carve([P, WORDS]), carve([P, WORDS])]
        wgu_s = [w[:, 0:NW].rearrange("p (k f) -> p k f", k=KD) for w in wbuf]
        wd_s = [w[:, NW:WORDS].rearrange("p (k d) -> p k d", k=FC) for w in wbuf]
        rest = [whole[0][:, WORDS:KD * T], whole[1][:, WORDS:KD * T]]
        xe = [carve([P, D]) for _ in range(UNROLL)]
        dsc = [carve([P, D]) for _ in range(UNROLL)]
        xeT = [rest[0][:, 0:D].rearrange("p (k c) -> p k c", k=KD),
               rest[0][:, D:2 * D].rearrange("p (k c) -> p k c", k=KD)]
        sil = [rest[0][:, 2 * D:2 * D + F], rest[0][:, 2 * D + F:2 * D + 2 * F]]
        gu = [rest[1][:, 0:F], rest[1][:, F:2 * F]]
        guT = [rest[1][:, 2 * F:2 * F + FC * P].rearrange("p (k c) -> p k c", k=FC),
               rest[1][:, 2 * F + FC * P:2 * F + 2 * FC * P].rearrange("p (k c) -> p k c", k=FC)]
        slots = carve([P, E, 2])
        slot_tok = sb("slot_tok", [P, E], U32)
        get_idx = [sb(f"get_idx{u}", [P, 1], U32) for u in range(UNROLL)]
        add_idx = [sb(f"add_idx{u}", [P, 1], U32) for u in range(UNROLL)]

        slots_in = sem("slots_in")
        tok_ready = sem("tok_ready")
        w_in = [sem(f"w_in{u}") for u in range(UNROLL)]
        get_ready = sem("get_ready")
        add_ready = sem("add_ready")
        xe_in = [sem(f"xe_in{u}") for u in range(UNROLL)]
        xt_mm = sem("xt_mm")
        xt_out = sem("xt_out")
        g_mm = sem("g_mm")
        u_mm = sem("u_mm")
        silu_done = sem("silu_done")
        gu_out = sem("gu_out")
        gt_mm = sem("gt_mm")
        gt_out = sem("gt_out")
        d_mm = sem("d_mm")
        d_out = sem("d_out")

        def wait_for(eng, what, value):
            if not isinstance(value, int) or value > 0:
                eng.wait_ge(what, value)

        def over_experts(eng, step):
            for u in range(UNROLL):
                step(0, u)
            with eng.Fori(1, E // UNROLL - 1) as i:
                for u in range(UNROLL):
                    step(i, u)
            for u in range(UNROLL):
                step(E // UNROLL - 1, u)

        def exists(e):
            return not isinstance(e, int) or 0 <= e < E

        with nc.Block() as block:
            @block.sync
            def _(sp):
                sp.dma_start(slots, slot_dram.rearrange("(p e) w -> p e w", e=E)).then_inc(slots_in, 16)

                def step(i, u):
                    e = i * UNROLL + u
                    wait_for(sp, d_mm, e - UNROLL + 1)
                    rows = wgu[e] if isinstance(e, int) else wgu[bass.ds(e, 1)].rearrange("a p c -> p (a c)")
                    sp.dma_start(wgu_s[u], rows.rearrange("p (k f) -> p k f", k=KD)).then_inc(w_in[u], 16)
                    sp.dma_start(wd_s[u][:, 0:FC - 1, :],
                                 wd[e, 0:(FC - 1) * P, :].rearrange("(k p) d -> p k d", p=P)).then_inc(w_in[u], 16)
                    sp.dma_start(wd_s[u][0:FR, FC - 1, :], wd[e, (FC - 1) * P:F, :]).then_inc(w_in[u], 16)

                over_experts(sp, step)

            @block.gpsimd
            def _(pool):
                def gather(e, i, u):
                    if not exists(e):
                        return
                    if not isinstance(i, int) or i > 0:
                        wait_alone(pool, xe_in[u], i * 16)
                    nc.gpsimd.tensor_copy(get_idx[u][:, :], slot_tok[:, bass.ds(e, 1)]).then_inc(get_ready, 1)
                    pool.wait_ge(get_ready, e + 1)
                    if not isinstance(i, int) or i > 0:
                        wait_alone(pool, xt_mm, e - UNROLL + 1)
                    pool.indirect_dma_start(
                        out=xe[u], out_offset=None, in_=h2_dram,
                        in_offset=bass.IndirectOffsetOnAxis(ap=get_idx[u][:, 0:1], axis=0),
                        bounds_check=TD - 1, oob_is_err=True).then_inc(xe_in[u], 16)

                def step(i, u):
                    e = i * UNROLL + u
                    nc.gpsimd.tensor_copy(add_idx[u][:, :], slot_tok[:, bass.ds(e, 1)]).then_inc(add_ready, 1)
                    pool.wait_ge(add_ready, e + 1)
                    wait_alone(pool, d_out, e + 1)
                    wait_alone(pool, added, DSTART + e * 16)
                    pool.indirect_dma_start(
                        out=y_dram, out_offset=bass.IndirectOffsetOnAxis(ap=add_idx[u][:, 0:1], axis=0),
                        in_=dsc[u], in_offset=None, compute_op=ALU.add,
                        bounds_check=TD - 1, oob_is_err=True).then_inc(added, 16)
                    gather(e + UNROLL, i + 1, u)

                pool.wait_ge(tok_ready, 1)
                for u in range(UNROLL):
                    gather(u, 0, u)
                over_experts(pool, step)
                pool.wait_ge(added, DSTART + E * 16)

            @block.tensor
            def _(pe):
                def turn_rows(e, i, u):
                    if not exists(e):
                        return
                    pe.wait_ge(xe_in[u], i * 16 + 16)
                    wait_for(pe, xt_out, e)
                    for k in range(KD):
                        last = nc.tensor.transpose(psum[:, 0, k * P:(k + 1) * P], xe[u][:, k * P:(k + 1) * P],
                                                   ident[:, :])
                    last.then_inc(xt_mm, 1)

                def half(e, u, up):
                    for k in range(KD):
                        last = nc.tensor.matmul(psum[:, 2 + up, 0:F], xeT[u % 2][:, k, :],
                                                wgu_s[u][:, k, up * F:(up + 1) * F],
                                                start=(k == 0), stop=(k == KD - 1))
                    last.then_inc(u_mm if up else g_mm, 1)

                def turn_hidden(e, u):
                    if not exists(e):
                        return
                    pe.wait_ge(gu_out, e + 1)
                    wait_for(pe, gt_out, e)
                    for k in range(FC):
                        w = P if k < FC - 1 else FR
                        last = nc.tensor.transpose(psum[0:w, 1, k * P:(k + 1) * P], gu[u % 2][:, k * P:k * P + w],
                                                   ident[:, :])
                    last.then_inc(gt_mm, 1)

                def down(e, u):
                    if not exists(e):
                        return
                    pe.wait_ge(gt_out, e + 1)
                    wait_for(pe, d_out, e - 1)
                    for k in range(FC):
                        w = P if k < FC - 1 else FR
                        last = nc.tensor.matmul(psum[:, 4 + u % 2, :], guT[u % 2][0:w, k, :], wd_s[u][0:w, k, :],
                                                start=(k == 0), stop=(k == FC - 1))
                    last.then_inc(d_mm, 1)

                def step(i, u):
                    e = i * UNROLL + u
                    pe.wait_ge(w_in[u], i * 48 + 48)
                    pe.wait_ge(xt_out, e + 1)
                    wait_for(pe, silu_done, e)
                    half(e, u, 0)
                    turn_hidden(e - 1, (u - 1) % UNROLL)
                    turn_rows(e + 1, i + (u + 1) // UNROLL, (u + 1) % UNROLL)
                    wait_for(pe, gu_out, e)
                    half(e, u, 1)
                    down(e - 1, (u - 1) % UNROLL)

                turn_rows(0, 0, 0)
                over_experts(pe, step)
                turn_hidden(E - 1, (E - 1) % UNROLL)
                down(E - 1, (E - 1) % UNROLL)

            @block.scalar
            def _(act):
                def weigh(e, u):
                    if not exists(e):
                        return
                    act.wait_ge(d_mm, e + 1)
                    wait_for(act, added, DSTART + (e - UNROLL + 1) * 16 if not isinstance(e, int) or e >= UNROLL
                             else 0)
                    nc.scalar.activation(dsc[u], psum[:, 4 + u % 2, :], ACT.Copy, scale=slots[:, bass.ds(e, 1), 1])\
                        .then_inc(d_out, 1)

                def step(i, u):
                    e = i * UNROLL + u
                    act.wait_ge(g_mm, e + 1)
                    wait_for(act, gu_out, e - 1)
                    nc.scalar.activation(sil[u % 2], psum[:, 2, 0:F], ACT.Silu).then_inc(silu_done, 1)
                    weigh(e - 1, (u - 1) % UNROLL)

                act.wait_ge(tok_ready, 1)
                over_experts(act, step)
                weigh(E - 1, (E - 1) % UNROLL)

            @block.vector
            def _(dve):
                def keep_rows(e, u):
                    if not exists(e):
                        return
                    dve.wait_ge(xt_mm, e + 1)
                    wait_for(dve, u_mm, e - 1)
                    nc.vector.tensor_copy(xeT[u % 2].rearrange("p k c -> p (k c)"), psum[:, 0, :]).then_inc(xt_out, 1)

                def keep_hidden(e, u):
                    if not exists(e):
                        return
                    dve.wait_ge(gt_mm, e + 1)
                    wait_for(dve, d_mm, e - 1)
                    nc.vector.tensor_copy(guT[u % 2][:, 0:FC - 1, :],
                                          psum[:, 1, 0:(FC - 1) * P].rearrange("p (k c) -> p k c", c=P))
                    nc.vector.tensor_copy(guT[u % 2][0:FR, FC - 1, :], psum[0:FR, 1, (FC - 1) * P:FC * P])\
                        .then_inc(gt_out, 1)

                def step(i, u):
                    e = i * UNROLL + u
                    keep_hidden(e - 1, (u - 1) % UNROLL)
                    keep_rows(e + 1, (u + 1) % UNROLL)
                    dve.wait_ge(silu_done, e + 1)
                    dve.wait_ge(u_mm, e + 1)
                    wait_for(dve, gt_mm, e - 1)
                    nc.vector.tensor_tensor(gu[u % 2], sil[u % 2], psum[:, 3, 0:F], ALU.mult).then_inc(gu_out, 1)

                dve.wait_ge(slots_in, 16)
                nc.vector.tensor_copy(slot_tok[:, :], slots[:, :, 0]).then_inc(tok_ready, 1)
                keep_rows(0, 0)
                over_experts(dve, step)
                keep_hidden(E - 1, (E - 1) % UNROLL)

        used[0] = 0
        yt = [carve([P, GT, D]) for _ in range(2)]
        y_in = [sem("y_in0"), sem("y_in1")]
        f_tmp = sem("f_tmp")
        f_done = sem("f_done")
        stored = sem("stored")
        with nc.Block() as block:
            @block.sync
            def _(sp):
                for n in range(NGRP):
                    if n >= 2:
                        sp.wait_ge(f_done, n - 1)
                    sp.dma_start(yt[n % 2], y_rows[:, n * GT:(n + 1) * GT, :]).then_inc(y_in[n % 2], 16)

            @block.scalar
            def _(act):
                for n in range(NGRP):
                    act.wait_ge(f_done, n + 1)
                    act.dma_start(out_rows[:, n * GT:(n + 1) * GT, :], xs[:, n * GT:(n + 1) * GT, :])\
                        .then_inc(stored, 16)
                act.wait_ge(stored, 16 * NGRP)

            @block.vector
            def _(dve):
                for n in range(NGRP):
                    dve.wait_ge(y_in[n % 2], 16 * (n // 2 + 1))
                    for t in range(GT):
                        i_ = nc.vector.tensor_tensor(yt[n % 2][:, t, :], yt[n % 2][:, t, :],
                                                     rowsB[:, 2, n // HB, :], ALU.mult)
                    i_.then_inc(f_tmp, 1)
                    dve.wait_ge(f_tmp, n + 1)
                    nc.vector.tensor_tensor(xs[:, n * GT:(n + 1) * GT, :], xs[:, n * GT:(n + 1) * GT, :], yt[n % 2],
                                            ALU.add).then_inc(f_done, 1)


def lay_out(a):
    import numpy as np

    def per_partition(v):
        return np.ascontiguousarray(np.moveaxis(v.reshape(*v.shape[:-1], -1, P), -1, 0))

    E_ = {}
    E_["x"] = a["L0_attn_x"].reshape(T, D)
    w = a["L0_attn_w_qkv"].reshape(3, NG, P, KD, P)
    E_["wqkv"] = w.transpose(1, 4, 3, 0, 2).reshape(NG, P, KD * 3 * P)
    E_["bqkv"] = a["L0_attn_b_qkv"].reshape(3, NG, P).transpose(2, 0, 1)
    E_["wo"] = a["L0_attn_w_out"].reshape(D, KD, P).transpose(2, 1, 0)
    E_["bo"] = per_partition(a["L0_attn_b_out"])
    E_["gatew"] = a["L0_ffn_gate_w"].reshape(E, KD, P).transpose(2, 1, 0)
    g = a["L0_ffn_w_gate"].reshape(E, KD, P, F)
    u = a["L0_ffn_w_up"].reshape(E, KD, P, F)
    E_["wgu"] = np.concatenate([g, u], axis=3).transpose(0, 2, 1, 3).reshape(E, P, KD * 2 * F)
    E_["wd"] = a["L0_ffn_w_down"]
    cols = []
    for f in range(SC):
        r = slice(f * P, min(FS, (f + 1) * P))
        cols += [a["L0_ffn_sh_gate"][r], a["L0_ffn_sh_up"][r]]
    s = np.concatenate(cols, axis=0)
    E_["shgu"] = s.reshape(2 * FS, KD, P).transpose(2, 1, 0).reshape(P, KD * 2 * FS)
    E_["shd"] = a["L0_ffn_sh_down"].T
    E_["c"] = a["L0_c"].reshape(B, KD, P).transpose(2, 1, 0)
    E_["wmod"] = a["L0_wmod"].reshape(KD, P, 6, D).transpose(2, 1, 0, 3)
    return {k: np.ascontiguousarray(v) for k, v in E_.items()}


def kernel(**inputs):
    import numpy as _np
    import concourse.bacc as _bacc
    from concourse.bass_utils import run_bass_kernel_spmd as _run

    arrays = lay_out({k: _np.asarray(v) for k, v in inputs.items()})
    nc = _bacc.Bacc("TRN2", target_bir_lowering=False, num_devices=1)
    args = {k: nc.dram_tensor(k, v.shape, mybir.dt.from_np(v.dtype), kind="ExternalInput").ap()
            for k, v in arrays.items()}
    o = nc.dram_tensor("out", [T, D], F32, kind="ExternalOutput").ap()
    build(nc, out=o, **args)
    r = _run(nc, [arrays], core_ids=[0])
    return r.results[0]["out"].reshape(B, S, D)
```

```python
from contextlib import ExitStack

import concourse.bass as bass
from concourse import mybir

P = 128
F32 = mybir.dt.float32
F32R = mybir.dt.float32r
BF16 = mybir.dt.bfloat16
U32 = mybir.dt.uint32
ACT = mybir.ActivationFunctionType
ALU = mybir.AluOpType
AX_X = mybir.AxisListType.X

B, S, D = 2, 1024, 512
T = B * S
KD = D // P
NT = T // P
TB = S // P
H, HD = 16, 32
HG = P // HD
NG = H // HG
GT = 4
GN = GT * P
NGRP = T // GN
HB = S // GN
E, F, TOPK, CAP = 64, 352, 6, 128
FC = -(-F // P)
FR = F - (FC - 1) * P
FS = 2 * F
SC = -(-FS // P)
SR = FS - (SC - 1) * P
TD = T + P
EPS = 1e-5
SCALE = float(HD) ** -0.5
MASKED = 1e30
DROPPED = float(1 << 20)
SA, CA, GA, SB, CB, GB = range(6)
START, DSTART = 1, 16
UNROLL = 4


class Arena:

    def __init__(self, tensor, words):
        self.tensor, self.words, self.used = tensor, words, 0

    def carve(self, shape, dt=F32):
        words = 1
        for n in shape[1:]:
            words *= n
        if dt is BF16:
            words = (words + 1) // 2
        v = self.tensor[0:shape[0], self.used:self.used + words]
        self.used += words
        assert self.used <= self.words, (self.used, self.words)
        if dt is not F32:
            v = v.bitcast(dt)
        if len(shape) == 3:
            v = v.rearrange("p (a b) -> p a b", b=shape[2])
        elif len(shape) == 4:
            v = v.rearrange("p (a b c) -> p a b c", b=shape[2], c=shape[3])
        return v


def build(nc, x, wqkv, bqkv, wo, bo, gatew, wgu, wd, shgu, shd, c, wmod, out):
    x_rows = x.rearrange("(t p) d -> p t d", p=P)
    out_rows = out.rearrange("(t p) d -> p t d", p=P)
    h2_dram = nc.dram_tensor("h2_dram", [TD, D], F32, kind="Internal").ap()
    y_dram = nc.dram_tensor("y_dram", [TD, D], F32, kind="Internal").ap()
    oT_dram = nc.dram_tensor("oT_dram", [D, T], F32, kind="Internal").ap()
    slot_dram = nc.dram_tensor("slot_dram", [CAP * E, 2], F32, kind="Internal").ap()
    h2_rows = h2_dram.rearrange("(t p) d -> p t d", p=P)
    y_rows = y_dram.rearrange("(t p) d -> p t d", p=P)
    oT_cols = oT_dram.rearrange("(k p) t -> p k t", p=P)

    with ExitStack() as ctx:
        def sb(name, shape, dt=F32, scope=ctx):
            return scope.enter_context(nc.sbuf_tensor(name, shape, dt))

        def sem(name):
            return ctx.enter_context(nc.semaphore(name))

        def wait_alone(eng, what, value):
            eng.wait_ge(what, value)
            eng.nop(nofuse=True)

        psum = ctx.enter_context(nc.psum_tensor("psum", [P, 8, 512], F32))

        ident = sb("ident", [P, P])
        ident_bf = sb("ident_bf", [P, P], BF16)
        mask_bf = sb("mask_bf", [P, P], BF16)
        before_bf = sb("before_bf", [P, P], BF16)
        ones_bf = sb("ones_bf", [P, P], BF16)
        ones = sb("ones", [P, P])
        modT = sb("modT", [P, 6, KD, B])
        rowsB = sb("rowsB", [P, 3, B, D])
        bq = sb("bq", [P, 3, NG])
        boT = sb("boT", [P, KD])
        iota_e = sb("iota_e", [P, E])
        tok_id = sb("tok_id", [P, GT])

        attention_scope = ctx.enter_context(ExitStack())
        hT = sb("hT", [P, KD, T], scope=attention_scope)

        scope = ExitStack()
        xs = sb("xs1", [P, NT, D], scope=scope)
        words1 = 16 * 1024
        carve = Arena(sb("arena1", [P, words1], scope=scope), words1).carve
        cT = carve([P, KD, B])
        cs = carve([P, KD, B])
        wm = [carve([P, KD, D]) for _ in range(2)]
        xn = carve([P, 2, GT * D]).rearrange("p n (t d) -> p n t d", d=D)
        stats = carve([P, TB, 6])
        mv = carve([P, TB, 2])
        var = carve([P, TB])
        std = carve([P, TB])
        rstd = carve([P, TB])
        clamp = carve([P, KD, B])
        diag = [carve([P, P]) for _ in range(2)]
        zeros = carve([P, D])
        empty = carve([P, E, 2])

        small_in = sem("small_in")
        x_in = sem("x_in")
        wm_in = [sem(f"wm_in{i}") for i in range(2)]
        const_v = sem("const_v")
        const_g = sem("const_g")
        c_silu = sem("c_silu")
        mod_mm = sem("mod_mm")
        mod_out = sem("mod_out")
        mod_fix = sem("mod_fix")
        diag_ready = sem("diag_ready")
        row_mm = sem("row_mm")
        row_out = sem("row_out")
        ln_v = sem("ln_v")
        ln_var = sem("ln_var")
        ln_std = sem("ln_std")
        xn_ready = sem("xn_ready")
        h_mm = sem("h_mm")
        h_out = sem("h_out")
        init_out = sem("init_out")
        scattered = sem("scattered")
        added = sem("added")
        ROW_SRC = (CB, SB, GB)

        with nc.Block() as block:
            @block.sync
            def _(sp):
                sp.dma_start(cT, c).then_inc(small_in, 16)
                sp.dma_start(bq[:, :, :], bqkv).then_inc(small_in, 16)
                sp.dma_start(boT[:, :], bo).then_inc(small_in, 16)
                for w in range(6):
                    if w >= 2:
                        sp.wait_ge(mod_mm, w - 1)
                    sp.dma_start(wm[w % 2], wmod[w]).then_inc(wm_in[w % 2], 16)
                    if w < NT // GT:
                        if w:
                            sp.wait_ge(x_in, 16 * w)
                        sp.dma_start(xs[:, w * GT:(w + 1) * GT, :], x_rows[:, w * GT:(w + 1) * GT, :])\
                            .then_inc(x_in, 16)
                sp.wait_ge(const_v, 5)
                sp.wait_ge(const_g, 7)
                n_init = 0
                for t in range(NT):
                    sp.dma_start(y_rows[:, t, :], zeros).then_inc(init_out, 16)
                    n_init += 1
                sp.dma_start(slot_dram.rearrange("(p e) w -> p e w", e=E), empty).then_inc(init_out, 16)
                sp.wait_ge(init_out, 16 * (n_init + 1))

            @block.gpsimd
            def _(pool):
                nc.gpsimd.iota(iota_e[:, :], [[1, E]], base=0, channel_multiplier=0,
                               allow_small_or_imprecise_dtypes=True).then_inc(const_g, 1)
                nc.gpsimd.iota(tok_id[:, :], [[P, GT]], base=0, channel_multiplier=1,
                               allow_small_or_imprecise_dtypes=True).then_inc(const_g, 1)
                nc.gpsimd.iota(empty[:, :, 0], [[0, E]], base=T, channel_multiplier=1,
                               allow_small_or_imprecise_dtypes=True).then_inc(const_g, 1)
                pool.wait_ge(const_v, 5)
                nc.gpsimd.affine_select(out=ident[:, :], in_=ident[:, :], compare_op=ALU.not_equal, fill=1.0,
                                        base=0, pattern=[[-1, P]], channel_multiplier=1).then_inc(const_g, 1)
                nc.gpsimd.affine_select(out=ident_bf[:, :], in_=ident_bf[:, :], compare_op=ALU.not_equal,
                                        fill=1.0, base=0, pattern=[[-1, P]], channel_multiplier=1)\
                    .then_inc(const_g, 1)
                nc.gpsimd.affine_select(out=mask_bf[:, :], in_=mask_bf[:, :], compare_op=ALU.is_ge, fill=MASKED,
                                        base=0, pattern=[[-1, P]], channel_multiplier=1).then_inc(const_g, 1)
                nc.gpsimd.affine_select(out=before_bf[:, :], in_=ones_bf[:, :], compare_op=ALU.is_gt, fill=0.0,
                                        base=0, pattern=[[1, P]], channel_multiplier=-1).then_inc(const_g, 1)
                pool.dma_start(h2_rows[:, NT, :], zeros).then_inc(scattered, 16)
                pool.dma_start(y_rows[:, NT, :], zeros).then_inc(added, 16)
                pool.wait_ge(scattered, 16)
                pool.wait_ge(added, 16)

            @block.tensor
            def _(pe):
                pe.sem_inc(h_mm, START)
                pe.wait_ge(c_silu, 1)
                for w in range(6):
                    pe.wait_ge(wm_in[w % 2], 16 * (w // 2 + 1))
                    if w >= 2:
                        pe.wait_ge(mod_out, w - 1)
                    for j in range(KD):
                        for k in range(KD):
                            last = nc.tensor.matmul(psum[:, 7 * (w % 2), j * B:(j + 1) * B],
                                                    wm[w % 2][:, k, j * P:(j + 1) * P], cs[:, k, :],
                                                    start=(k == 0), stop=(k == KD - 1))
                    last.then_inc(mod_mm, 1)
                pe.wait_ge(const_v, 5)
                for n in range(3 * B):
                    for k in range(KD):
                        pe.wait_ge(diag_ready, n * KD + k + 1)
                        last = nc.tensor.matmul(psum[:, 1 + n, k * P:(k + 1) * P], ones[:, :],
                                                diag[(n * KD + k) % 2], start=True, stop=True)
                        last.then_inc(row_mm, 1)
                pe.wait_ge(const_g, 7)
                pe.wait_ge(row_out, 3 * B)
                with pe.Fori(0, B) as b:
                    for n in range(2):
                        pe.wait_ge(h_out, START + b * 2 * KD)
                        for t in range(GT):
                            pe.wait_ge(xn_ready, b * TB + n * GT + t + 1)
                            for k in range(KD):
                                last = nc.tensor.transpose(psum[:, n * KD + k, t * P:(t + 1) * P],
                                                           xn[:, n, t, k * P:(k + 1) * P], ident[:, :])
                        last.then_inc(h_mm, 1)

            @block.scalar
            def _(act):
                act.sem_inc(h_out, START)
                act.wait_ge(small_in, 48)
                nc.scalar.activation(cs, cT, ACT.Silu).then_inc(c_silu, 1)
                with act.Fori(0, B) as b:
                    act.wait_ge(ln_var, b + 1)
                    nc.scalar.activation(std, var, ACT.Sqrt).then_inc(ln_std, 1)
                    act.wait_ge(mod_fix, 5)
                    for n in range(2):
                        act.wait_ge(h_mm, START + b * 2 + n + 1)
                        for k in range(KD):
                            nc.scalar.activation(hT[:, k, bass.ds(b * S + n * GN, GN)], psum[:, n * KD + k, :],
                                                 ACT.Identity, bias=modT[:, SA, k, bass.ds(b, 1)],
                                                 scale=modT[:, CA, k, bass.ds(b, 1)]).then_inc(h_out, 1)

            @block.vector
            def _(dve):
                nc.vector.memset(ident[:, :], 0.0).then_inc(const_v, 1)
                nc.vector.memset(ident_bf[:, :], 0.0).then_inc(const_v, 1)
                nc.vector.memset(mask_bf[:, :], 0.0).then_inc(const_v, 1)
                nc.vector.memset(ones_bf[:, :], 1.0).then_inc(const_v, 1)
                nc.vector.memset(zeros, 0.0)
                nc.vector.memset(empty[:, :, 1], 0.0)
                nc.vector.memset(ones[:, :], 1.0).then_inc(const_v, 1)
                for w in range(6):
                    dve.wait_ge(mod_mm, w + 1)
                    nc.vector.tensor_copy(modT[:, w, :, :].rearrange("p k b -> p (k b)"),
                                          psum[:, 7 * (w % 2), 0:KD * B]).then_inc(mod_out, 1)
                dve.wait_ge(mod_out, 6)
                fixed = 0
                for w in (CA, CB):
                    nc.vector.tensor_scalar(modT[:, w, :, :], modT[:, w, :, :], 1.0, None, ALU.add)\
                        .then_inc(mod_fix, 1)
                    fixed += 1
                for w in (GA, GB):
                    nc.vector.tensor_scalar(clamp, modT[:, w, :, :], -0.25, None, ALU.min).then_inc(mod_fix, 1)
                    nc.vector.tensor_scalar(cT, modT[:, w, :, :], 0.0, None, ALU.is_ge).then_inc(mod_fix, 1)
                    nc.vector.tensor_scalar(modT[:, w, :, :], modT[:, w, :, :], 0.25, None, ALU.max)\
                        .then_inc(mod_fix, 1)
                    fixed += 3
                    dve.wait_ge(mod_fix, fixed)
                    nc.vector.tensor_tensor(modT[:, w, :, :], modT[:, w, :, :], clamp, ALU.subtract)\
                        .then_inc(mod_fix, 1)
                    fixed += 1
                    dve.wait_ge(mod_fix, fixed)
                    nc.vector.tensor_tensor(modT[:, w, :, :], modT[:, w, :, :], cT, ALU.mult).then_inc(mod_fix, 1)
                    fixed += 1
                    dve.wait_ge(mod_fix, fixed)
                    nc.vector.tensor_tensor(modT[:, w, :, :], modT[:, w, :, :], clamp, ALU.add)\
                        .then_inc(mod_fix, 1)
                    fixed += 1
                    dve.wait_ge(mod_fix, fixed)
                dve.wait_ge(const_g, 4)
                for n in range(3 * B):
                    r, b = divmod(n, B)
                    for k in range(KD):
                        m = n * KD + k
                        if m >= 2:
                            dve.wait_ge(row_mm, m - 1)
                        nc.vector.tensor_scalar(diag[m % 2], ident[:, :], modT[:, ROW_SRC[r], k, b:b + 1], None,
                                                ALU.mult).then_inc(diag_ready, 1)
                for n in range(3 * B):
                    dve.wait_ge(row_mm, (n + 1) * KD)
                    nc.vector.tensor_copy(rowsB[:, n // B, n % B, :], psum[:, 1 + n, :]).then_inc(row_out, 1)
                with dve.Fori(0, B) as b:
                    dve.wait_ge(x_in, b * 32 + 32)
                    for t in range(TB):
                        nc.vector.bn_stats(stats[:, t, :], xs[:, b * TB + t, :]).then_inc(ln_v, 1)
                    wait_alone(dve, ln_v, b * 17 + 8)
                    for t in range(TB):
                        nc.vector.bn_aggr(mv[:, t, :], stats[:, t, :]).then_inc(ln_v, 1)
                    dve.wait_ge(ln_v, b * 17 + 16)
                    nc.vector.tensor_scalar(var, mv[:, :, 1], EPS, None, ALU.add).then_inc(ln_var, 1)
                    dve.wait_ge(ln_std, b + 1)
                    nc.vector.reciprocal(rstd, std).then_inc(ln_v, 1)
                    dve.wait_ge(ln_v, b * 17 + 17)
                    for t in range(TB):
                        n = t // GT
                        if t % GT == 0:
                            dve.wait_ge(h_mm, START + b * 2)
                        nc.vector.tensor_scalar(xn[:, n, t % GT, :], xs[:, b * TB + t, :], mv[:, t, 0:1],
                                                rstd[:, t:t + 1], ALU.subtract, ALU.mult).then_inc(xn_ready, 1)
        scope.close()

        scope = ExitStack()
        qs = [sb(f"qs{b}", [P, HG, S], F32R, scope) for b in range(B)]
        ks = [sb(f"ks{b}", [P, HG, S], F32R, scope) for b in range(B)]
        words2 = 23552
        carve = Arena(sb("arena2", [P, words2], scope=scope), words2).carve
        wg = carve([P, KD * 3, P])
        part_hi = [carve([P, S]) for _ in range(2)]
        part_lo = [carve([P, S]) for _ in range(2)]
        vT = carve([P, S])
        v = [carve([P, TB, P]) for _ in range(B)]
        prob = carve([P, 4, S])
        pT = carve([P, 2, HG, TB * P])
        low = carve([P, 2, HG])
        den = carve([P, 2, HG])
        rden = carve([P, 2, HG])
        rden_T = carve([P, 2, P])
        bqs = carve([P, NG])
        oS = carve([P, B, S])

        wg_in = sem("wg_in")
        bqs_ready = sem("bqs_ready")
        t_ready = [sem("t_ready_act"), sem("t_ready_dve")]
        t_free = [sem("t_free_act"), sem("t_free_dve")]
        split_done = sem("split_done")
        parts_in = [sem("parts_in0"), sem("parts_in1")]
        s_ready = sem("s_ready")
        low_ready = sem("low_ready")
        probs = sem("probs")
        pv_done = sem("pv_done")
        rden_ready = sem("rden_ready")
        rb_done = sem("rb_done")
        rb_copied = sem("rb_copied")
        o_done = sem("o_done")
        o_stored = [sem("o_stored0"), sem("o_stored1")]

        BANKS = (4, 5)
        O_BANKS = (6, 7)
        units = [(i, h) for i in range(TB) for h in range(HG)]
        NU = len(units)
        PROJ = [("q", 0), ("q", 1), ("k", 0), ("k", 1), ("v", 0), ("v", 1), ("vt", 0), ("vt", 1)]
        AFTER = dict(zip((1, 3, 5, 7, 9, 11, 14, 15), range(len(PROJ))))
        NP = len(PROJ)
        DMAS = 2 * 16
        uses, of_unit, of_proj = [], [], [None] * NP
        for n, (i, h) in enumerate(units):
            of_unit.append([])
            for j0 in range(0, i + 1, 4):
                of_unit[-1].append(len(uses))
                uses.append((i, h, j0))
            if n in AFTER:
                of_proj[AFTER[n]] = len(uses)
                uses.append(PROJ[AFTER[n]])
        assert len(uses) % 2 == 0
        PER = len(uses) // 2
        SPLITS = 4

        def use_no(it, m):
            return m // 2 if it is None else NP // 2 + it * PER + m // 2

        def s_bank(n):
            return psum[:, 2 * (n % 2):2 * (n % 2) + 2, :].rearrange("p a b -> p (a b)")

        def pairs(step):
            def run(eng):
                with eng.Fori(0, NG - 1) as g:
                    for b in range(B):
                        step(g, b, False)
                for b in range(B):
                    step(NG - 1, b, b == B - 1)
            return run

        def uses_after(n, last):
            return [] if last or n not in AFTER else [(AFTER[n], of_proj[AFTER[n]])]

        def unit_use(m, last):
            return m if not last else m - sum(1 for q in of_proj if q < m)

        def successor(g, b):
            return (g, 1) if b == 0 else (g + 1, 0)

        def empty_proj(eng, mine, it, p, m, g, b):
            eng.wait_ge(t_ready[mine], use_no(it, m) + 1)
            kind, n = PROJ[p]
            src = psum[:, BANKS[mine], :]
            half = slice(n * GN, (n + 1) * GN)

            def project(dst, part, scale, bias):
                bias = bias[:, g:g + 1] if isinstance(g, int) else bias[:, bass.ds(g, 1)]
                if mine == 0:
                    return nc.scalar.activation(dst, src, ACT.Identity, bias=bias, scale=scale)
                return nc.vector.tensor_scalar(dst, src, scale, bias, ALU.mult, ALU.add)

            if kind in ("q", "k"):
                part = "qk".index(kind)
                args = (part, (-SCALE, 1.0)[part], (bqs, bq[:, 1, :])[part])
                project(part_lo[part][:, half], *args)
                project(part_hi[part][:, half].bitcast(F32R), *args).then_inc(t_free[mine], 1)
            elif kind == "v":
                project(vT[:, half], 2, 1.0, bq[:, 2, :]).then_inc(t_free[mine], 1)
            else:
                dst = v[b][:, n * 4:n * 4 + 4, :].rearrange("p a b -> p (a b)")
                ins = nc.scalar.copy(dst, src) if mine == 0 else nc.vector.tensor_copy(dst, src)
                ins.then_inc(t_free[mine], 1)

        def empty_unit(eng, mine, it, m, last):
            i, h, j0 = uses[m]
            mu = unit_use(m, last)
            if mu % 2 != mine:
                return
            eng.wait_ge(t_ready[mine], use_no(it, mu) + 1)
            w = (min(i + 1, j0 + 4) - j0) * P
            if i >= 2:
                eng.wait_ge(pv_done, it * TB + i - 1)
            dst = pT[:, i % 2, h, j0 * P:j0 * P + w]
            src = psum[:, BANKS[mine], 0:w]
            ins = nc.scalar.copy(dst, src) if mine == 0 else nc.vector.tensor_copy(dst, src)
            ins.then_inc(t_free[mine], 1)

        def split(dve, it, p, m):
            kind, n = PROJ[p]
            if kind not in ("q", "k"):
                return
            mine = m % 2
            part = "qk".index(kind)
            half = slice(n * GN, (n + 1) * GN)
            dve.wait_ge(t_free[mine], START + use_no(it, m) + 1)
            nc.vector.tensor_tensor(part_lo[part][:, half], part_lo[part][:, half], part_hi[part][:, half],
                                    ALU.subtract).then_inc(split_done, 1)

        with nc.Block() as block:
            @block.sync
            def _(sp):
                def load_w(g):
                    sp.dma_start(wg, wqkv[g].rearrange("p (a c) -> p a c", c=P)).then_inc(wg_in, 16)

                def lay_parts(splits, b):
                    for part, buf, which in ((0, qs[b], (0, 0, 1, 1)), (1, ks[b], (0, 1, 0, 1))):
                        sp.wait_ge(split_done, splits + 2 * (part + 1))
                        for h in range(HG):
                            for row, lo in enumerate(which):
                                src = (part_lo if lo else part_hi)[part]
                                sp.dma_start(buf[row * HD:(row + 1) * HD, h, :].bitcast(F32),
                                             src[h * HD:(h + 1) * HD, :]).then_inc(parts_in[b], 16)

                def step(g, b, last):
                    it = g * B + b
                    if not last:
                        lay_parts(it * SPLITS + SPLITS, successor(g, b)[1])
                    if b == 0 and not isinstance(g, int):
                        m = of_proj[5]
                        sp.wait_ge(t_ready[m % 2], use_no(it, m) + 1)
                        load_w(g + 1)
                    sp.wait_ge(o_done, START + it * TB + TB)
                    sp.dma_start(oT_cols[:, g, b * S:(b + 1) * S] if isinstance(g, int) else
                                 oT_cols[:, bass.ds(g, 1), b * S:(b + 1) * S].rearrange("p a t -> p (a t)"),
                                 oS[:, b, :]).then_inc(o_stored[b], 16)

                for b in range(B):
                    sp.sem_inc(o_stored[b], DSTART)
                load_w(0)
                lay_parts(0, 0)
                pairs(step)(sp)
                for b in range(B):
                    sp.wait_ge(o_stored[b], DSTART + 16 * NG)

            @block.tensor
            def _(pe):
                def project(it, p, m, g, b, n_w):
                    kind, n = PROJ[p]
                    if p == 0:
                        pe.wait_ge(wg_in, n_w * 16)
                    pe.wait_ge(t_free[m % 2], START + use_no(it, m))
                    if kind == "vt":
                        mv = (4 + n) if it is None else of_proj[4 + n]
                        pe.wait_ge(t_free[mv % 2], START + use_no(it, mv) + 1)
                        for j in range(4):
                            last = nc.tensor.transpose(psum[:, BANKS[m % 2], j * P:(j + 1) * P],
                                                       vT[:, (n * 4 + j) * P:(n * 4 + j + 1) * P], ident[:, :])
                    else:
                        part = "qkv".index(kind)
                        for k in range(KD):
                            last = nc.tensor.matmul(psum[:, BANKS[m % 2], :], wg[:, k * 3 + part, :],
                                                    hT[:, k, b * S + n * GN:b * S + (n + 1) * GN],
                                                    start=(k == 0), stop=(k == KD - 1))
                    last.then_inc(t_ready[m % 2], 1)

                def scores(it, b, n):
                    i, h = units[n]
                    if n >= 2:
                        pe.wait_ge(probs, it * NU + n - 1)
                    s = s_bank(n)
                    w = (i + 1) * P
                    for a in range(0, w, 512):
                        e = min(w, a + 512)
                        nc.tensor.matmul(s[:, a:e], qs[b][:, h, i * P:(i + 1) * P], ks[b][:, h, a:e],
                                         start=True, stop=(e < w))
                    nc.tensor.matmul(s[:, i * P:w], ident_bf[:, :], mask_bf[:, :], start=False, stop=True)\
                        .then_inc(s_ready, 1)

                def turn(it, n, last_it):
                    i, h = units[n]
                    pe.wait_ge(probs, it * NU + n + 1)
                    for m in of_unit[n]:
                        j0 = uses[m][2]
                        mu = unit_use(m, last_it)
                        pe.wait_ge(t_free[mu % 2], START + use_no(it, mu))
                        for j in range(j0, min(i + 1, j0 + 4)):
                            last = nc.tensor.transpose(psum[:, BANKS[mu % 2], (j - j0) * P:(j - j0 + 1) * P],
                                                       prob[:, n % 4, j * P:(j + 1) * P], ident[:, :])
                        last.then_inc(t_ready[mu % 2], 1)

                def values(it, b, i, last_it):
                    mu = unit_use(of_unit[4 * i + 3][-1], last_it)
                    for m in (mu - 1, mu):
                        pe.wait_ge(t_free[m % 2], START + use_no(it, m) + 1)
                    if i == 0:
                        pe.wait_ge(o_done, START + it * TB)
                    elif i >= 2:
                        pe.wait_ge(o_done, START + it * TB + i - 1)
                    bank = O_BANKS[i % 2]
                    for j in range(i + 1):
                        for h in range(HG):
                            last = nc.tensor.matmul(psum[h * HD:(h + 1) * HD, bank, 0:P],
                                                    v[b][:, j, h * HD:(h + 1) * HD], pT[:, i % 2, h, j * P:(j + 1) * P],
                                                    start=(j == 0), stop=(j == i))
                    last.then_inc(pv_done, 1)
                    pe.wait_ge(rden_ready, START + it * TB + i + 1)
                    for h in range(HG):
                        last = nc.tensor.matmul(psum[h * HD:(h + 1) * HD, bank, P:2 * P],
                                                rden[:, i % 2, h:h + 1].broadcast_to([P, HD]), ident[:, :],
                                                start=True, stop=True)
                    last.then_inc(rb_done, 1)

                def step(g, b, last):
                    it = g * B + b
                    g2, b2 = successor(g, b)
                    for n in range(NU):
                        turn(it, n, last)
                        if n + 2 < NU:
                            scores(it, b, n + 2)
                        for p, m in uses_after(n, last):
                            project(it, p, m, g2, b2, g2 + 1)
                        if n % HG == 0 and n:
                            values(it, b, n // HG - 1, last)
                    if not last:
                        pe.wait_ge(parts_in[b2], (g2 + 1) * DMAS * 16)
                        scores(it + 1, b2, 0)
                        scores(it + 1, b2, 1)
                    values(it, b, TB - 1, last)

                for p in range(NP):
                    project(None, p, p, 0, 0, 1)
                pe.wait_ge(parts_in[0], DMAS * 16)
                scores(0, 0, 0)
                scores(0, 0, 1)
                pairs(step)(pe)

            @block.scalar
            def _(act):
                act.sem_inc(t_free[0], START)
                act.wait_ge(bqs_ready, 1)

                def exps(it, n):
                    i, h = units[n]
                    w = (i + 1) * P
                    act.wait_ge(low_ready, it * NU + n + 1)
                    if h == 0 and not (isinstance(it, int) and i < 2):
                        act.wait_ge(rden_ready, START + it * TB + i - 1)
                    nc.scalar.activation(prob[:, n % 4, 0:w], s_bank(n)[:, 0:w], ACT.Exp,
                                         bias=low[:, i % 2, h:h + 1], scale=-1.0,
                                         accum_out=den[:, i % 2, h:h + 1]).then_inc(probs, 1)

                def step(g, b, last):
                    it = g * B + b
                    g2, b2 = successor(g, b)
                    for n in range(NU):
                        for m in of_unit[n]:
                            empty_unit(act, 0, it, m, last)
                        if n + 2 < NU:
                            if n >= 2:
                                mu = unit_use(of_unit[n - 2][-1], last)
                                act.wait_ge(t_ready[mu % 2], use_no(it, mu) + 1)
                            exps(it, n + 2)
                        for p, m in uses_after(n, last):
                            if m % 2 == 0:
                                empty_proj(act, 0, it, p, m, g2, b2)
                    if not last:
                        exps(it + 1, 0)
                        exps(it + 1, 1)

                for p in range(0, NP, 2):
                    empty_proj(act, 0, None, p, p, 0, 0)
                exps(0, 0)
                exps(0, 1)
                pairs(step)(act)

            @block.vector
            def _(dve):
                dve.sem_inc(t_free[1], START)
                dve.sem_inc(o_done, START)
                dve.sem_inc(rden_ready, START)
                nc.vector.tensor_scalar(bqs, bq[:, 0, :], -SCALE, None, ALU.mult).then_inc(bqs_ready, 1)
                dve.wait_ge(bqs_ready, 1)

                def lows(it, n):
                    i, h = units[n]
                    dve.wait_ge(s_ready, it * NU + n + 1)
                    nc.vector.tensor_reduce(low[:, i % 2, h:h + 1], s_bank(n)[:, 0:(i + 1) * P], AX_X, ALU.min)\
                        .then_inc(low_ready, 1)

                def combine(it, i, b, g):
                    dve.wait_ge(rb_done, it * TB + i + 1)
                    if i == 0:
                        dve.wait_ge(o_stored[b], DSTART + g * 16)
                    nc.vector.tensor_copy(rden_T[:, i % 2, :], psum[:, O_BANKS[i % 2], P:2 * P])\
                        .then_inc(rb_copied, 1)
                    dve.wait_ge(rb_copied, it * TB + i + 1)
                    nc.vector.tensor_tensor(oS[:, b, i * P:(i + 1) * P], psum[:, O_BANKS[i % 2], 0:P],
                                            rden_T[:, i % 2, :], ALU.mult).then_inc(o_done, 1)

                def step(g, b, last):
                    it = g * B + b
                    g2, b2 = successor(g, b)
                    for n in range(NU):
                        for m in of_unit[n]:
                            empty_unit(dve, 1, it, m, last)
                        if n + 2 < NU:
                            lows(it, n + 2)
                        if n - 1 in AFTER and not last:
                            split(dve, it, AFTER[n - 1], of_proj[AFTER[n - 1]])
                        for p, m in uses_after(n, last):
                            if m % 2 == 1:
                                empty_proj(dve, 1, it, p, m, g2, b2)
                        if n % HG == HG - 1:
                            i = n // HG
                            dve.wait_ge(probs, it * NU + n + 1)
                            nc.vector.reciprocal(rden[:, i % 2, :], den[:, i % 2, :]).then_inc(rden_ready, 1)
                        if n % HG == 0 and n:
                            combine(it, n // HG - 1, b, g)
                    if not last:
                        lows(it + 1, 0)
                        lows(it + 1, 1)
                    combine(it, TB - 1, b, g)

                for p in range(NP):
                    if p % 2 == 1:
                        empty_proj(dve, 1, None, p, p, 0, 0)
                    split(dve, None, p, p)
                lows(0, 0)
                lows(0, 1)
                pairs(step)(dve)
        scope.close()
        attention_scope.close()

        xs = sb("xs", [P, NT, D])
        hT = sb("late_a", [P, KD, T])
        oT = sb("late_b", [P, KD, T])
        arena = sb("arena", [P, 20 * 1024])
        used = [0]

        def carve(shape, dt=F32, at=None):
            n = 1
            for s in shape[1:]:
                n *= s
            words = n if dt is not BF16 else (n + 1) // 2
            start = used[0] if at is None else at
            if at is None:
                used[0] += words
                assert used[0] <= 20 * 1024, used[0]
            v = arena[0:shape[0], start:start + words]
            if dt is not F32:
                v = v.bitcast(dt)
            if len(shape) == 3:
                v = v.rearrange("p (a b) -> p a b", b=shape[2])
            elif len(shape) == 4:
                v = v.rearrange("p (a b c) -> p a b c", b=shape[2], c=shape[3])
            return v

        woT = carve([P, KD, D])
        gw = carve([P, KD, E])
        sgu = carve([P, KD * (2 * SC - 1), P])
        sd = carve([P, SC, D])
        yT = carve([P, KD, GN])
        h2 = yT.rearrange("p k (t x) -> p (k t x)", x=P).rearrange("p (t d) -> p t d", d=D)
        h2T = carve([P, KD, GN])
        guS = carve([P, SC, GN])
        silu = hT[:, 0, 0:2 * GN].rearrange("p (a b) -> p a b", b=GN)
        x_mod = hT[:, 1, 0:2 * D].rearrange("p (a b) -> p a b", b=D)
        scr = hT[:, 2, :]
        hot = scr[:, 0:GT * TOPK * E].rearrange("p (t k e) -> p t k e", k=TOPK, e=E)
        scr2 = hT[:, 3, :]
        hot_pos = scr2[:, 0:GT * TOPK * E].rearrange("p (t k e) -> p t k e", k=TOPK, e=E)
        c3 = [0]
        base3 = hT[:, 1, 2 * D:T]

        def c3arve(shape, dt=F32):
            n = 1
            for q in shape[1:]:
                n *= q
            words = n if dt is not BF16 else (n + 1) // 2
            vv = base3[:, c3[0]:c3[0] + words]
            c3[0] += words
            assert c3[0] <= T - 2 * D
            if dt is not F32:
                vv = vv.bitcast(dt)
            if len(shape) == 3:
                vv = vv.rearrange("p (a b) -> p a b", b=shape[2])
            if len(shape) == 4:
                vv = vv.rearrange("p (a b c) -> p a b c", b=shape[2], c=shape[3])
            return vv

        stats3 = c3arve([P, GT, 6])
        mv3 = c3arve([P, GT, 2])
        var3 = c3arve([P, GT])
        std3 = c3arve([P, GT])
        rstd3 = c3arve([P, GT])
        boga = c3arve([P, KD, B])
        lmax = c3arve([P, GT])
        lsub = c3arve([P, GT, E])
        lexp = c3arve([P, GT, E])
        lsum = c3arve([P, GT])
        lrec = c3arve([P, GT])
        top = sb("top", [P, GT, 8])
        top_i = sb("top_i", [P, GT, 8], U32)
        top_f = c3arve([P, GT, 8])
        picked = sb("picked", [P, GT, E], BF16)
        carry = sb("carry", [P, E])
        carry_bf = sb("carry_bf", [P, E], BF16)
        gsum = sb("gsum", [P, E])
        pos_k = sb("pos_k", [P, GT, TOPK])
        over = sb("over", [P, GT, TOPK])
        dest = sb("dest", [P, GT, TOPK])
        dest_u = sb("dest_u", [P, GT, TOPK], U32)
        entry = sb("entry", [P, GT, TOPK, 2])

        w3_in = sem("w3_in")
        wo_in = sem("wo_in")
        oT_in = sem("oT_in")
        x3_in = sem("x3_in")
        bg_ready = sem("bg_ready")
        y_mm = sem("y_mm")
        y_act = sem("y_act")
        y_dve = sem("y_dve")
        yt_mm = sem("yt_mm")
        x1_done = sem("x1_done")
        l2_v = sem("l2_v")
        l2_var = sem("l2_var")
        l2_std = sem("l2_std")
        h2_ready = sem("h2_ready")
        h2_out = sem("h2_out")
        h2t_mm = sem("h2t_mm")
        h2t_act = sem("h2t_act")
        h2t_dve = sem("h2t_dve")
        lg_mm = sem("lg_mm")
        r_v = sem("r_v")
        r_sub = sem("r_sub")
        r_exp = sem("r_exp")
        pick_ready = sem("pick_ready")
        pos_mm = sem("pos_mm")
        dest_ready = sem("dest_ready")
        gu_mm = sem("gu_mm")
        gu_silu = sem("gu_silu")
        gu_done = sem("gu_done")
        sd_mm = sem("sd_mm")
        sd_tmp = sem("sd_tmp")
        sd_done = sem("sd_done")

        with nc.Block() as block:
            @block.sync
            def _(sp):
                sp.sem_inc(h2_out, DSTART)
                sp.dma_start(woT, wo).then_inc(wo_in, 16)
                sp.dma_start(oT[:, :, 0:GN], oT_cols[:, :, 0:GN]).then_inc(oT_in, 16)
                sp.dma_start(xs[:, 0:GT, :], x_rows[:, 0:GT, :]).then_inc(x3_in, 16)
                sp.dma_start(gw, gatew).then_inc(w3_in, 16)
                sp.dma_start(sgu, shgu.rearrange("p (a c) -> p a c", c=P)).then_inc(w3_in, 16)
                sp.dma_start(sd[:, 0:SC - 1, :], shd[0:(SC - 1) * P, :].rearrange("(a p) d -> p a d", p=P))\
                    .then_inc(w3_in, 16)
                sp.dma_start(sd[0:SR, SC - 1, :], shd[(SC - 1) * P:FS, :]).then_inc(w3_in, 16)
                sp.dma_start(oT[:, :, GN:T], oT_cols[:, :, GN:T]).then_inc(oT_in, 16)
                sp.dma_start(xs[:, GT:NT, :], x_rows[:, GT:NT, :]).then_inc(x3_in, 16)
                with sp.Fori(0, NGRP) as it:
                    sp.wait_ge(h2_ready, it * GT + GT)
                    sp.dma_start(h2_rows[:, bass.ds(it * GT, GT), :], h2).then_inc(h2_out, 16)
                sp.wait_ge(h2_out, DSTART + 16 * NGRP)

            @block.gpsimd
            def _(pool):
                with pool.Fori(0, NGRP) as it:
                    wait_alone(pool, dest_ready, it + 1)
                    for t in range(GT):
                        for k in range(TOPK):
                            pool.indirect_dma_start(
                                out=slot_dram, out_offset=bass.IndirectOffsetOnAxis(ap=dest_u[:, t, k:k + 1], axis=0),
                                in_=entry[:, t, k, :], in_offset=None, bounds_check=CAP * E - 1,
                                oob_is_err=False).then_inc(scattered, 16)
                pool.wait_ge(scattered, DSTART + NGRP * GT * TOPK * 16)

            @block.tensor
            def _(pe):
                pe.wait_ge(wo_in, 16)
                pe.wait_ge(oT_in, 32)
                with pe.Fori(0, NGRP) as it:
                    pe.wait_ge(sd_done, START + it * GT)
                    for j in range(KD):
                        for k in range(KD):
                            last = nc.tensor.matmul(psum[:, j, :], woT[:, k, j * P:(j + 1) * P],
                                                    oT[:, k, bass.ds(it * GN, GN)], start=(k == 0), stop=(k == KD - 1))
                        last.then_inc(y_mm, 1)
                    pe.wait_ge(y_act, it * 2 + 2)
                    pe.wait_ge(y_dve, it * 2 + 2)
                    for t in range(GT):
                        for j in range(KD):
                            last = nc.tensor.transpose(psum[:, 4 + t, j * P:(j + 1) * P],
                                                       yT[:, j, t * P:(t + 1) * P], ident[:, :])
                        last.then_inc(yt_mm, 1)
                    for t in range(GT):
                        pe.wait_ge(h2_ready, it * GT + t + 1)
                        for k in range(KD):
                            last = nc.tensor.transpose(psum[:, k, t * P:(t + 1) * P],
                                                       h2[:, t, k * P:(k + 1) * P], ident[:, :])
                    last.then_inc(h2t_mm, 1)
                    pe.wait_ge(h2t_act, it * 2 + 2)
                    pe.wait_ge(h2t_dve, it * 2 + 2)
                    pe.wait_ge(x1_done, it * GT + GT)
                    pe.wait_ge(w3_in, 64)
                    for t in range(GT):
                        for k in range(KD):
                            last = nc.tensor.matmul(psum[:, 4, t * E:(t + 1) * E], h2T[:, k, t * P:(t + 1) * P],
                                                    gw[:, k, :], start=(k == 0), stop=(k == KD - 1))
                    last.then_inc(lg_mm, 1)

                    def gate_up(f):
                        if f >= 2:
                            pe.wait_ge(gu_done, it * SC + f - 1)
                        for half in range(2 if f < SC - 1 else 1):
                            for k in range(KD):
                                last = nc.tensor.matmul(psum[:, (f % 2) * 2 + half, :],
                                                        sgu[:, k * (2 * SC - 1) + 2 * f + half, :], h2T[:, k, :],
                                                        start=(k == 0), stop=(k == KD - 1))
                        last.then_inc(gu_mm, 1)

                    for f in range(2):
                        gate_up(f)
                    pe.wait_ge(pick_ready, it + 1)
                    for t in range(GT):
                        nc.tensor.matmul(psum[:, 5, t * E:(t + 1) * E], before_bf[:, :], picked[:, t, :],
                                         start=True, stop=False)
                        for u in range(t):
                            nc.tensor.matmul(psum[:, 5, t * E:(t + 1) * E], ones_bf[:, :], picked[:, u, :],
                                             start=False, stop=False)
                        last = nc.tensor.matmul(psum[:, 5, t * E:(t + 1) * E], ones_bf[:, :], carry_bf[:, :],
                                                start=False, stop=True)
                    last.then_inc(pos_mm, 1)
                    for f in range(2, SC):
                        gate_up(f)
                    pe.wait_ge(gu_done, it * SC + SC)
                    for t in range(GT):
                        if t >= 2:
                            pe.wait_ge(sd_done, START + it * GT + t - 1)
                        for f in range(SC):
                            rows = P if f < SC - 1 else SR
                            last = nc.tensor.matmul(psum[:, 6 + t % 2, :], guS[0:rows, f, t * P:(t + 1) * P],
                                                    sd[0:rows, f, :], start=(f == 0), stop=(f == SC - 1))
                        last.then_inc(sd_mm, 1)

            @block.scalar
            def _(act):
                act.wait_ge(bg_ready, 1)
                with act.Fori(0, B) as b:
                    with act.Fori(0, HB) as m:
                        it = b * HB + m
                        act.wait_ge(h2_out, DSTART + it * 16)
                        for j in (0, 2):
                            act.wait_ge(y_mm, it * KD + j + 1)
                            nc.scalar.activation(yT[:, j, :], psum[:, j, :], ACT.Identity,
                                                 bias=boga[:, j, bass.ds(b, 1)],
                                                 scale=modT[:, GA, j, bass.ds(b, 1)]).then_inc(y_act, 1)
                        act.wait_ge(l2_var, it + 1)
                        nc.scalar.activation(std3, var3, ACT.Sqrt).then_inc(l2_std, 1)
                        act.wait_ge(h2t_mm, it + 1)
                        for k in (0, 2):
                            nc.scalar.copy(h2T[:, k, :], psum[:, k, :]).then_inc(h2t_act, 1)
                        act.wait_ge(r_sub, it + 1)
                        nc.scalar.activation(lexp, lsub, ACT.Exp).then_inc(r_exp, 1)
                        for f in range(SC):
                            act.wait_ge(gu_mm, it * SC + f + 1)
                            if f >= 2:
                                act.wait_ge(gu_done, it * SC + f - 1)
                            rows = P if f < SC - 1 else SR
                            nc.scalar.activation(silu[0:rows, f % 2, :], psum[0:rows, (f % 2) * 2, :], ACT.Silu)\
                                .then_inc(gu_silu, 1)

            @block.vector
            def _(dve):
                dve.sem_inc(sd_done, START)
                for b in range(B):
                    i_ = nc.vector.tensor_tensor(boga[:, :, b], boT[:, :], modT[:, GA, :, b], ALU.mult)
                nc.vector.memset(carry[:, :], 0.0)
                nc.vector.memset(carry_bf[:, :], 0.0).then_inc(bg_ready, 1)
                dve.wait_ge(bg_ready, 1)
                dve.wait_ge(x3_in, 32)
                with dve.Fori(0, B) as b:
                    with dve.Fori(0, HB) as m:
                        it = b * HB + m
                        dve.wait_ge(h2_out, DSTART + it * 16)
                        for j in (1, 3):
                            dve.wait_ge(y_mm, it * KD + j + 1)
                            nc.vector.tensor_scalar(yT[:, j, :], psum[:, j, :], modT[:, GA, j, bass.ds(b, 1)],
                                                    boga[:, j, bass.ds(b, 1)], ALU.mult, ALU.add).then_inc(y_dve, 1)
                        N2 = 3 * GT + 1
                        for t in range(GT):
                            xt = xs[:, bass.ds(it * GT + t, 1), :].rearrange("p a d -> p (a d)")
                            dve.wait_ge(yt_mm, it * GT + t + 1)
                            nc.vector.tensor_tensor(xt, xt, psum[:, 4 + t, :], ALU.add).then_inc(x1_done, 1)
                            wait_alone(dve, x1_done, it * GT + t + 1)
                            nc.vector.bn_stats(stats3[:, t, :], xt).then_inc(l2_v, 1)
                        wait_alone(dve, l2_v, it * N2 + GT)
                        for t in range(GT):
                            nc.vector.bn_aggr(mv3[:, t, :], stats3[:, t, :]).then_inc(l2_v, 1)
                        dve.wait_ge(l2_v, it * N2 + 2 * GT)
                        nc.vector.tensor_scalar(var3, mv3[:, :, 1], EPS, None, ALU.add).then_inc(l2_var, 1)
                        dve.wait_ge(l2_std, it + 1)
                        nc.vector.reciprocal(rstd3, std3).then_inc(l2_v, 1)
                        dve.wait_ge(l2_v, it * N2 + 2 * GT + 1)
                        for t in range(GT):
                            xt = xs[:, bass.ds(it * GT + t, 1), :].rearrange("p a d -> p (a d)")
                            r1 = rowsB[:, 0, bass.ds(b, 1), :].rearrange("p a d -> p (a d)")
                            r2 = rowsB[:, 1, bass.ds(b, 1), :].rearrange("p a d -> p (a d)")
                            nc.vector.scalar_tensor_tensor(out=x_mod[:, t % 2, :], in0=xt, scalar=mv3[:, t, 0:1], in1=r1,
                                                           op0=ALU.subtract, op1=ALU.mult).then_inc(l2_v, 1)
                            dve.wait_ge(l2_v, it * N2 + 2 * GT + 2 + t)
                            nc.vector.scalar_tensor_tensor(out=h2[:, t, :], in0=x_mod[:, t % 2, :],
                                                           scalar=rstd3[:, t:t + 1], in1=r2,
                                                           op0=ALU.mult, op1=ALU.add).then_inc(h2_ready, 1)
                        dve.wait_ge(h2t_mm, it + 1)
                        for k in (1, 3):
                            nc.vector.tensor_copy(h2T[:, k, :], psum[:, k, :]).then_inc(h2t_dve, 1)
                        NR = 22
                        step = [0]

                        def then(ins):
                            step[0] += 1
                            ins.then_inc(r_v, 1)
                            wait_alone(dve, r_v, it * NR + step[0])

                        lg = psum[:, 4, 0:GT * E].rearrange("p (t e) -> p t e", e=E)
                        dve.wait_ge(lg_mm, it + 1)
                        then(nc.vector.tensor_reduce(lmax, lg, AX_X, ALU.max))
                        nc.vector.tensor_tensor(lsub, lg,
                                                lmax.rearrange("p (t o) -> p t o", o=1).broadcast_to([P, GT, E]),
                                                ALU.subtract).then_inc(r_sub, 1)
                        dve.wait_ge(r_exp, it + 1)
                        then(nc.vector.tensor_reduce(lsum, lexp, AX_X, ALU.add))
                        then(nc.vector.reciprocal(lrec, lsum))
                        then(nc.vector.tensor_tensor(lexp, lexp,
                                                     lrec.rearrange("p (t o) -> p t o", o=1).broadcast_to([P, GT, E]),
                                                     ALU.mult))
                        wait_alone(dve, scattered, DSTART + it * GT * TOPK * 16)
                        for t in range(GT):
                            i_ = nc.vector.max(top[:, t, :], lexp[:, t, :])
                        then(i_)
                        for t in range(GT):
                            i_ = nc.vector.max_index(top_i[:, t, :], top[:, t, :], lexp[:, t, :])
                        then(i_)
                        then(nc.vector.tensor_copy(top_f, top_i[:, :, :]))
                        for t in range(GT):
                            i_ = nc.vector.tensor_tensor(
                                hot[:, t], iota_e[:, :].rearrange("p (o e) -> p o e", o=1).broadcast_to([P, TOPK, E]),
                                top_f[:, t, 0:TOPK].rearrange("p (k o) -> p k o", o=1).broadcast_to([P, TOPK, E]),
                                ALU.is_equal)
                        then(i_)
                        with nc.allow_low_precision(reason="zeros and ones, exact in bfloat16"):
                            for t in range(GT):
                                i_ = nc.vector.tensor_reduce(picked[:, t, :], hot[:, t].rearrange("p k e -> p e k"),
                                                             AX_X, ALU.add)
                        i_.then_inc(pick_ready, 1)
                        dve.wait_ge(pick_ready, it + 1)
                        then(nc.vector.tensor_reduce(gsum[:, :], picked[:, :, :].rearrange("p t e -> p e t"), AX_X,
                                                     ALU.add))
                        then(nc.vector.tensor_tensor(carry[:, :], carry[:, :], gsum[:, :], ALU.add))
                        dve.wait_ge(pos_mm, it + 1)
                        then(nc.vector.tensor_copy(carry_bf[:, :], carry[:, :]))
                        for t in range(GT):
                            i_ = nc.vector.tensor_tensor(
                                hot_pos[:, t], hot[:, t],
                                psum[:, 5, t * E:(t + 1) * E].rearrange("p (o e) -> p o e", o=1)
                                .broadcast_to([P, TOPK, E]), ALU.mult)
                        then(i_)
                        for t in range(GT):
                            i_ = nc.vector.tensor_reduce(pos_k[:, t, :], hot_pos[:, t], AX_X, ALU.add)
                        then(i_)
                        then(nc.vector.tensor_scalar(over[:, :, :], pos_k[:, :, :], float(CAP), DROPPED, ALU.is_ge,
                                                     ALU.mult))
                        then(nc.vector.scalar_tensor_tensor(out=dest[:, :, :], in0=pos_k[:, :, :], scalar=float(E),
                                                            in1=top_f[:, :, 0:TOPK], op0=ALU.mult, op1=ALU.add))
                        then(nc.vector.tensor_tensor(dest[:, :, :], dest[:, :, :], over[:, :, :], ALU.add))
                        then(nc.vector.tensor_copy(dest_u[:, :, :], dest[:, :, :]))
                        then(nc.vector.tensor_copy(entry[:, :, :, 1], top[:, :, 0:TOPK]))
                        then(nc.vector.tensor_copy(
                            entry[:, :, :, 0],
                            tok_id[:, :].rearrange("p (t o) -> p t o", o=1).broadcast_to([P, GT, TOPK])))
                        nc.vector.tensor_scalar(tok_id[:, :], tok_id[:, :], float(GN), None, ALU.add)\
                            .then_inc(dest_ready, 1)
                        assert step[0] <= NR
                        for _ in range(NR - step[0]):
                            dve.sem_inc(r_v, 1)
                        for f in range(SC):
                            dve.wait_ge(gu_silu, it * SC + f + 1)
                            rows = P if f < SC - 1 else SR
                            up = psum[:, (f % 2) * 2 + 1, :] if f < SC - 1 else psum[SR:SR + SR, (f % 2) * 2, :]
                            nc.vector.tensor_tensor(guS[0:rows, f, :], silu[0:rows, f % 2, :], up, ALU.mult)\
                                .then_inc(gu_done, 1)
                        for t in range(GT):
                            xt = xs[:, bass.ds(it * GT + t, 1), :].rearrange("p a d -> p (a d)")
                            r3 = rowsB[:, 2, bass.ds(b, 1), :].rearrange("p a d -> p (a d)")
                            dve.wait_ge(sd_mm, it * GT + t + 1)
                            nc.vector.tensor_tensor(x_mod[:, t % 2, :], psum[:, 6 + t % 2, :], r3, ALU.mult)\
                                .then_inc(sd_tmp, 1)
                            dve.wait_ge(sd_tmp, it * GT + t + 1)
                            nc.vector.tensor_tensor(xt, xt, x_mod[:, t % 2, :], ALU.add).then_inc(sd_done, 1)

        used[0] = 0
        NW = KD * 2 * F
        WORDS = NW + FC * D
        whole = [hT[:, :, :].rearrange("p k t -> p (k t)"), oT[:, :, :].rearrange("p k t -> p (k t)")]
        wbuf = [whole[0][:, 0:WORDS], whole[1][:, 0:WORDS], carve([P, WORDS]), carve([P, WORDS])]
        wgu_s = [w[:, 0:NW].rearrange("p (k f) -> p k f", k=KD) for w in wbuf]
        wd_s = [w[:, NW:WORDS].rearrange("p (k d) -> p k d", k=FC) for w in wbuf]
        rest = [whole[0][:, WORDS:KD * T], whole[1][:, WORDS:KD * T]]
        xe = [carve([P, D]) for _ in range(UNROLL)]
        dsc = [carve([P, D]) for _ in range(UNROLL)]
        xeT = [rest[0][:, 0:D].rearrange("p (k c) -> p k c", k=KD),
               rest[0][:, D:2 * D].rearrange("p (k c) -> p k c", k=KD)]
        sil = [rest[0][:, 2 * D:2 * D + F], rest[0][:, 2 * D + F:2 * D + 2 * F]]
        gu = [rest[1][:, 0:F], rest[1][:, F:2 * F]]
        guT = [rest[1][:, 2 * F:2 * F + FC * P].rearrange("p (k c) -> p k c", k=FC),
               rest[1][:, 2 * F + FC * P:2 * F + 2 * FC * P].rearrange("p (k c) -> p k c", k=FC)]
        slots = carve([P, E, 2])
        slot_tok = sb("slot_tok", [P, E], U32)
        get_idx = [sb(f"get_idx{u}", [P, 1], U32) for u in range(UNROLL)]
        add_idx = [sb(f"add_idx{u}", [P, 1], U32) for u in range(UNROLL)]

        slots_in = sem("slots_in")
        tok_ready = sem("tok_ready")
        w_in = [sem(f"w_in{u}") for u in range(UNROLL)]
        get_ready = sem("get_ready")
        add_ready = sem("add_ready")
        xe_in = [sem(f"xe_in{u}") for u in range(UNROLL)]
        xt_mm = sem("xt_mm")
        xt_out = sem("xt_out")
        g_mm = sem("g_mm")
        u_mm = sem("u_mm")
        silu_done = sem("silu_done")
        gu_out = sem("gu_out")
        gt_mm = sem("gt_mm")
        gt_out = sem("gt_out")
        d_mm = sem("d_mm")
        d_out = sem("d_out")

        def wait_for(eng, what, value):
            if not isinstance(value, int) or value > 0:
                eng.wait_ge(what, value)

        def over_experts(eng, step):
            for u in range(UNROLL):
                step(0, u)
            with eng.Fori(1, E // UNROLL - 1) as i:
                for u in range(UNROLL):
                    step(i, u)
            for u in range(UNROLL):
                step(E // UNROLL - 1, u)

        def exists(e):
            return not isinstance(e, int) or 0 <= e < E

        with nc.Block() as block:
            @block.sync
            def _(sp):
                sp.dma_start(slots, slot_dram.rearrange("(p e) w -> p e w", e=E)).then_inc(slots_in, 16)

                def step(i, u):
                    e = i * UNROLL + u
                    wait_for(sp, d_mm, e - UNROLL + 1)
                    rows = wgu[e] if isinstance(e, int) else wgu[bass.ds(e, 1)].rearrange("a p c -> p (a c)")
                    sp.dma_start(wgu_s[u], rows.rearrange("p (k f) -> p k f", k=KD)).then_inc(w_in[u], 16)
                    sp.dma_start(wd_s[u][:, 0:FC - 1, :],
                                 wd[e, 0:(FC - 1) * P, :].rearrange("(k p) d -> p k d", p=P)).then_inc(w_in[u], 16)
                    sp.dma_start(wd_s[u][0:FR, FC - 1, :], wd[e, (FC - 1) * P:F, :]).then_inc(w_in[u], 16)

                over_experts(sp, step)

            @block.gpsimd
            def _(pool):
                def gather(e, i, u):
                    if not exists(e):
                        return
                    if not isinstance(i, int) or i > 0:
                        wait_alone(pool, xe_in[u], i * 16)
                    nc.gpsimd.tensor_copy(get_idx[u][:, :], slot_tok[:, bass.ds(e, 1)]).then_inc(get_ready, 1)
                    pool.wait_ge(get_ready, e + 1)
                    if not isinstance(i, int) or i > 0:
                        wait_alone(pool, xt_mm, e - UNROLL + 1)
                    pool.indirect_dma_start(
                        out=xe[u], out_offset=None, in_=h2_dram,
                        in_offset=bass.IndirectOffsetOnAxis(ap=get_idx[u][:, 0:1], axis=0),
                        bounds_check=TD - 1, oob_is_err=True).then_inc(xe_in[u], 16)

                def step(i, u):
                    e = i * UNROLL + u
                    nc.gpsimd.tensor_copy(add_idx[u][:, :], slot_tok[:, bass.ds(e, 1)]).then_inc(add_ready, 1)
                    pool.wait_ge(add_ready, e + 1)
                    wait_alone(pool, d_out, e + 1)
                    wait_alone(pool, added, DSTART + e * 16)
                    pool.indirect_dma_start(
                        out=y_dram, out_offset=bass.IndirectOffsetOnAxis(ap=add_idx[u][:, 0:1], axis=0),
                        in_=dsc[u], in_offset=None, compute_op=ALU.add,
                        bounds_check=TD - 1, oob_is_err=True).then_inc(added, 16)
                    gather(e + UNROLL, i + 1, u)

                pool.wait_ge(tok_ready, 1)
                for u in range(UNROLL):
                    gather(u, 0, u)
                over_experts(pool, step)
                pool.wait_ge(added, DSTART + E * 16)

            @block.tensor
            def _(pe):
                def turn_rows(e, i, u):
                    if not exists(e):
                        return
                    pe.wait_ge(xe_in[u], i * 16 + 16)
                    wait_for(pe, xt_out, e)
                    for k in range(KD):
                        last = nc.tensor.transpose(psum[:, 0, k * P:(k + 1) * P], xe[u][:, k * P:(k + 1) * P],
                                                   ident[:, :])
                    last.then_inc(xt_mm, 1)

                def half(e, u, up):
                    for k in range(KD):
                        last = nc.tensor.matmul(psum[:, 2 + up, 0:F], xeT[u % 2][:, k, :],
                                                wgu_s[u][:, k, up * F:(up + 1) * F],
                                                start=(k == 0), stop=(k == KD - 1))
                    last.then_inc(u_mm if up else g_mm, 1)

                def turn_hidden(e, u):
                    if not exists(e):
                        return
                    pe.wait_ge(gu_out, e + 1)
                    wait_for(pe, gt_out, e)
                    for k in range(FC):
                        w = P if k < FC - 1 else FR
                        last = nc.tensor.transpose(psum[0:w, 1, k * P:(k + 1) * P], gu[u % 2][:, k * P:k * P + w],
                                                   ident[:, :])
                    last.then_inc(gt_mm, 1)

                def down(e, u):
                    if not exists(e):
                        return
                    pe.wait_ge(gt_out, e + 1)
                    wait_for(pe, d_out, e - 1)
                    for k in range(FC):
                        w = P if k < FC - 1 else FR
                        last = nc.tensor.matmul(psum[:, 4 + u % 2, :], guT[u % 2][0:w, k, :], wd_s[u][0:w, k, :],
                                                start=(k == 0), stop=(k == FC - 1))
                    last.then_inc(d_mm, 1)

                def step(i, u):
                    e = i * UNROLL + u
                    pe.wait_ge(w_in[u], i * 48 + 48)
                    pe.wait_ge(xt_out, e + 1)
                    wait_for(pe, silu_done, e)
                    half(e, u, 0)
                    turn_hidden(e - 1, (u - 1) % UNROLL)
                    turn_rows(e + 1, i + (u + 1) // UNROLL, (u + 1) % UNROLL)
                    wait_for(pe, gu_out, e)
                    half(e, u, 1)
                    down(e - 1, (u - 1) % UNROLL)

                turn_rows(0, 0, 0)
                over_experts(pe, step)
                turn_hidden(E - 1, (E - 1) % UNROLL)
                down(E - 1, (E - 1) % UNROLL)

            @block.scalar
            def _(act):
                def weigh(e, u):
                    if not exists(e):
                        return
                    act.wait_ge(d_mm, e + 1)
                    wait_for(act, added, DSTART + (e - UNROLL + 1) * 16 if not isinstance(e, int) or e >= UNROLL
                             else 0)
                    nc.scalar.activation(dsc[u], psum[:, 4 + u % 2, :], ACT.Copy, scale=slots[:, bass.ds(e, 1), 1])\
                        .then_inc(d_out, 1)

                def step(i, u):
                    e = i * UNROLL + u
                    act.wait_ge(g_mm, e + 1)
                    wait_for(act, gu_out, e - 1)
                    nc.scalar.activation(sil[u % 2], psum[:, 2, 0:F], ACT.Silu).then_inc(silu_done, 1)
                    weigh(e - 1, (u - 1) % UNROLL)

                act.wait_ge(tok_ready, 1)
                over_experts(act, step)
                weigh(E - 1, (E - 1) % UNROLL)

            @block.vector
            def _(dve):
                def keep_rows(e, u):
                    if not exists(e):
                        return
                    dve.wait_ge(xt_mm, e + 1)
                    wait_for(dve, u_mm, e - 1)
                    nc.vector.tensor_copy(xeT[u % 2].rearrange("p k c -> p (k c)"), psum[:, 0, :]).then_inc(xt_out, 1)

                def keep_hidden(e, u):
                    if not exists(e):
                        return
                    dve.wait_ge(gt_mm, e + 1)
                    wait_for(dve, d_mm, e - 1)
                    nc.vector.tensor_copy(guT[u % 2][:, 0:FC - 1, :],
                                          psum[:, 1, 0:(FC - 1) * P].rearrange("p (k c) -> p k c", c=P))
                    nc.vector.tensor_copy(guT[u % 2][0:FR, FC - 1, :], psum[0:FR, 1, (FC - 1) * P:FC * P])\
                        .then_inc(gt_out, 1)

                def step(i, u):
                    e = i * UNROLL + u
                    keep_hidden(e - 1, (u - 1) % UNROLL)
                    keep_rows(e + 1, (u + 1) % UNROLL)
                    dve.wait_ge(silu_done, e + 1)
                    dve.wait_ge(u_mm, e + 1)
                    wait_for(dve, gt_mm, e - 1)
                    nc.vector.tensor_tensor(gu[u % 2], sil[u % 2], psum[:, 3, 0:F], ALU.mult).then_inc(gu_out, 1)

                dve.wait_ge(slots_in, 16)
                nc.vector.tensor_copy(slot_tok[:, :], slots[:, :, 0]).then_inc(tok_ready, 1)
                keep_rows(0, 0)
                over_experts(dve, step)
                keep_hidden(E - 1, (E - 1) % UNROLL)

        used[0] = 0
        yt = [carve([P, GT, D]) for _ in range(2)]
        y_in = [sem("y_in0"), sem("y_in1")]
        f_tmp = sem("f_tmp")
        f_done = sem("f_done")
        stored = sem("stored")
        with nc.Block() as block:
            @block.sync
            def _(sp):
                for n in range(NGRP):
                    if n >= 2:
                        sp.wait_ge(f_done, n - 1)
                    sp.dma_start(yt[n % 2], y_rows[:, n * GT:(n + 1) * GT, :]).then_inc(y_in[n % 2], 16)

            @block.scalar
            def _(act):
                for n in range(NGRP):
                    act.wait_ge(f_done, n + 1)
                    act.dma_start(out_rows[:, n * GT:(n + 1) * GT, :], xs[:, n * GT:(n + 1) * GT, :])\
                        .then_inc(stored, 16)
                act.wait_ge(stored, 16 * NGRP)

            @block.vector
            def _(dve):
                for n in range(NGRP):
                    dve.wait_ge(y_in[n % 2], 16 * (n // 2 + 1))
                    for t in range(GT):
                        i_ = nc.vector.tensor_tensor(yt[n % 2][:, t, :], yt[n % 2][:, t, :],
                                                     rowsB[:, 2, n // HB, :], ALU.mult)
                    i_.then_inc(f_tmp, 1)
                    dve.wait_ge(f_tmp, n + 1)
                    nc.vector.tensor_tensor(xs[:, n * GT:(n + 1) * GT, :], xs[:, n * GT:(n + 1) * GT, :], yt[n % 2],
                                            ALU.add).then_inc(f_done, 1)


def lay_out(a):
    import numpy as np

    def per_partition(v):
        return np.ascontiguousarray(np.moveaxis(v.reshape(*v.shape[:-1], -1, P), -1, 0))

    E_ = {}
    E_["x"] = a["L0_attn_x"].reshape(T, D)
    w = a["L0_attn_w_qkv"].reshape(3, NG, P, KD, P)
    E_["wqkv"] = w.transpose(1, 4, 3, 0, 2).reshape(NG, P, KD * 3 * P)
    E_["bqkv"] = a["L0_attn_b_qkv"].reshape(3, NG, P).transpose(2, 0, 1)
    E_["wo"] = a["L0_attn_w_out"].reshape(D, KD, P).transpose(2, 1, 0)
    E_["bo"] = per_partition(a["L0_attn_b_out"])
    E_["gatew"] = a["L0_ffn_gate_w"].reshape(E, KD, P).transpose(2, 1, 0)
    g = a["L0_ffn_w_gate"].reshape(E, KD, P, F)
    u = a["L0_ffn_w_up"].reshape(E, KD, P, F)
    E_["wgu"] = np.concatenate([g, u], axis=3).transpose(0, 2, 1, 3).reshape(E, P, KD * 2 * F)
    E_["wd"] = a["L0_ffn_w_down"]
    cols = []
    for f in range(SC):
        r = slice(f * P, min(FS, (f + 1) * P))
        cols += [a["L0_ffn_sh_gate"][r], a["L0_ffn_sh_up"][r]]
    s = np.concatenate(cols, axis=0)
    E_["shgu"] = s.reshape(2 * FS, KD, P).transpose(2, 1, 0).reshape(P, KD * 2 * FS)
    E_["shd"] = a["L0_ffn_sh_down"].T
    E_["c"] = a["L0_c"].reshape(B, KD, P).transpose(2, 1, 0)
    E_["wmod"] = a["L0_wmod"].reshape(KD, P, 6, D).transpose(2, 1, 0, 3)
    return {k: np.ascontiguousarray(v) for k, v in E_.items()}


def kernel(**inputs):
    import numpy as _np
    import concourse.bacc as _bacc
    from concourse.bass_utils import run_bass_kernel_spmd as _run

    arrays = lay_out({k: _np.asarray(v) for k, v in inputs.items()})
    nc = _bacc.Bacc("TRN2", target_bir_lowering=False, num_devices=1)
    args = {k: nc.dram_tensor(k, v.shape, mybir.dt.from_np(v.dtype), kind="ExternalInput").ap()
            for k, v in arrays.items()}
    o = nc.dram_tensor("out", [T, D], F32, kind="ExternalOutput").ap()
    build(nc, out=o, **args)
    r = _run(nc, [arrays], core_ids=[0])
    return r.results[0]["out"].reshape(B, S, D)
```

```python
from contextlib import ExitStack

import concourse.bass as bass
from concourse import mybir

P = 128
F32 = mybir.dt.float32
F32R = mybir.dt.float32r
BF16 = mybir.dt.bfloat16
U32 = mybir.dt.uint32
ACT = mybir.ActivationFunctionType
ALU = mybir.AluOpType
AX_X = mybir.AxisListType.X

B, S, D = 2, 1024, 512
T = B * S
KD = D // P
NT = T // P
TB = S // P
H, HD = 16, 32
HG = P // HD
NG = H // HG
GT = 4
GN = GT * P
NGRP = T // GN
HB = S // GN
E, F, TOPK, CAP = 64, 352, 6, 128
FC = -(-F // P)
FR = F - (FC - 1) * P
FS = 2 * F
SC = -(-FS // P)
SR = FS - (SC - 1) * P
TD = T + P
EPS = 1e-5
SCALE = float(HD) ** -0.5
MASKED = 1e30
DROPPED = float(1 << 20)
SA, CA, GA, SB, CB, GB = range(6)
START, DSTART = 1, 16
UNROLL = 4


class Arena:

    def __init__(self, tensor, words):
        self.tensor, self.words, self.used = tensor, words, 0

    def carve(self, shape, dt=F32):
        words = 1
        for n in shape[1:]:
            words *= n
        if dt is BF16:
            words = (words + 1) // 2
        v = self.tensor[0:shape[0], self.used:self.used + words]
        self.used += words
        assert self.used <= self.words, (self.used, self.words)
        if dt is not F32:
            v = v.bitcast(dt)
        if len(shape) == 3:
            v = v.rearrange("p (a b) -> p a b", b=shape[2])
        elif len(shape) == 4:
            v = v.rearrange("p (a b c) -> p a b c", b=shape[2], c=shape[3])
        return v


def build(nc, x, wqkv, bqkv, wo, bo, gatew, wgu, wd, shgu, shd, c, wmod, out):
    x_rows = x.rearrange("(t p) d -> p t d", p=P)
    out_rows = out.rearrange("(t p) d -> p t d", p=P)
    h2_dram = nc.dram_tensor("h2_dram", [TD, D], F32, kind="Internal").ap()
    oT_dram = nc.dram_tensor("oT_dram", [D, T], F32, kind="Internal").ap()
    slot_dram = nc.dram_tensor("slot_dram", [CAP * E, 2], F32, kind="Internal").ap()
    h2_rows = h2_dram.rearrange("(t p) d -> p t d", p=P)
    oT_cols = oT_dram.rearrange("(k p) t -> p k t", p=P)

    with ExitStack() as ctx:
        def sb(name, shape, dt=F32, scope=ctx):
            return scope.enter_context(nc.sbuf_tensor(name, shape, dt))

        def sem(name):
            return ctx.enter_context(nc.semaphore(name))

        def wait_alone(eng, what, value):
            eng.wait_ge(what, value)
            eng.nop(nofuse=True)

        psum = ctx.enter_context(nc.psum_tensor("psum", [P, 8, 512], F32))

        ident = sb("ident", [P, P])
        ident_bf = sb("ident_bf", [P, P], BF16)
        mask_bf = sb("mask_bf", [P, P], BF16)
        before_bf = sb("before_bf", [P, P], BF16)
        ones_bf = sb("ones_bf", [P, P], BF16)
        zeros = sb("zeros", [P, D])
        empty = sb("empty", [P, E, 2])
        modT = sb("modT", [P, 3, KD, B])
        rowsB = sb("rowsB", [P, 3, B, D])
        bq = sb("bq", [P, 3, NG])
        boT = sb("boT", [P, KD])
        iota_e = sb("iota_e", [P, E])
        tok_id = sb("tok_id", [P, GT])

        wg_scope = ctx.enter_context(ExitStack())
        wg = sb("wg", [P, KD * 3, P], scope=wg_scope)
        attention_scope = ctx.enter_context(ExitStack())
        hT = sb("hT", [P, KD, T], scope=attention_scope)

        scope = ExitStack()
        xs = sb("xs1", [P, NT, D], scope=scope)
        words1 = 24 * 1024
        carve = Arena(sb("arena1", [P, words1], scope=scope), words1).carve
        cT = carve([P, KD, B])
        cs = carve([P, KD, B])
        HALF = P // B
        cs_wide = carve([P, KD, P])
        WM_BUFS = 4
        wm = [carve([P, KD, D]) for _ in range(WM_BUFS)]
        mod_row = carve([P, 6, D])
        size = carve([P, D])
        twice_pos = carve([P, D])
        xn = carve([P, NT, D])
        stats = carve([P, NT, 6])
        mv = carve([P, NT, 2])
        var = carve([P, NT])
        std = carve([P, NT])
        rstd = carve([P, NT])

        c_in = sem("c_in")
        small_in = sem("small_in")
        x_in = [sem(f"x_in{n}") for n in range(B)]
        wm_in = [sem(f"wm_in{n}") for n in range(WM_BUFS)]
        const_v = sem("const_v")
        const_g = sem("const_g")
        c_silu = sem("c_silu")
        wide_ready = sem("wide_ready")
        mod_mm = sem("mod_mm")
        mod_out = sem("mod_out")
        mod_fix = sem("mod_fix")
        modT_mm = sem("modT_mm")
        modT_out = sem("modT_out")
        rows_out = sem("rows_out")
        ln_v = sem("ln_v")
        ln_var = sem("ln_var")
        ln_std = sem("ln_std")
        xn_ready = sem("xn_ready")
        h_mm = sem("h_mm")
        h_out = sem("h_out")
        init_out = sem("init_out")
        wg_in = sem("wg_in")
        scattered = sem("scattered")
        MODS = (SA, CA, GA, CB, SB, GB)
        COLS = (SA, CA, GA)
        ROWS = (CB, SB, GB)
        FIXES = {}
        for m in MODS:
            FIXES[m] = max(FIXES.values(), default=0) + {CA: 1, CB: 1, GA: 4, GB: 4}.get(m, 0)
        H_BANKS = 5
        V_BANKS = (5, 6)

        with nc.Block() as block:
            @block.sync
            def _(sp):
                sp.dma_start(cT, c).then_inc(c_in, 16)

                def load_mod(n):
                    if n >= WM_BUFS:
                        sp.wait_ge(mod_mm, n - WM_BUFS + 1)
                    sp.dma_start(wm[n % WM_BUFS], wmod[MODS[n]]).then_inc(wm_in[n % WM_BUFS], 16)

                for b in range(B):
                    sp.dma_start(xs[:, b * TB:(b + 1) * TB, :], x_rows[:, b * TB:(b + 1) * TB, :])\
                        .then_inc(x_in[b], 16)
                    load_mod(2 * b)
                    load_mod(2 * b + 1)
                sp.dma_start(bq[:, :, :], bqkv).then_inc(small_in, 16)
                sp.dma_start(boT[:, :], bo).then_inc(small_in, 16)
                load_mod(4)
                load_mod(5)
                sp.dma_start(wg[:, :, :], wqkv[0].rearrange("p (a c) -> p a c", c=P)).then_inc(wg_in, 16)
                n_rows = 0
                for r, m in enumerate(ROWS):
                    sp.wait_ge(mod_out, MODS.index(m) + 1)
                    sp.wait_ge(mod_fix, FIXES[m])
                    for b in range(B):
                        for part in range(B):
                            sp.dma_start(rowsB[part * HALF:(part + 1) * HALF, r, b, :],
                                         mod_row[b * HALF:(b + 1) * HALF, m, :]).then_inc(rows_out, 16)
                            n_rows += 1
                sp.wait_ge(small_in, 32)
                sp.wait_ge(rows_out, 16 * n_rows)

            @block.gpsimd
            def _(pool):
                nc.gpsimd.iota(iota_e[:, :], [[1, E]], base=0, channel_multiplier=0,
                               allow_small_or_imprecise_dtypes=True).then_inc(const_g, 1)
                nc.gpsimd.iota(tok_id[:, :], [[P, GT]], base=0, channel_multiplier=1,
                               allow_small_or_imprecise_dtypes=True).then_inc(const_g, 1)
                nc.gpsimd.iota(empty[:, :, 0], [[0, E]], base=T, channel_multiplier=1,
                               allow_small_or_imprecise_dtypes=True).then_inc(const_g, 1)
                pool.wait_ge(const_v, 5)
                nc.gpsimd.affine_select(out=ident[:, :], in_=ident[:, :], compare_op=ALU.not_equal, fill=1.0,
                                        base=0, pattern=[[-1, P]], channel_multiplier=1).then_inc(const_g, 1)
                nc.gpsimd.affine_select(out=ident_bf[:, :], in_=ident_bf[:, :], compare_op=ALU.not_equal,
                                        fill=1.0, base=0, pattern=[[-1, P]], channel_multiplier=1)\
                    .then_inc(const_g, 1)
                nc.gpsimd.affine_select(out=mask_bf[:, :], in_=mask_bf[:, :], compare_op=ALU.is_ge, fill=MASKED,
                                        base=0, pattern=[[-1, P]], channel_multiplier=1).then_inc(const_g, 1)
                nc.gpsimd.affine_select(out=before_bf[:, :], in_=ones_bf[:, :], compare_op=ALU.is_gt, fill=0.0,
                                        base=0, pattern=[[1, P]], channel_multiplier=-1).then_inc(const_g, 1)
                pool.dma_start(h2_rows[:, NT, :], zeros[:, :]).then_inc(scattered, 16)
                pool.wait_ge(scattered, 16)

            @block.tensor
            def _(pe):
                def vector(n):
                    pe.wait_ge(wm_in[n % WM_BUFS], 16 * (n // WM_BUFS + 1))
                    if n >= 2:
                        pe.wait_ge(mod_out, n - 1)
                    for k in range(KD):
                        last = nc.tensor.matmul(psum[:, V_BANKS[n % 2], :], cs_wide[:, k, :], wm[n % WM_BUFS][:, k, :],
                                                start=(k == 0), stop=(k == KD - 1))
                    last.then_inc(mod_mm, 1)

                def turn_vector(n):
                    m = MODS[n]
                    pe.wait_ge(mod_out, n + 1)
                    if FIXES[m]:
                        pe.wait_ge(mod_fix, FIXES[m])
                    if n:
                        pe.wait_ge(modT_out, n)
                    for k in range(KD):
                        last = nc.tensor.transpose(psum[:, 7, k * P:(k + 1) * P], mod_row[:, m, k * P:(k + 1) * P],
                                                   ident[:, :])
                    last.then_inc(modT_mm, 1)

                def turn_x(g):
                    pe.wait_ge(xn_ready, (g + 1) * GT)
                    for k in range(KD):
                        q = g * KD + k
                        if q >= H_BANKS:
                            pe.wait_ge(h_out, q - H_BANKS + 1)
                        for t in range(GT):
                            last = nc.tensor.transpose(psum[:, q % H_BANKS, t * P:(t + 1) * P],
                                                       xn[:, g * GT + t, k * P:(k + 1) * P], ident[:, :])
                        last.then_inc(h_mm, 1)

                pe.wait_ge(wide_ready, 1)
                pe.wait_ge(const_g, 7)
                vector(0)
                vector(1)
                vector(2)
                turn_vector(0)
                turn_vector(1)
                turn_x(0)
                turn_x(1)
                vector(3)
                vector(4)
                turn_x(2)
                turn_x(3)
                turn_vector(2)
                vector(5)

            @block.scalar
            def _(act):
                act.wait_ge(c_in, 16)
                nc.scalar.activation(cs, cT, ACT.Silu).then_inc(c_silu, 1)

                def keep_vector(n):
                    act.wait_ge(mod_mm, n + 1)
                    nc.scalar.copy(mod_row[:, MODS[n], :], psum[:, V_BANKS[n % 2], :]).then_inc(mod_out, 1)

                def deviation(b):
                    act.wait_ge(ln_var, b + 1)
                    nc.scalar.activation(std[:, b * TB:(b + 1) * TB], var[:, b * TB:(b + 1) * TB], ACT.Sqrt)\
                        .then_inc(ln_std, 1)

                def modulate(g):
                    b = g // HB
                    act.wait_ge(modT_out, 2)
                    for k in range(KD):
                        q = g * KD + k
                        act.wait_ge(h_mm, q + 1)
                        nc.scalar.activation(hT[:, k, g * GN:(g + 1) * GN], psum[:, q % H_BANKS, :],
                                             ACT.Identity, bias=modT[:, SA, k, b:b + 1],
                                             scale=modT[:, CA, k, b:b + 1]).then_inc(h_out, 1)

                deviation(0)
                keep_vector(0)
                keep_vector(1)
                keep_vector(2)
                modulate(0)
                modulate(1)
                keep_vector(3)
                deviation(1)
                keep_vector(4)
                modulate(2)
                modulate(3)
                keep_vector(5)

            @block.vector
            def _(dve):
                nc.vector.memset(ident[:, :], 0.0).then_inc(const_v, 1)
                nc.vector.memset(ident_bf[:, :], 0.0).then_inc(const_v, 1)
                nc.vector.memset(mask_bf[:, :], 0.0).then_inc(const_v, 1)
                nc.vector.memset(ones_bf[:, :], 1.0).then_inc(const_v, 1)
                nc.vector.memset(empty[:, :, 1], 0.0)
                nc.vector.memset(zeros[:, :], 0.0).then_inc(const_v, 1)
                dve.wait_ge(c_silu, 1)
                for b in range(B):
                    i_ = nc.vector.tensor_copy(cs_wide[:, :, b * HALF:(b + 1) * HALF],
                                               cs[:, :, b:b + 1].broadcast_to([P, KD, HALF]))
                i_.then_inc(wide_ready, 1)

                def norm(b, done):
                    tiles = range(b * TB, (b + 1) * TB)
                    row = slice(b * TB, (b + 1) * TB)
                    dve.wait_ge(x_in[b], 16)
                    for t in tiles:
                        nc.vector.bn_stats(stats[:, t, :], xs[:, t, :]).then_inc(ln_v, 1)
                    dve.wait_ge(ln_v, done + TB)
                    for t in tiles:
                        nc.vector.bn_aggr(mv[:, t, :], stats[:, t, :]).then_inc(ln_v, 1)
                    dve.wait_ge(ln_v, done + 2 * TB)
                    nc.vector.tensor_scalar(var[:, row], mv[:, row, 1], EPS, None, ALU.add).then_inc(ln_var, 1)
                    dve.wait_ge(ln_std, b + 1)
                    nc.vector.reciprocal(rstd[:, row], std[:, row]).then_inc(ln_v, 1)
                    dve.wait_ge(ln_v, done + 2 * TB + 1)
                    for t in tiles:
                        nc.vector.tensor_scalar(xn[:, t, :], xs[:, t, :], mv[:, t, 0:1], rstd[:, t:t + 1],
                                                ALU.subtract, ALU.mult).then_inc(xn_ready, 1)
                    return done + 2 * TB + 1

                def correct(n):
                    m = MODS[n]
                    row = mod_row[:, m, :]
                    dve.wait_ge(mod_out, n + 1)
                    if m in (CA, CB):
                        nc.vector.tensor_scalar(row, row, 1.0, None, ALU.add).then_inc(mod_fix, 1)
                    elif m in (GA, GB):
                        nc.vector.scalar_tensor_tensor(out=size, in0=row, scalar=-1.0, in1=row,
                                                       op0=ALU.mult, op1=ALU.max).then_inc(mod_fix, 1)
                        dve.wait_ge(mod_fix, FIXES[m] - 3)
                        nc.vector.tensor_scalar(size, size, 0.25, None, ALU.max).then_inc(mod_fix, 1)
                        nc.vector.tensor_scalar(twice_pos, row, 0.0, 2.0, ALU.is_ge, ALU.mult).then_inc(mod_fix, 1)
                        dve.wait_ge(mod_fix, FIXES[m] - 1)
                        nc.vector.scalar_tensor_tensor(out=row, in0=twice_pos, scalar=1.0, in1=size,
                                                       op0=ALU.subtract, op1=ALU.mult).then_inc(mod_fix, 1)

                def keep_turned(n):
                    dve.wait_ge(modT_mm, n + 1)
                    nc.vector.tensor_copy(modT[:, MODS[n], :, :],
                                          psum[:, 7, :].rearrange("p (k b x) -> p k b x", b=B, x=HALF)[:, :, :, 0])\
                        .then_inc(modT_out, 1)

                done = norm(0, 0)
                correct(1)
                keep_turned(0)
                keep_turned(1)
                norm(1, done)
                correct(2)
                keep_turned(2)
                for n in range(3, 6):
                    correct(n)
        scope.close()

        scope = ExitStack()
        qs = [sb(f"qs{b}", [P, HG, S], F32R, scope) for b in range(B)]
        ks = [sb(f"ks{b}", [P, HG, S], F32R, scope) for b in range(B)]
        words2 = 22016
        carve = Arena(sb("arena2", [P, words2], scope=scope), words2).carve
        part_hi = [carve([P, S]) for _ in range(2)]
        part_lo = [carve([P, S]) for _ in range(2)]
        vT = carve([P, S])
        v = [carve([P, TB, P]) for _ in range(B)]
        prob = carve([P, 4, S])
        pT = carve([P, 2, HG, TB * P])
        low = carve([P, 2, HG])
        den = carve([P, 2, HG])
        rden = carve([P, 2, HG])
        rden_T = carve([P, 2, P])
        bqs = carve([P, NG])
        oS = carve([P, B, S])

        bqs_ready = sem("bqs_ready")
        p_ready = sem("p_ready")
        p_free = [sem("p_free_act"), sem("p_free_dve")]
        t_ready = [sem("t_ready_act"), sem("t_ready_dve")]
        t_free = [sem("t_free_act"), sem("t_free_dve")]
        split_first = [sem("rounded_first"), sem("split_first_done")]
        split_next = [sem("rounded"), sem("split_done")]
        parts_in = [sem("parts_in0"), sem("parts_in1")]
        parts_first = [sem("parts_first_sp"), sem("parts_first_pool")]
        SP_HEADS, POOL_HEADS = range(HG // 2 + 1), range(HG // 2 + 1, HG)
        s_ready = sem("s_ready")
        low_ready = sem("low_ready")
        probs = sem("probs")
        pv_done = sem("pv_done")
        rden_ready = sem("rden_ready")
        rb_done = sem("rb_done")
        rb_copied = sem("rb_copied")
        o_done = sem("o_done")
        o_stored = [sem("o_stored0"), sem("o_stored1")]

        BANKS = (4, 5)
        O_BANK = 6
        P_BANK = 7
        units = [(i, h) for i in range(TB) for h in range(HG)]
        NU = len(units)
        uses, of_unit = [], []
        for n, (i, h) in enumerate(units):
            of_unit.append([])
            for j0 in range(0, i + 1, 4):
                of_unit[-1].append(len(uses))
                uses.append((i, h, j0))
        assert len(uses) % 2 == 0
        PER = len(uses) // 2
        PROJ = [("q", 0), ("q", 1), ("k", 0), ("k", 1), ("v", 0), ("v", 1), ("vt", 0), ("vt", 1)]
        NP = len(PROJ)
        SPLITS = 4
        PIECES = {0: (0, 2), 1: (4, 6), 2: (8, 10), 3: (12, 14), 4: (16, 20), 5: (22, 26), 6: (28,), 7: (30,)}
        at_unit = {n: (p, piece) for p, ns in PIECES.items() for piece, n in enumerate(ns)}
        ends = {ns[-1]: p for p, ns in PIECES.items()}
        DMAS = 2 * 16

        def use_no(it, m):
            return it * PER + m // 2

        def p_bank(r, p):
            return O_BANK if isinstance(r, int) and r == 0 and p % 2 else P_BANK

        def emptied(r, p):
            return r * (NP // 2) + p // 2 + 1

        def s_bank(n):
            return psum[:, 2 * (n % 2):2 * (n % 2) + 2, :].rearrange("p a b -> p (a b)")

        def pairs(step):
            def run(eng):
                with eng.Fori(0, NG - 1) as g:
                    for b in range(B):
                        step(g, b, False)
                for b in range(B):
                    step(NG - 1, b, b == B - 1)
            return run

        def successor(g, b):
            return (g, 1) if b == 0 else (g + 1, 0)

        def empty_proj(eng, mine, r, p, g, b):
            if p % 2 != mine:
                return
            eng.wait_ge(p_ready, r * NP + p + 1)
            kind, n = PROJ[p]
            src = psum[:, p_bank(r, p), :]
            half = slice(n * GN, (n + 1) * GN)

            def project(dst, part, scale, bias):
                bias = bias[:, g:g + 1] if isinstance(g, int) else bias[:, bass.ds(g, 1)]
                if mine == 0:
                    return nc.scalar.activation(dst, src, ACT.Identity, bias=bias, scale=scale)
                return nc.vector.tensor_scalar(dst, src, scale, bias, ALU.mult, ALU.add)

            if kind in ("q", "k"):
                part = "qk".index(kind)
                args = (part, (-SCALE, 1.0)[part], (bqs, bq[:, 1, :])[part])
                project(part_lo[part][:, half], *args).then_inc(p_free[mine], 1)
            elif kind == "v":
                project(vT[:, half], 2, 1.0, bq[:, 2, :]).then_inc(p_free[mine], 1)
            else:
                dst = v[b][:, n * 4:n * 4 + 4, :].rearrange("p a b -> p (a b)")
                ins = nc.scalar.copy(dst, src) if mine == 0 else nc.vector.tensor_copy(dst, src)
                ins.then_inc(p_free[mine], 1)

        def empty_unit(eng, mine, it, m):
            i, h, j0 = uses[m]
            if m % 2 != mine:
                return
            eng.wait_ge(t_ready[mine], use_no(it, m) + 1)
            w = (min(i + 1, j0 + 4) - j0) * P
            if i >= 2:
                eng.wait_ge(pv_done, it * TB + i - 1)
            dst = pT[:, i % 2, h, j0 * P:j0 * P + w]
            src = psum[:, BANKS[mine], 0:w]
            ins = nc.scalar.copy(dst, src) if mine == 0 else nc.vector.tensor_copy(dst, src)
            ins.then_inc(t_free[mine], 1)

        def split(eng, vector, done, r, p):
            part, n = "qk".index(PROJ[p][0]), PROJ[p][1]
            half = slice(n * GN, (n + 1) * GN)
            wait_alone(eng, p_free[p % 2], emptied(r, p))
            vector.tensor_copy(part_hi[part][:, half].bitcast(F32R), part_lo[part][:, half]).then_inc(done[0], 1)
            wait_alone(eng, done[0], splits_before(r, p) + 1)
            vector.tensor_tensor(part_lo[part][:, half], part_lo[part][:, half], part_hi[part][:, half],
                                 ALU.subtract).then_inc(done[1], 1)

        def splits_before(r, p):
            return p if isinstance(r, int) and r == 0 else (r - 1) * SPLITS + p

        def lay_parts(eng, done, splits, b, laid, heads=range(HG)):
            for part, buf, which in ((0, qs[b], (0, 0, 1, 1)), (1, ks[b], (0, 1, 0, 1))):
                eng.wait_ge(done, splits + 2 * (part + 1))
                for h in heads:
                    for row, lo in enumerate(which):
                        src = (part_lo if lo else part_hi)[part]
                        eng.dma_start(buf[row * HD:(row + 1) * HD, h, :].bitcast(F32),
                                      src[h * HD:(h + 1) * HD, :]).then_inc(laid, 16)

        with nc.Block() as block:
            @block.sync
            def _(sp):
                def load_w(g):
                    sp.dma_start(wg[:, :, :], wqkv[g].rearrange("p (a c) -> p a c", c=P)).then_inc(wg_in, 16)

                def step(g, b, last):
                    it = g * B + b
                    if not last:
                        lay_parts(sp, split_next[1], it * SPLITS, successor(g, b)[1],
                                  parts_in[successor(g, b)[1]])
                    if b == 0 and not isinstance(g, int):
                        sp.wait_ge(p_ready, (it + 1) * NP + 6)
                        load_w(g + 1)
                    sp.wait_ge(o_done, START + it * TB + TB)
                    sp.dma_start(oT_cols[:, g, b * S:(b + 1) * S] if isinstance(g, int) else
                                 oT_cols[:, bass.ds(g, 1), b * S:(b + 1) * S].rearrange("p a t -> p (a t)"),
                                 oS[:, b, :]).then_inc(o_stored[b], 16)

                for b in range(B):
                    sp.sem_inc(o_stored[b], DSTART)
                lay_parts(sp, split_first[1], 0, 0, parts_first[0], SP_HEADS)
                sp.dma_start(slot_dram.rearrange("(p e) w -> p e w", e=E), empty[:, :, :]).then_inc(init_out, 16)
                pairs(step)(sp)
                for b in range(B):
                    sp.wait_ge(o_stored[b], DSTART + 16 * NG)
                sp.wait_ge(init_out, 16)

            @block.gpsimd
            def _(pool):
                def step(g, b, last):
                    for p in range(SPLITS):
                        if not last:
                            split(pool, nc.gpsimd, split_next, g * B + b + 1, p)

                lay_parts(pool, split_first[1], 0, 0, parts_first[1], POOL_HEADS)
                pairs(step)(pool)

            @block.tensor
            def _(pe):
                def project(r, p, g, b, n_w, piece=None):
                    kind, n = PROJ[p]
                    if piece is None or piece == 0:
                        if p == 0:
                            pe.wait_ge(wg_in, n_w * 16)
                        if isinstance(r, int) and r == 0:
                            if p >= 2:
                                pe.wait_ge(p_free[p % 2], emptied(r, p - 2))
                        elif p == 0:
                            for q in (NP - 2, NP - 1):
                                pe.wait_ge(p_free[q % 2], emptied(r - 1, q))
                        else:
                            pe.wait_ge(p_free[(p - 1) % 2], emptied(r, p - 1))
                    if kind == "vt":
                        pe.wait_ge(p_free[(4 + n) % 2], emptied(r, 4 + n))
                        for j in range(4):
                            last = nc.tensor.transpose(psum[:, p_bank(r, p), j * P:(j + 1) * P],
                                                       vT[:, (n * 4 + j) * P:(n * 4 + j + 1) * P], ident[:, :])
                    else:
                        part = "qkv".index(kind)
                        for k in range(KD) if piece is None else range(piece * KD // 2, (piece + 1) * KD // 2):
                            last = nc.tensor.matmul(psum[:, p_bank(r, p), :], wg[:, k * 3 + part, :],
                                                    hT[:, k, b * S + n * GN:b * S + (n + 1) * GN],
                                                    start=(k == 0), stop=(k == KD - 1))
                        if piece == 0:
                            return
                    last.then_inc(p_ready, 1)

                def scores(it, b, n):
                    i, h = units[n]
                    if n >= 2:
                        pe.wait_ge(probs, it * NU + n - 1)
                    s = s_bank(n)
                    w = (i + 1) * P
                    for a in range(0, w, 512):
                        e = min(w, a + 512)
                        nc.tensor.matmul(s[:, a:e], qs[b][:, h, i * P:(i + 1) * P], ks[b][:, h, a:e],
                                         start=True, stop=(e < w))
                    nc.tensor.matmul(s[:, i * P:w], ident_bf[:, :], mask_bf[:, :], start=False, stop=True)\
                        .then_inc(s_ready, 1)

                def turn(it, n):
                    i, h = units[n]
                    pe.wait_ge(probs, it * NU + n + 1)
                    for m in of_unit[n]:
                        j0 = uses[m][2]
                        pe.wait_ge(t_free[m % 2], START + use_no(it, m))
                        for j in range(j0, min(i + 1, j0 + 4)):
                            last = nc.tensor.transpose(psum[:, BANKS[m % 2], (j - j0) * P:(j - j0 + 1) * P],
                                                       prob[:, n % 4, j * P:(j + 1) * P], ident[:, :])
                        last.then_inc(t_ready[m % 2], 1)

                def values(it, b, i, thirds=range(3)):
                    if 0 in thirds:
                        mu = of_unit[4 * i + 3][-1]
                        for m in (mu - 1, mu):
                            pe.wait_ge(t_free[m % 2], START + use_no(it, m) + 1)
                        pe.wait_ge(o_done, START + it * TB + i)
                    for j in [j for q in thirds for j in range(q * (i + 1) // 3, (q + 1) * (i + 1) // 3)]:
                        for h in range(HG):
                            last = nc.tensor.matmul(psum[h * HD:(h + 1) * HD, O_BANK, 0:P],
                                                    v[b][:, j, h * HD:(h + 1) * HD], pT[:, i % 2, h, j * P:(j + 1) * P],
                                                    start=(j == 0), stop=(j == i))
                    if 2 not in thirds:
                        return
                    last.then_inc(pv_done, 1)
                    pe.wait_ge(rden_ready, START + it * TB + i + 1)
                    for h in range(HG):
                        last = nc.tensor.matmul(psum[h * HD:(h + 1) * HD, O_BANK, P:2 * P],
                                                rden[:, i % 2, h:h + 1].broadcast_to([P, HD]), ident[:, :],
                                                start=True, stop=True)
                    last.then_inc(rb_done, 1)

                def step(g, b, last):
                    it = g * B + b
                    g2, b2 = successor(g, b)
                    for n in range(NU):
                        if n + 2 < NU:
                            scores(it, b, n + 2)
                        turn(it, n)
                        if not last and n in at_unit:
                            p, piece = at_unit[n]
                            project(it + 1, p, g2, b2, g2 + 1, piece)
                        if n >= HG and n % HG:
                            values(it, b, n // HG - 1, [n % HG - 1])
                    if not last:
                        pe.wait_ge(parts_in[b2], (g + 1) * DMAS * 16)
                        scores(it + 1, b2, 0)
                        scores(it + 1, b2, 1)
                    values(it, b, TB - 1)

                for p in range(NP):
                    project(0, p, 0, 0, 1)
                for laid, heads in zip(parts_first, (SP_HEADS, POOL_HEADS)):
                    pe.wait_ge(laid, DMAS // HG * len(heads) * 16)
                scores(0, 0, 0)
                scores(0, 0, 1)
                pairs(step)(pe)

            @block.scalar
            def _(act):
                act.sem_inc(t_free[0], START)
                act.wait_ge(bqs_ready, 1)

                def exps(it, n):
                    i, h = units[n]
                    w = (i + 1) * P
                    act.wait_ge(low_ready, it * NU + n + 1)
                    if h == 0 and not (isinstance(it, int) and i < 2):
                        act.wait_ge(rden_ready, START + it * TB + i - 1)
                    nc.scalar.activation(prob[:, n % 4, 0:w], s_bank(n)[:, 0:w], ACT.Exp,
                                         bias=low[:, i % 2, h:h + 1], scale=-1.0,
                                         accum_out=den[:, i % 2, h:h + 1]).then_inc(probs, 1)

                def step(g, b, last):
                    it = g * B + b
                    g2, b2 = successor(g, b)
                    for n in range(NU):
                        for m in of_unit[n]:
                            empty_unit(act, 0, it, m)
                        if n + 2 < NU:
                            if n >= 2:
                                m = of_unit[n - 2][-1]
                                act.wait_ge(t_ready[m % 2], use_no(it, m) + 1)
                            exps(it, n + 2)
                        if not last and n in ends:
                            empty_proj(act, 0, it + 1, ends[n], g2, b2)
                    if not last:
                        exps(it + 1, 0)
                        exps(it + 1, 1)

                for p in range(NP):
                    empty_proj(act, 0, 0, p, 0, 0)
                exps(0, 0)
                exps(0, 1)
                pairs(step)(act)

            @block.vector
            def _(dve):
                dve.sem_inc(t_free[1], START)
                dve.sem_inc(o_done, START)
                dve.sem_inc(rden_ready, START)
                nc.vector.tensor_scalar(bqs, bq[:, 0, :], -SCALE, None, ALU.mult).then_inc(bqs_ready, 1)
                dve.wait_ge(bqs_ready, 1)

                def lows(it, n):
                    i, h = units[n]
                    dve.wait_ge(s_ready, it * NU + n + 1)
                    nc.vector.tensor_reduce(low[:, i % 2, h:h + 1], s_bank(n)[:, 0:(i + 1) * P], AX_X, ALU.min)\
                        .then_inc(low_ready, 1)

                def combine(it, i, b, g):
                    dve.wait_ge(rb_done, it * TB + i + 1)
                    if i == 0:
                        dve.wait_ge(o_stored[b], DSTART + g * 16)
                    nc.vector.tensor_copy(rden_T[:, i % 2, :], psum[:, O_BANK, P:2 * P])\
                        .then_inc(rb_copied, 1)
                    dve.wait_ge(rb_copied, it * TB + i + 1)
                    nc.vector.tensor_tensor(oS[:, b, i * P:(i + 1) * P], psum[:, O_BANK, 0:P],
                                            rden_T[:, i % 2, :], ALU.mult).then_inc(o_done, 1)

                def step(g, b, last):
                    it = g * B + b
                    g2, b2 = successor(g, b)
                    for n in range(NU):
                        if n + 2 < NU:
                            lows(it, n + 2)
                        for m in of_unit[n]:
                            empty_unit(dve, 1, it, m)
                        if not last and n in ends:
                            empty_proj(dve, 1, it + 1, ends[n], g2, b2)
                        if n % HG == HG - 1:
                            i = n // HG
                            dve.wait_ge(probs, it * NU + n + 1)
                            nc.vector.reciprocal(rden[:, i % 2, :], den[:, i % 2, :]).then_inc(rden_ready, 1)
                        if n % HG == 0 and n > HG:
                            combine(it, n // HG - 2, b, g)
                    combine(it, TB - 2, b, g)
                    if not last:
                        lows(it + 1, 0)
                        lows(it + 1, 1)
                    combine(it, TB - 1, b, g)

                for p in range(NP):
                    empty_proj(dve, 1, 0, p, 0, 0)
                    if p < SPLITS:
                        split(dve, nc.vector, split_first, 0, p)
                lows(0, 0)
                lows(0, 1)
                pairs(step)(dve)
        scope.close()
        attention_scope.close()
        wg_scope.close()

        NW = KD * 2 * F
        WORDS = NW + FC * D
        GU_W = KD * (2 * SC - 1) * P
        HOT_W = GT * TOPK * E
        late_a = sb("late_a", [P, 4 * GN + 2 * HOT_W])
        late_b = sb("late_b", [P, 2 * KD * GN + KD * D])
        slot_tok = sb("slot_tok", [P, E], U32)
        get_idx = [sb(f"get_idx{u}", [P, 1], U32) for u in range(UNROLL)]
        carve = Arena(late_a, 4 * GN + 2 * HOT_W).carve
        hot = carve([P, GT, TOPK * E]).rearrange("p t (k e) -> p t k e", e=E)
        hot_pos = carve([P, GT, TOPK * E]).rearrange("p t (k e) -> p t k e", e=E)
        silu = carve([P, 2, GN])
        x_mod = carve([P, 2, D])
        after_routing = Arena(late_a, 2 * HOT_W)
        slots = after_routing.carve([P, E, 2])
        xe = [after_routing.carve([P, D]) for _ in range(UNROLL)]
        carve = Arena(late_b, 2 * KD * GN + KD * D).carve
        oT = carve([P, 2 * KD, GN])
        woT = carve([P, KD, D])
        first_w = late_b[:, 0:WORDS]

        scope = ExitStack()
        xs = sb("xs", [P, NT, D], scope=scope)
        sgu_parts = [sb(n, [P, KD * (2 * SC - 1), P], F32R, scope) for n in ("sgu_hi", "sgu_lo")]
        h2T_parts = [sb(n, [P, KD, GN], F32R, scope) for n in ("h2T_hi", "h2T_lo")]
        words3 = 11 * 1024
        carve = Arena(sb("arena3", [P, words3], scope=scope), words3).carve
        gw = carve([P, KD, E])
        sd = carve([P, SC, D])
        yT = carve([P, KD, GN])
        h2 = yT.rearrange("p k (t x) -> p (k t x)", x=P).rearrange("p (t d) -> p t d", d=D)
        h2T = carve([P, KD, GN])
        guS = carve([P, SC, GN])
        sgu_raw = [late_a[:, 0:GU_W // 2], guS.rearrange("p f t -> p (f t)")[:, 0:GU_W // 2]]
        stats3 = carve([P, GT, 6])
        mv3 = carve([P, GT, 2])
        var3 = carve([P, GT])
        std3 = carve([P, GT])
        rstd3 = carve([P, GT])
        boga = carve([P, KD, B])
        lmax = carve([P, GT])
        lsub = carve([P, GT, E])
        lexp = carve([P, GT, E])
        lsum = carve([P, GT])
        lrec = carve([P, GT])
        top = sb("top", [P, GT, 8], scope=scope)
        top_i = sb("top_i", [P, GT, 8], U32, scope=scope)
        top_f = carve([P, GT, 8])
        picked = sb("picked", [P, GT, E], BF16, scope=scope)
        carry = sb("carry", [P, E], scope=scope)
        carry_bf = sb("carry_bf", [P, E], BF16, scope=scope)
        gsum = sb("gsum", [P, E], scope=scope)
        pos_k = sb("pos_k", [P, GT, TOPK], scope=scope)
        over = sb("over", [P, GT, TOPK], scope=scope)
        dest = sb("dest", [P, GT, TOPK], scope=scope)
        dest_u = sb("dest_u", [P, GT, TOPK], U32, scope=scope)
        entry = sb("entry", [P, GT, TOPK, 2], scope=scope)

        PAIR = 2
        OUT_ORDER = (2, 3, 0, 1)

        slots_in = sem("slots_in")
        tok_ready = sem("tok_ready")
        get_ready = sem("get_ready")
        xe_in = [sem(f"xe_in{u}") for u in range(UNROLL)]
        xt_mm = sem("xt_mm")
        w_in = [sem(f"w_in{u}") for u in range(UNROLL)]
        out_base = sem("out_base")
        w3_in = sem("w3_in")
        wo_in = sem("wo_in")
        oT_in = sem("oT_in")
        sgu_in = [sem("sgu_in0"), sem("sgu_in1")]
        sgu_hi = sem("sgu_hi")
        sgu_lo = sem("sgu_lo")
        h2_hi = sem("h2_hi")
        h2_lo = sem("h2_lo")
        x3_in = [sem("x3_in_first"), sem("x3_in_rest")]
        pos_read = sem("pos_read")
        bg_ready = sem("bg_ready")
        y_mm = sem("y_mm")
        y_act = sem("y_act")
        y_dve = sem("y_dve")
        yt_mm = sem("yt_mm")
        x1_done = sem("x1_done")
        l2_v = sem("l2_v")
        l2_var = sem("l2_var")
        l2_std = sem("l2_std")
        h2_ready = sem("h2_ready")
        h2_out = sem("h2_out")
        h2t_mm = sem("h2t_mm")
        h2t_act = sem("h2t_act")
        h2t_dve = sem("h2t_dve")
        lg_mm = sem("lg_mm")
        r_v = sem("r_v")
        r_sub = sem("r_sub")
        r_exp = sem("r_exp")
        pick_ready = sem("pick_ready")
        pos_mm = sem("pos_mm")
        dest_ready = sem("dest_ready")
        gu_mm = sem("gu_mm")
        gu_silu = sem("gu_silu")
        gu_done = sem("gu_done")
        sd_mm = sem("sd_mm")
        sd_tmp = sem("sd_tmp")
        sd_done = sem("sd_done")

        def wait_for(eng, what, value):
            if not isinstance(value, int) or value > 0:
                eng.wait_ge(what, value)

        def groups(eng, step):
            step(0)
            with eng.Fori(1, NGRP) as it:
                step(it)

        def some_x(it, t):
            return xs[:, bass.ds(it * GT + t, 1), :].rearrange("p a d -> p (a d)")

        def mod_rows(r, it):
            return rowsB[:, r, bass.ds(it // HB, 1), :].rearrange("p a d -> p (a d)")

        first = lambda it: isinstance(it, int) and it == 0
        PRODUCTS = ((0, 0), (0, 1), (1, 0))
        sgu_flat = [w[:, :, :].rearrange("p a c -> p (a c)") for w in sgu_parts]

        def load_expert(sp, e, u, buf):
            gu_w, d_w = expert_weights(buf)
            rows = wgu[e] if isinstance(e, int) else wgu[bass.ds(e, 1)].rearrange("a p c -> p (a c)")
            sp.dma_start(gu_w, rows.rearrange("p (k f) -> p k f", k=KD)).then_inc(w_in[u], 16)
            sp.dma_start(d_w[:, 0:FC - 1, :],
                         wd[e, 0:(FC - 1) * P, :].rearrange("(k p) d -> p k d", p=P)).then_inc(w_in[u], 16)
            sp.dma_start(d_w[0:FR, FC - 1, :], wd[e, (FC - 1) * P:F, :]).then_inc(w_in[u], 16)

        def expert_weights(buf):
            return (buf[:, 0:NW].rearrange("p (k f) -> p k f", k=KD),
                    buf[:, NW:WORDS].rearrange("p (k d) -> p k d", k=FC))

        def exists(e):
            return not isinstance(e, int) or 0 <= e < E

        def gather(pool, e, i, u):
            if not exists(e):
                return
            if not isinstance(i, int) or i > 0:
                wait_alone(pool, xe_in[u], i * 16)
            nc.gpsimd.tensor_copy(get_idx[u][:, :], slot_tok[:, bass.ds(e, 1)]).then_inc(get_ready, 1)
            pool.wait_ge(get_ready, e + 1)
            if not isinstance(i, int) or i > 0:
                wait_alone(pool, xt_mm, e - UNROLL + 1)
            pool.indirect_dma_start(
                out=xe[u], out_offset=None, in_=h2_dram,
                in_offset=bass.IndirectOffsetOnAxis(ap=get_idx[u][:, 0:1], axis=0),
                bounds_check=TD - 1, oob_is_err=True).then_inc(xe_in[u], 16)

        with nc.Block() as block:
            @block.sync
            def _(sp):
                def load_oT(it):
                    sp.dma_start(oT[:, it % 2 * KD:(it % 2 + 1) * KD, :], oT_cols[:, :, it * GN:(it + 1) * GN])\
                        .then_inc(oT_in, 16)

                def store_rows(it):
                    sp.wait_ge(sd_done, START + it * GT + GT)
                    sp.dma_start(out_rows[:, it * GT:(it + 1) * GT, :], xs[:, it * GT:(it + 1) * GT, :])\
                        .then_inc(out_base, 16)

                sp.sem_inc(h2_out, DSTART)
                load_oT(0)
                sp.dma_start(woT, wo).then_inc(wo_in, 16)
                for n in range(2):
                    sp.dma_start(sgu_raw[n], shgu[:, n * (GU_W // 2):(n + 1) * (GU_W // 2)]).then_inc(sgu_in[n], 16)
                sp.dma_start(xs[:, 0:GT, :], x_rows[:, 0:GT, :]).then_inc(x3_in[0], 16)
                sp.dma_start(gw, gatew).then_inc(w3_in, 16)
                sp.wait_ge(oT_in, 16)
                load_oT(1)
                sp.dma_start(sd[:, 0:SC - 1, :], shd[0:(SC - 1) * P, :].rearrange("(a p) d -> p a d", p=P))\
                    .then_inc(w3_in, 16)
                sp.dma_start(sd[0:SR, SC - 1, :], shd[(SC - 1) * P:FS, :]).then_inc(w3_in, 16)
                sp.dma_start(xs[:, GT:NT, :], x_rows[:, GT:NT, :]).then_inc(x3_in[1], 16)
                for it in range(NGRP):
                    if 1 <= it < NGRP - 1:
                        sp.wait_ge(oT_in, (it + 1) * 16)
                        sp.wait_ge(y_mm, it * KD)
                        load_oT(it + 1)
                    sp.wait_ge(h2_ready, it * GT + GT)
                    sp.dma_start(h2_rows[:, it * GT:(it + 1) * GT, :], h2).then_inc(h2_out, 16)
                    if it:
                        store_rows(it - 1)
                sp.wait_ge(y_mm, NGRP * KD)
                load_expert(sp, 0, 0, first_w)
                sp.wait_ge(dest_ready, NGRP)
                sp.wait_ge(scattered, DSTART + NGRP * GT * TOPK * 16)
                sp.dma_start(slots, slot_dram.rearrange("(p e) w -> p e w", e=E)).then_inc(slots_in, 16)
                store_rows(NGRP - 1)
                sp.wait_ge(h2_out, DSTART + 16 * NGRP)
                sp.wait_ge(out_base, 16 * NGRP)

            @block.gpsimd
            def _(pool):
                with pool.Fori(0, NGRP) as it:
                    wait_alone(pool, dest_ready, it + 1)
                    for t in range(GT):
                        for k in range(TOPK):
                            pool.indirect_dma_start(
                                out=slot_dram, out_offset=bass.IndirectOffsetOnAxis(ap=dest_u[:, t, k:k + 1], axis=0),
                                in_=entry[:, t, k, :], in_offset=None, bounds_check=CAP * E - 1,
                                oob_is_err=False).then_inc(scattered, 16)
                pool.wait_ge(scattered, DSTART + NGRP * GT * TOPK * 16)
                pool.wait_ge(h2_out, DSTART + 16 * NGRP)
                pool.wait_ge(tok_ready, 1)
                for u in range(UNROLL):
                    gather(pool, u, 0, u)

            @block.tensor
            def _(pe):
                def output_projection(it):
                    pe.wait_ge(oT_in, it * 16 + 16)
                    for j in OUT_ORDER:
                        if j == 0:
                            wait_for(pe, r_sub, it)
                        elif j == 1:
                            wait_for(pe, pos_read, it)
                        for k in range(KD):
                            last = nc.tensor.matmul(psum[:, j, :], woT[:, k, j * P:(j + 1) * P],
                                                    oT[:, bass.ds(it % 2 * KD + k, 1), :]
                                                    .rearrange("p a t -> p (a t)"),
                                                    start=(k == 0), stop=(k == KD - 1))
                        last.then_inc(y_mm, 1)

                def gate_up(it, f):
                    if f == 0:
                        pe.wait_ge(sd_done, START + it * GT)
                        pe.wait_ge(h2_lo, (it + 1) * KD)
                        pe.wait_ge(sgu_lo, 2)
                    pe.wait_ge(gu_done, PAIR + it * SC + f - 1)
                    for half in range(2 if f < SC - 1 else 1):
                        for k in range(KD):
                            for w, x in PRODUCTS:
                                last = nc.tensor.matmul(psum[:, 4 + (f % 2) * 2 + half, :],
                                                        sgu_parts[w][:, k * (2 * SC - 1) + 2 * f + half, :],
                                                        h2T_parts[x][:, k, :], start=(k == 0 and (w, x) == PRODUCTS[0]),
                                                        stop=(k == KD - 1 and (w, x) == PRODUCTS[-1]))
                    last.then_inc(gu_mm, 1)

                def down(it):
                    pe.wait_ge(gu_done, PAIR + it * SC + SC)
                    for t in range(GT):
                        for f in range(SC):
                            rows = P if f < SC - 1 else SR
                            last = nc.tensor.matmul(psum[:, 4 + t, :], guS[0:rows, f, t * P:(t + 1) * P],
                                                    sd[0:rows, f, :], start=(f == 0), stop=(f == SC - 1))
                        last.then_inc(sd_mm, 1)

                def step(it):
                    output_projection(it)
                    if not first(it):
                        gate_up(it - 1, 0)
                    pe.wait_ge(y_act, it * 2 + 2)
                    pe.wait_ge(y_dve, it * 2 + 2)
                    for t in range(GT):
                        for j in range(KD):
                            last = nc.tensor.transpose(psum[:, t, j * P:(j + 1) * P],
                                                       yT[:, j, t * P:(t + 1) * P], ident[:, :])
                        last.then_inc(yt_mm, 1)
                    if not first(it):
                        for f in range(1, SC):
                            gate_up(it - 1, f)
                    pe.wait_ge(x1_done, it * GT + GT)
                    for t in range(GT):
                        pe.wait_ge(h2_ready, it * GT + t + 1)
                        for k in range(KD):
                            last = nc.tensor.transpose(psum[:, k, t * P:(t + 1) * P],
                                                       h2[:, t, k * P:(k + 1) * P], ident[:, :])
                    last.then_inc(h2t_mm, 1)
                    pe.wait_ge(h2t_act, it * 2 + 2)
                    pe.wait_ge(h2t_dve, it * 2 + 2)
                    if first(it):
                        pe.wait_ge(w3_in, 48)
                    for t in range(GT):
                        for k in range(KD):
                            last = nc.tensor.matmul(psum[:, 0, t * E:(t + 1) * E], h2T[:, k, t * P:(t + 1) * P],
                                                    gw[:, k, :], start=(k == 0), stop=(k == KD - 1))
                    last.then_inc(lg_mm, 1)
                    if not first(it):
                        down(it - 1)
                    pe.wait_ge(pick_ready, it + 1)
                    for t in range(GT):
                        nc.tensor.matmul(psum[:, 1, t * E:(t + 1) * E], before_bf[:, :], picked[:, t, :],
                                         start=True, stop=False)
                        for u in range(t):
                            nc.tensor.matmul(psum[:, 1, t * E:(t + 1) * E], ones_bf[:, :], picked[:, u, :],
                                             start=False, stop=False)
                        last = nc.tensor.matmul(psum[:, 1, t * E:(t + 1) * E], ones_bf[:, :], carry_bf[:, :],
                                                start=False, stop=True)
                    last.then_inc(pos_mm, 1)

                pe.wait_ge(wo_in, 16)
                groups(pe, step)
                for f in range(SC):
                    gate_up(NGRP - 1, f)
                down(NGRP - 1)

            @block.scalar
            def _(act):
                def silu_chunk(it, f):
                    act.wait_ge(gu_mm, it * SC + f + 1)
                    act.wait_ge(gu_done, PAIR + it * SC + f - 1)
                    rows = P if f < SC - 1 else SR
                    nc.scalar.activation(silu[0:rows, f % 2, :], psum[0:rows, 4 + (f % 2) * 2, :], ACT.Silu)\
                        .then_inc(gu_silu, 1)

                def step(it):
                    act.wait_ge(h2_out, DSTART + it * 16)
                    for n, j in enumerate(OUT_ORDER):
                        if first(it) and n == 1:
                            for part in range(2):
                                act.wait_ge(sgu_in[part], 16)
                                nc.scalar.copy(sgu_flat[0][:, part * (GU_W // 2):(part + 1) * (GU_W // 2)],
                                               sgu_raw[part]).then_inc(sgu_hi, 1)
                        if j % 2 == 0:
                            act.wait_ge(y_mm, it * KD + n + 1)
                            nc.scalar.activation(yT[:, j, :], psum[:, j, :], ACT.Identity,
                                                 bias=boga[:, j, bass.ds(it // HB, 1)],
                                                 scale=modT[:, GA, j, bass.ds(it // HB, 1)]).then_inc(y_act, 1)
                    if not first(it):
                        silu_chunk(it - 1, 0)
                    act.wait_ge(l2_var, it + 1)
                    nc.scalar.activation(std3, var3, ACT.Sqrt).then_inc(l2_std, 1)
                    if not first(it):
                        for f in range(1, SC):
                            silu_chunk(it - 1, f)
                    act.wait_ge(h2t_mm, it + 1)
                    for k in (0, 2):
                        nc.scalar.copy(h2T[:, k, :], psum[:, k, :]).then_inc(h2t_act, 1)
                    act.wait_ge(r_sub, it + 1)
                    nc.scalar.activation(lexp, lsub, ACT.Exp).then_inc(r_exp, 1)
                    act.wait_ge(h2t_dve, it * 2 + 2)
                    act.wait_ge(h2t_act, it * 2 + 2)
                    for k in range(KD):
                        nc.scalar.copy(h2T_parts[0][:, k, :], h2T[:, k, :]).then_inc(h2_hi, 1)

                act.wait_ge(bg_ready, 1)
                groups(act, step)
                for f in range(SC):
                    silu_chunk(NGRP - 1, f)

            @block.vector
            def _(dve):
                N2 = 3 * GT + 1
                NR = 22
                made = [0]

                def product(it, f):
                    dve.wait_ge(gu_silu, it * SC + f + 1)
                    rows = P if f < SC - 1 else SR
                    bank = 4 + (f % 2) * 2
                    up = psum[:, bank + 1, :] if f < SC - 1 else psum[SR:SR + SR, bank, :]
                    nc.vector.tensor_tensor(guS[0:rows, f, :], silu[0:rows, f % 2, :], up, ALU.mult)\
                        .then_inc(gu_done, 1)

                def shared_result(it):
                    for t in range(GT):
                        dve.wait_ge(sd_mm, it * GT + t + 1)
                        nc.vector.tensor_tensor(x_mod[:, t % 2, :], psum[:, 4 + t, :], mod_rows(2, it), ALU.mult)\
                            .then_inc(sd_tmp, 1)
                        dve.wait_ge(sd_tmp, it * GT + t + 1)
                        nc.vector.tensor_tensor(some_x(it, t), some_x(it, t), x_mod[:, t % 2, :], ALU.add)\
                            .then_inc(sd_done, 1)

                def normalize(it):
                    for t in range(GT):
                        xt = some_x(it, t)
                        dve.wait_ge(yt_mm, it * GT + t + 1)
                        nc.vector.tensor_tensor(xt, xt, psum[:, t, :], ALU.add).then_inc(x1_done, 1)
                        wait_alone(dve, x1_done, it * GT + t + 1)
                        nc.vector.bn_stats(stats3[:, t, :], xt).then_inc(l2_v, 1)
                    wait_alone(dve, l2_v, it * N2 + GT)
                    for t in range(GT):
                        nc.vector.bn_aggr(mv3[:, t, :], stats3[:, t, :]).then_inc(l2_v, 1)
                    dve.wait_ge(l2_v, it * N2 + 2 * GT)
                    nc.vector.tensor_scalar(var3, mv3[:, :, 1], EPS, None, ALU.add).then_inc(l2_var, 1)
                    dve.wait_ge(l2_std, it + 1)
                    nc.vector.reciprocal(rstd3, std3).then_inc(l2_v, 1)
                    dve.wait_ge(l2_v, it * N2 + 2 * GT + 1)
                    for t in range(GT):
                        nc.vector.scalar_tensor_tensor(out=x_mod[:, t % 2, :], in0=some_x(it, t),
                                                       scalar=mv3[:, t, 0:1], in1=mod_rows(0, it),
                                                       op0=ALU.subtract, op1=ALU.mult).then_inc(l2_v, 1)
                        dve.wait_ge(l2_v, it * N2 + 2 * GT + 2 + t)
                        nc.vector.scalar_tensor_tensor(out=h2[:, t, :], in0=x_mod[:, t % 2, :],
                                                       scalar=rstd3[:, t:t + 1], in1=mod_rows(1, it),
                                                       op0=ALU.mult, op1=ALU.add).then_inc(h2_ready, 1)
                        if t == 1 and not first(it):
                            product(it - 1, 1)

                def step(it):
                    if first(it):
                        dve.wait_ge(x3_in[0], 16)
                    else:
                        dve.wait_ge(x3_in[1], 16)
                    dve.wait_ge(h2_out, DSTART + it * 16)
                    for n, j in enumerate(OUT_ORDER):
                        if first(it) and n == 2:
                            for part in range(2):
                                span = slice(part * (GU_W // 2), (part + 1) * (GU_W // 2))
                                dve.wait_ge(sgu_hi, part + 1)
                                nc.vector.tensor_tensor(sgu_flat[1][:, span], sgu_raw[part],
                                                        sgu_flat[0][:, span].bitcast(F32), ALU.subtract)\
                                    .then_inc(sgu_lo, 1)
                        if j % 2 == 1:
                            dve.wait_ge(y_mm, it * KD + n + 1)
                            nc.vector.tensor_scalar(yT[:, j, :], psum[:, j, :],
                                                    modT[:, GA, j, bass.ds(it // HB, 1)],
                                                    boga[:, j, bass.ds(it // HB, 1)], ALU.mult, ALU.add)\
                                .then_inc(y_dve, 1)
                    if not first(it):
                        product(it - 1, 0)
                    normalize(it)
                    if not first(it):
                        for f in range(2, SC):
                            product(it - 1, f)
                    dve.wait_ge(h2t_mm, it + 1)
                    for k in (1, 3):
                        nc.vector.tensor_copy(h2T[:, k, :], psum[:, k, :]).then_inc(h2t_dve, 1)
                    step = [0]

                    def then(ins):
                        step[0] += 1
                        ins.then_inc(r_v, 1)
                        wait_alone(dve, r_v, it * NR + step[0])

                    lg = psum[:, 0, 0:GT * E].rearrange("p (t e) -> p t e", e=E)
                    dve.wait_ge(lg_mm, it + 1)
                    then(nc.vector.tensor_reduce(lmax, lg, AX_X, ALU.max))
                    nc.vector.tensor_tensor(lsub, lg,
                                            lmax.rearrange("p (t o) -> p t o", o=1).broadcast_to([P, GT, E]),
                                            ALU.subtract).then_inc(r_sub, 1)
                    dve.wait_ge(r_exp, it + 1)
                    then(nc.vector.tensor_reduce(lsum, lexp, AX_X, ALU.add))
                    then(nc.vector.reciprocal(lrec, lsum))
                    then(nc.vector.tensor_tensor(lexp, lexp,
                                                 lrec.rearrange("p (t o) -> p t o", o=1).broadcast_to([P, GT, E]),
                                                 ALU.mult))
                    for t in range(GT):
                        i_ = nc.vector.max(top[:, t, :], lexp[:, t, :])
                    then(i_)
                    for t in range(GT):
                        i_ = nc.vector.max_index(top_i[:, t, :], top[:, t, :], lexp[:, t, :])
                    then(i_)
                    then(nc.vector.tensor_copy(top_f, top_i[:, :, :]))
                    for t in range(GT):
                        i_ = nc.vector.tensor_tensor(
                            hot[:, t], iota_e[:, :].rearrange("p (o e) -> p o e", o=1).broadcast_to([P, TOPK, E]),
                            top_f[:, t, 0:TOPK].rearrange("p (k o) -> p k o", o=1).broadcast_to([P, TOPK, E]),
                            ALU.is_equal)
                    then(i_)
                    with nc.allow_low_precision(reason="zeros and ones, exact in bfloat16"):
                        for t in range(GT):
                            i_ = nc.vector.tensor_reduce(picked[:, t, :], hot[:, t].rearrange("p k e -> p e k"),
                                                         AX_X, ALU.add)
                    i_.then_inc(pick_ready, 1)
                    dve.wait_ge(pick_ready, it + 1)
                    then(nc.vector.tensor_reduce(gsum[:, :], picked[:, :, :].rearrange("p t e -> p e t"), AX_X,
                                                 ALU.add))
                    then(nc.vector.tensor_tensor(carry[:, :], carry[:, :], gsum[:, :], ALU.add))
                    for k in range(KD):
                        dve.wait_ge(h2_hi, it * KD + k + 1)
                        nc.vector.tensor_tensor(h2T_parts[1][:, k, :], h2T[:, k, :],
                                                h2T_parts[0][:, k, :].bitcast(F32), ALU.subtract).then_inc(h2_lo, 1)
                    if not first(it):
                        shared_result(it - 1)
                    dve.wait_ge(pos_mm, it + 1)
                    then(nc.vector.tensor_copy(carry_bf[:, :], carry[:, :]))
                    for t in range(GT):
                        i_ = nc.vector.tensor_tensor(
                            hot_pos[:, t], hot[:, t],
                            psum[:, 1, t * E:(t + 1) * E].rearrange("p (o e) -> p o e", o=1)
                            .broadcast_to([P, TOPK, E]), ALU.mult)
                    i_.then_inc(pos_read, 1)
                    dve.wait_ge(pos_read, it + 1)
                    for t in range(GT):
                        i_ = nc.vector.tensor_reduce(pos_k[:, t, :], hot_pos[:, t], AX_X, ALU.add)
                    then(i_)
                    then(nc.vector.tensor_scalar(over[:, :, :], pos_k[:, :, :], float(CAP), DROPPED, ALU.is_ge,
                                                 ALU.mult))
                    then(nc.vector.scalar_tensor_tensor(out=dest[:, :, :], in0=pos_k[:, :, :], scalar=float(E),
                                                        in1=top_f[:, :, 0:TOPK], op0=ALU.mult, op1=ALU.add))
                    then(nc.vector.tensor_tensor(dest[:, :, :], dest[:, :, :], over[:, :, :], ALU.add))
                    wait_alone(dve, scattered, DSTART + it * GT * TOPK * 16)
                    then(nc.vector.tensor_copy(dest_u[:, :, :], dest[:, :, :]))
                    then(nc.vector.tensor_copy(entry[:, :, :, 1], top[:, :, 0:TOPK]))
                    then(nc.vector.tensor_copy(
                        entry[:, :, :, 0],
                        tok_id[:, :].rearrange("p (t o) -> p t o", o=1).broadcast_to([P, GT, TOPK])))
                    nc.vector.tensor_scalar(tok_id[:, :], tok_id[:, :], float(GN), None, ALU.add)\
                        .then_inc(dest_ready, 1)
                    assert step[0] <= NR
                    for _ in range(NR - step[0]):
                        dve.sem_inc(r_v, 1)
                dve.sem_inc(sd_done, START)
                dve.sem_inc(gu_done, PAIR)
                for b in range(B):
                    i_ = nc.vector.tensor_tensor(boga[:, :, b], boT[:, :], modT[:, GA, :, b], ALU.mult)
                nc.vector.memset(carry[:, :], 0.0)
                nc.vector.memset(carry_bf[:, :], 0.0).then_inc(bg_ready, 1)
                dve.wait_ge(bg_ready, 1)
                groups(dve, step)
                for f in range(SC):
                    product(NGRP - 1, f)
                dve.wait_ge(slots_in, 16)
                nc.vector.tensor_copy(slot_tok[:, :], slots[:, :, 0]).then_inc(tok_ready, 1)
                shared_result(NGRP - 1)
        scope.close()

        words4 = 18 * 1024 + 512
        carve = Arena(sb("arena4", [P, words4]), words4).carve
        wbuf = [first_w] + [carve([P, WORDS]) for _ in range(UNROLL - 1)]
        wgu_s = [expert_weights(w)[0] for w in wbuf]
        wd_s = [expert_weights(w)[1] for w in wbuf]
        dsc = [carve([P, D]) for _ in range(UNROLL)]
        part_sum = [carve([P, D]) for _ in range(B)]
        w_row = carve([P, B, E])
        xeT = [carve([P, KD, P]) for _ in range(2)]
        sil = [carve([P, F]) for _ in range(2)]
        gu = [carve([P, F]) for _ in range(2)]
        wd_parts = [[sb(f"wd_{n}{u}", [P, FC, D], F32R) for n in ("hi", "lo")] for u in range(2)]
        guT_parts = [[sb(f"guT_{n}{u}", [P, FC, P], F32R) for n in ("hi", "lo")] for u in range(2)]
        add_idx = [sb(f"add_idx{u}", [P, 1], U32) for u in range(UNROLL)]

        add_ready = sem("add_ready")
        weights_v = sem("weights_v")
        xt_out = sem("xt_out")
        g_mm = sem("g_mm")
        u_mm = sem("u_mm")
        silu_done = sem("silu_done")
        gu_out = sem("gu_out")
        gt_mm = sem("gt_mm")
        gt_hi = sem("gt_hi")
        gt_out = sem("gt_out")
        wd_hi = sem("wd_hi")
        wd_lo = sem("wd_lo")
        d_mm = sem("d_mm")
        d_read = sem("d_read")
        d_out = sem("d_out")
        added = sem("added")

        FULL_AND_REST = ((P, slice(0, FC - 1)), (FR, slice(FC - 1, FC)))

        def hidden_T(rows, ks):
            return psum[0:rows, 1, ks.start * P:ks.stop * P].rearrange("p (k c) -> p k c", c=P)

        def over_experts(eng, step):
            for u in range(UNROLL):
                step(0, u)
            with eng.Fori(1, E // UNROLL - 1) as i:
                for u in range(UNROLL):
                    step(i, u)
            for u in range(UNROLL):
                step(E // UNROLL - 1, u)

        with nc.Block() as block:
            @block.sync
            def _(sp):
                def step(i, u):
                    e = i * UNROLL + u
                    if isinstance(e, int) and e == 0:
                        return
                    wait_for(sp, d_mm, e - UNROLL + 1)
                    load_expert(sp, e, u, wbuf[u])

                over_experts(sp, step)

            @block.gpsimd
            def _(pool):
                def step(i, u):
                    e = i * UNROLL + u
                    gather(pool, e + UNROLL, i + 1, u)
                    nc.gpsimd.tensor_copy(add_idx[u][:, :], slot_tok[:, bass.ds(e, 1)]).then_inc(add_ready, 1)
                    pool.wait_ge(add_ready, e + 1)
                    wait_alone(pool, d_out, e + 1)
                    if exists(e - 1):
                        wait_alone(pool, added, e * 16)
                    pool.indirect_dma_start(
                        out=out, out_offset=bass.IndirectOffsetOnAxis(ap=add_idx[u][:, 0:1], axis=0),
                        in_=dsc[u], in_offset=None, compute_op=ALU.add,
                        bounds_check=T - 1, oob_is_err=False).then_inc(added, 16)

                over_experts(pool, step)
                pool.wait_ge(added, E * 16)

            @block.tensor
            def _(pe):
                def turn_rows(e, i, u):
                    if not exists(e):
                        return
                    pe.wait_ge(xe_in[u], i * 16 + 16)
                    wait_for(pe, xt_out, e)
                    for k in range(KD):
                        last = nc.tensor.transpose(psum[:, 0, k * P:(k + 1) * P], xe[u][:, k * P:(k + 1) * P],
                                                   ident[:, :])
                    last.then_inc(xt_mm, 1)

                def half(e, u, up):
                    for k in range(KD):
                        last = nc.tensor.matmul(psum[:, 2 + up, 0:F], xeT[u % 2][:, k, :],
                                                wgu_s[u][:, k, up * F:(up + 1) * F],
                                                start=(k == 0), stop=(k == KD - 1))
                    last.then_inc(u_mm if up else g_mm, 1)

                def turn_hidden(e, u):
                    if not exists(e):
                        return
                    pe.wait_ge(gu_out, e + 1)
                    wait_for(pe, gt_out, e)
                    for k in range(FC):
                        w = P if k < FC - 1 else FR
                        last = nc.tensor.transpose(psum[0:w, 1, k * P:(k + 1) * P], gu[u % 2][:, k * P:k * P + w],
                                                   ident[:, :])
                    last.then_inc(gt_mm, 1)

                def down(e, u):
                    if not exists(e):
                        return
                    pe.wait_ge(gt_out, e + 1)
                    wait_for(pe, d_read, e - 1)
                    pe.wait_ge(wd_lo, e + 1)
                    for k in range(FC):
                        w = P if k < FC - 1 else FR
                        for x, y in PRODUCTS:
                            last = nc.tensor.matmul(psum[:, 4 + u % 2, :], guT_parts[u % 2][x][0:w, k, :],
                                                    wd_parts[u % 2][y][0:w, k, :],
                                                    start=(k == 0 and (x, y) == PRODUCTS[0]),
                                                    stop=(k == FC - 1 and (x, y) == PRODUCTS[-1]))
                    last.then_inc(d_mm, 1)

                def step(i, u):
                    e = i * UNROLL + u
                    pe.wait_ge(w_in[u], i * 48 + 48)
                    pe.wait_ge(xt_out, e + 1)
                    wait_for(pe, silu_done, e)
                    half(e, u, 0)
                    turn_hidden(e - 1, (u - 1) % UNROLL)
                    turn_rows(e + 1, i + (u + 1) // UNROLL, (u + 1) % UNROLL)
                    wait_for(pe, gu_out, e)
                    half(e, u, 1)
                    down(e - 1, (u - 1) % UNROLL)

                turn_rows(0, 0, 0)
                over_experts(pe, step)
                turn_hidden(E - 1, (E - 1) % UNROLL)
                down(E - 1, (E - 1) % UNROLL)

            @block.scalar
            def _(act):
                def keep_rows(e, u):
                    if not exists(e):
                        return
                    act.wait_ge(xt_mm, e + 1)
                    wait_for(act, u_mm, e - 1)
                    nc.scalar.copy(xeT[u % 2].rearrange("p k c -> p (k c)"), psum[:, 0, :]).then_inc(xt_out, 1)

                def round_hidden(e, u):
                    if not exists(e):
                        return
                    act.wait_ge(gt_mm, e + 1)
                    wait_for(act, d_mm, e - 1)
                    for rows, ks in FULL_AND_REST:
                        i_ = nc.scalar.copy(guT_parts[u % 2][0][0:rows, ks, :], hidden_T(rows, ks))
                    i_.then_inc(gt_hi, 1)

                def step(i, u):
                    e = i * UNROLL + u
                    act.wait_ge(g_mm, e + 1)
                    wait_for(act, gu_out, e - 1)
                    nc.scalar.activation(sil[u % 2], psum[:, 2, 0:F], ACT.Silu).then_inc(silu_done, 1)
                    round_hidden(e - 1, (u - 1) % UNROLL)
                    keep_rows(e + 1, (u + 1) % UNROLL)
                    wait_for(act, d_mm, e - 1)
                    act.wait_ge(w_in[u], i * 48 + 48)
                    for rows, ks in FULL_AND_REST:
                        i_ = nc.scalar.copy(wd_parts[u % 2][0][0:rows, ks, :], wd_s[u][0:rows, ks, :])
                    i_.then_inc(wd_hi, 1)

                keep_rows(0, 0)
                over_experts(act, step)
                round_hidden(E - 1, (E - 1) % UNROLL)

            @block.vector
            def _(dve):
                def rest_of_hidden(e, u):
                    if not exists(e):
                        return
                    dve.wait_ge(gt_hi, e + 1)
                    wait_for(dve, d_mm, e - 1)
                    for rows, ks in FULL_AND_REST:
                        i_ = nc.vector.tensor_tensor(guT_parts[u % 2][1][0:rows, ks, :], hidden_T(rows, ks),
                                                     guT_parts[u % 2][0][0:rows, ks, :].bitcast(F32), ALU.subtract)
                    i_.then_inc(gt_out, 1)

                def weigh(e, u):
                    if not exists(e):
                        return
                    dve.wait_ge(d_mm, e + 1)
                    wait_for(dve, d_out, e)
                    for b in range(B):
                        i_ = nc.vector.scalar_tensor_tensor(
                            out=part_sum[b], in0=psum[:, 4 + u % 2, :], scalar=w_row[:, b, bass.ds(e, 1)],
                            in1=rowsB[:, 2, b, :], op0=ALU.mult, op1=ALU.mult)
                    i_.then_inc(d_read, 1)
                    dve.wait_ge(d_read, e + 1)
                    if not isinstance(e, int) or e >= UNROLL:
                        dve.wait_ge(add_ready, e)
                    nc.vector.tensor_tensor(dsc[u], part_sum[0], part_sum[1], ALU.add).then_inc(d_out, 1)

                def step(i, u):
                    e = i * UNROLL + u
                    rest_of_hidden(e - 1, (u - 1) % UNROLL)
                    weigh(e - 2, (u - 2) % UNROLL)
                    dve.wait_ge(silu_done, e + 1)
                    dve.wait_ge(u_mm, e + 1)
                    wait_for(dve, gt_mm, e - 1)
                    nc.vector.tensor_tensor(gu[u % 2], sil[u % 2], psum[:, 3, 0:F], ALU.mult).then_inc(gu_out, 1)
                    dve.wait_ge(wd_hi, e + 1)
                    for rows, ks in FULL_AND_REST:
                        i_ = nc.vector.tensor_tensor(wd_parts[u % 2][1][0:rows, ks, :], wd_s[u][0:rows, ks, :],
                                                     wd_parts[u % 2][0][0:rows, ks, :].bitcast(F32), ALU.subtract)
                    i_.then_inc(wd_lo, 1)

                nc.vector.tensor_scalar(w_row[:, 1, :], slots[:, :, 0], float(S), None, ALU.is_ge)\
                    .then_inc(weights_v, 1)
                dve.wait_ge(weights_v, 1)
                nc.vector.tensor_tensor(w_row[:, 1, :], w_row[:, 1, :], slots[:, :, 1], ALU.mult)\
                    .then_inc(weights_v, 1)
                dve.wait_ge(weights_v, 2)
                nc.vector.tensor_tensor(w_row[:, 0, :], slots[:, :, 1], w_row[:, 1, :], ALU.subtract)\
                    .then_inc(weights_v, 1)
                dve.wait_ge(weights_v, 3)
                over_experts(dve, step)
                rest_of_hidden(E - 1, (E - 1) % UNROLL)
                weigh(E - 2, (E - 2) % UNROLL)
                weigh(E - 1, (E - 1) % UNROLL)



def lay_out(a):
    import numpy as np

    def per_partition(v):
        return np.ascontiguousarray(np.moveaxis(v.reshape(*v.shape[:-1], -1, P), -1, 0))

    E_ = {}
    E_["x"] = a["L0_attn_x"].reshape(T, D)
    w = a["L0_attn_w_qkv"].reshape(3, NG, P, KD, P)
    E_["wqkv"] = w.transpose(1, 4, 3, 0, 2).reshape(NG, P, KD * 3 * P)
    E_["bqkv"] = a["L0_attn_b_qkv"].reshape(3, NG, P).transpose(2, 0, 1)
    E_["wo"] = a["L0_attn_w_out"].reshape(D, KD, P).transpose(2, 1, 0)
    E_["bo"] = per_partition(a["L0_attn_b_out"])
    E_["gatew"] = a["L0_ffn_gate_w"].reshape(E, KD, P).transpose(2, 1, 0)
    g = a["L0_ffn_w_gate"].reshape(E, KD, P, F)
    u = a["L0_ffn_w_up"].reshape(E, KD, P, F)
    E_["wgu"] = np.concatenate([g, u], axis=3).transpose(0, 2, 1, 3).reshape(E, P, KD * 2 * F)
    E_["wd"] = a["L0_ffn_w_down"]
    cols = []
    for f in range(SC):
        r = slice(f * P, min(FS, (f + 1) * P))
        cols += [a["L0_ffn_sh_gate"][r], a["L0_ffn_sh_up"][r]]
    s = np.concatenate(cols, axis=0)
    E_["shgu"] = s.reshape(2 * FS, KD, P).transpose(2, 1, 0).reshape(P, KD * 2 * FS)
    E_["shd"] = a["L0_ffn_sh_down"].T
    E_["c"] = a["L0_c"].reshape(B, KD, P).transpose(2, 1, 0)
    E_["wmod"] = a["L0_wmod"].reshape(KD, P, 6, D).transpose(2, 1, 0, 3)
    return {k: np.ascontiguousarray(v) for k, v in E_.items()}


def kernel(**inputs):
    import numpy as _np
    import concourse.bacc as _bacc
    from concourse.bass_utils import run_bass_kernel_spmd as _run

    arrays = lay_out({k: _np.asarray(v) for k, v in inputs.items()})
    nc = _bacc.Bacc("TRN2", target_bir_lowering=False, num_devices=1)
    args = {k: nc.dram_tensor(k, v.shape, mybir.dt.from_np(v.dtype), kind="ExternalInput").ap()
            for k, v in arrays.items()}
    o = nc.dram_tensor("out", [T, D], F32, kind="ExternalOutput").ap()
    build(nc, out=o, **args)
    r = _run(nc, [arrays], core_ids=[0])
    return r.results[0]["out"].reshape(B, S, D)
```
